# Optimizing a Trainium2 kernel written in Bass

```python
import numpy as np
import jax
import jax.numpy as jnp

def _softmax(x, axis=-1):
    return jax.nn.softmax(x, axis=axis)

def _gelu(x):
    return jax.nn.gelu(x, approximate=True)

def _silu(x):
    return jax.nn.silu(x)

def _sigmoid(x):
    return jax.nn.sigmoid(x)

def _layernorm(x, axis=-1, eps=1e-05):
    m = jnp.mean(x, axis=axis, keepdims=True)
    v = jnp.var(x, axis=axis, keepdims=True)
    return (x - m) / jnp.sqrt(v + eps)

def _scatter_add(tgt, idx, src, axis=0):
    return tgt.at[idx].add(src)

def _segment_sum(src, seg, n):
    return jax.ops.segment_sum(src, seg, n)
kernel_name = 'mk_recurrent_d2_jaxref_r8_615867'

def setup_inputs(seed: int=0):
    np.random.seed(seed)
    _w = jnp.asarray

    def _L0_attn_setup():
        import jax, jax.numpy as jnp
        import numpy as np
        B, T, D, S = (4, 512, 256, 256)
        EPS = 1e-05

        def _rmsnorm(x, w, eps):
            var = jnp.mean(jnp.square(x), axis=-1, keepdims=True)
            return x * jax.lax.rsqrt(var + eps) * w

        def _linear_scan(f, z):

            def step(h, fz):
                f_t, z_t = fz
                h = f_t * h + z_t
                return (h, h)
            h0 = jnp.zeros((f.shape[0], f.shape[2]), dtype=f.dtype)
            fT = jnp.swapaxes(f, 0, 1)
            zT = jnp.swapaxes(z, 0, 1)
            _, hs = jax.lax.scan(step, h0, (fT, zT))
            return jnp.swapaxes(hs, 0, 1)
        key = jax.random.key(seed)
        ks = jax.random.split(key, 10)
        sd = 1.0 / np.sqrt(D)
        ss = 1.0 / np.sqrt(S)
        return {'x': jax.random.normal(ks[0], (B, T, D), dtype=jnp.float32), 'rms_w': jnp.ones((D,), dtype=jnp.float32), 'Wf_w': jax.random.uniform(ks[1], (S, D), minval=-sd, maxval=sd, dtype=jnp.float32), 'Wf_b': jax.random.uniform(ks[2], (S,), minval=-sd, maxval=sd, dtype=jnp.float32), 'Wzg_w': jax.random.uniform(ks[3], (S, D), minval=-sd, maxval=sd, dtype=jnp.float32), 'Wz_w': jax.random.uniform(ks[4], (S, D), minval=-sd, maxval=sd, dtype=jnp.float32), 'Wga_w': jax.random.uniform(ks[5], (S, D), minval=-sd, maxval=sd, dtype=jnp.float32), 'Wgb_w': jax.random.uniform(ks[6], (S, D), minval=-sd, maxval=sd, dtype=jnp.float32), 'Wout_w': jax.random.uniform(ks[7], (D, S), minval=-ss, maxval=ss, dtype=jnp.float32), 'Wout_b': jax.random.uniform(ks[8], (D,), minval=-ss, maxval=ss, dtype=jnp.float32)}
    _L0_attn_in = _L0_attn_setup()

    def _L0_ffn_setup():
        import jax, jax.numpy as jnp
        import numpy as np
        D_MODEL = 256
        D_FF = 1024
        N_EXPERTS = 4
        B, S = (2, 256)
        key = jax.random.key(seed)
        ks = jax.random.split(key, 6)
        scale = 0.02
        return {'hidden_states': jax.random.normal(ks[0], (B, S, D_MODEL), dtype=jnp.float32), 'Wr': jax.random.normal(ks[1], (D_MODEL, N_EXPERTS), dtype=jnp.float32) * scale, 'br': jnp.zeros((N_EXPERTS,), dtype=jnp.float32), 'Wg': jax.random.normal(ks[2], (N_EXPERTS, D_MODEL, D_FF), dtype=jnp.float32) * scale, 'Wu': jax.random.normal(ks[3], (N_EXPERTS, D_MODEL, D_FF), dtype=jnp.float32) * scale, 'Wd': jax.random.normal(ks[4], (N_EXPERTS, D_FF, D_MODEL), dtype=jnp.float32) * scale}
    _L0_ffn_in = _L0_ffn_setup()

    def _L1_attn_setup():
        import jax, jax.numpy as jnp
        import numpy as np
        BATCH, L = (2, 128)
        D_MODEL, D_INNER, D_STATE, DT_RANK, K = (256, 512, 16, 128, 4)

        def _reference_tuple_inner(hidden_states, W_in, conv_w, conv_b, W_x, W_dt, b_dt, A_log, D, W_out, b_out):
            b, l, _ = hidden_states.shape
            xz = jnp.einsum('bld,ed->bel', hidden_states, W_in)
            x, z = jnp.split(xz, 2, axis=1)
            conv_state = x[:, :, -K:]
            xc = jax.lax.conv_general_dilated(x, conv_w[:, None, :], window_strides=(1,), padding=[(K - 1, 0)], feature_group_count=D_INNER, dimension_numbers=('NCH', 'OIH', 'NCH'))
            xc = jax.nn.silu(xc + conv_b[None, :, None])
            x_dbl = jnp.einsum('bdl,ed->ble', xc, W_x)
            dt, Bm, Cm = jnp.split(x_dbl, [DT_RANK, DT_RANK + D_STATE], axis=-1)
            dt = jnp.einsum('blr,dr->bdl', dt, W_dt)
            delta = jax.nn.softplus(dt + b_dt[None, :, None])
            A = -jnp.exp(A_log)

            def step(state, inp):
                d_t, b_t, c_t, u_t = inp
                dA = jnp.exp(d_t[..., None] * A)
                state = dA * state + (d_t * u_t)[..., None] * b_t[:, None, :]
                y_t = jnp.einsum('bdn,bn->bd', state, c_t)
                return (state, y_t)
            xs = (delta.transpose(2, 0, 1), Bm.transpose(1, 0, 2), Cm.transpose(1, 0, 2), xc.transpose(2, 0, 1))
            init = jnp.zeros((b, D_INNER, D_STATE), delta.dtype)
            last_state, ys = jax.lax.scan(step, init, xs)
            y = ys.transpose(1, 2, 0) + D[None, :, None] * xc
            y = y * jax.nn.silu(z)
            out = jnp.einsum('bdl,ed->ble', y, W_out) + b_out
            return (out, conv_state, last_state)
        key = jax.random.key(seed)
        ks = jax.random.split(key, 9)
        g = lambda i, shape, s: jax.random.normal(ks[i], shape, jnp.float32) * s
        A_log = jnp.log(jnp.broadcast_to(jnp.arange(1, D_STATE + 1, dtype=jnp.float32), (D_INNER, D_STATE)))
        return {'hidden_states': g(0, (BATCH, L, D_MODEL), 1.0), 'W_in': g(1, (2 * D_INNER, D_MODEL), 0.02), 'conv_w': g(2, (D_INNER, K), 0.2), 'conv_b': g(3, (D_INNER,), 0.02), 'W_x': g(4, (DT_RANK + 2 * D_STATE, D_INNER), 0.02), 'W_dt': g(5, (D_INNER, DT_RANK), 0.02), 'b_dt': g(6, (D_INNER,), 0.02), 'A_log': A_log, 'D': jnp.ones((D_INNER,), jnp.float32), 'W_out': g(7, (D_MODEL, D_INNER), 0.02), 'b_out': g(8, (D_MODEL,), 0.02)}
    _L1_attn_in = _L1_attn_setup()

    def _L1_ffn_setup():
        import jax, jax.numpy as jnp
        import numpy as np

        def binarize_weight(w):
            alpha = jnp.mean(jnp.abs(w), axis=tuple(range(1, w.ndim)), keepdims=True)
            bw = jnp.where(w >= 0, 1.0, -1.0) * alpha
            return jax.lax.stop_gradient(bw - w) + w
        key = jax.random.key(seed)
        k1, k2, k3 = jax.random.split(key, 3)
        in_features, out_features = (256, 256)
        x = jax.random.normal(k1, (8, 256, in_features), dtype=jnp.float32)
        std = np.sqrt(2.0 / out_features).astype(np.float32)
        weight = jax.random.normal(k2, (out_features, in_features), dtype=jnp.float32) * std
        bias = jax.random.normal(k3, (out_features,), dtype=jnp.float32) * 0.01
        return {'x': x, 'weight': weight, 'bias': bias}
    _L1_ffn_in = _L1_ffn_setup()
    _d = {'L0_attn_x': _L0_attn_in['x'], 'L0_attn_rms_w': _L0_attn_in['rms_w'], 'L0_attn_Wf_w': _L0_attn_in['Wf_w'], 'L0_attn_Wf_b': _L0_attn_in['Wf_b'], 'L0_attn_Wzg_w': _L0_attn_in['Wzg_w'], 'L0_attn_Wz_w': _L0_attn_in['Wz_w'], 'L0_attn_Wga_w': _L0_attn_in['Wga_w'], 'L0_attn_Wgb_w': _L0_attn_in['Wgb_w'], 'L0_attn_Wout_w': _L0_attn_in['Wout_w'], 'L0_attn_Wout_b': _L0_attn_in['Wout_b'], 'L0_ffn_Wr': _L0_ffn_in['Wr'], 'L0_ffn_br': _L0_ffn_in['br'], 'L0_ffn_Wg': _L0_ffn_in['Wg'], 'L0_ffn_Wu': _L0_ffn_in['Wu'], 'L0_ffn_Wd': _L0_ffn_in['Wd'], 'L1_attn_W_in': _L1_attn_in['W_in'], 'L1_attn_conv_w': _L1_attn_in['conv_w'], 'L1_attn_conv_b': _L1_attn_in['conv_b'], 'L1_attn_W_x': _L1_attn_in['W_x'], 'L1_attn_W_dt': _L1_attn_in['W_dt'], 'L1_attn_b_dt': _L1_attn_in['b_dt'], 'L1_attn_A_log': _L1_attn_in['A_log'], 'L1_attn_D': _L1_attn_in['D'], 'L1_attn_W_out': _L1_attn_in['W_out'], 'L1_attn_b_out': _L1_attn_in['b_out'], 'L1_ffn_weight': _L1_ffn_in['weight'], 'L1_ffn_bias': _L1_ffn_in['bias']}
    _x0 = _d['L0_attn_x']
    _d['L0_attn_x'] = jax.random.normal(jax.random.fold_in(jax.random.key(seed), 1), (2, 2048, 256), dtype=_x0.dtype)
    del _x0
    return _d

def reference(L0_attn_x, L0_attn_rms_w, L0_attn_Wf_w, L0_attn_Wf_b, L0_attn_Wzg_w, L0_attn_Wz_w, L0_attn_Wga_w, L0_attn_Wgb_w, L0_attn_Wout_w, L0_attn_Wout_b, L0_ffn_Wr, L0_ffn_br, L0_ffn_Wg, L0_ffn_Wu, L0_ffn_Wd, L1_attn_W_in, L1_attn_conv_w, L1_attn_conv_b, L1_attn_W_x, L1_attn_W_dt, L1_attn_b_dt, L1_attn_A_log, L1_attn_D, L1_attn_W_out, L1_attn_b_out, L1_ffn_weight, L1_ffn_bias):

    def _L0_attn_ref(x, rms_w, Wf_w, Wf_b, Wzg_w, Wz_w, Wga_w, Wgb_w, Wout_w, Wout_b):
        import jax, jax.numpy as jnp
        import numpy as np
        B, T, D, S = (4, 512, 256, 256)
        EPS = 1e-05

        def _rmsnorm(x, w, eps):
            var = jnp.mean(jnp.square(x), axis=-1, keepdims=True)
            return x * jax.lax.rsqrt(var + eps) * w

        def _linear_scan(f, z):

            def step(h, fz):
                f_t, z_t = fz
                h = f_t * h + z_t
                return (h, h)
            h0 = jnp.zeros((f.shape[0], f.shape[2]), dtype=f.dtype)
            fT = jnp.swapaxes(f, 0, 1)
            zT = jnp.swapaxes(z, 0, 1)
            _, hs = jax.lax.scan(step, h0, (fT, zT))
            return jnp.swapaxes(hs, 0, 1)
        residual = x
        xn = _rmsnorm(x, rms_w, EPS)
        ga = jnp.einsum('btd,sd->bts', xn, Wga_w)
        gb = jnp.einsum('btd,sd->bts', xn, Wgb_w)
        out_gate = jax.nn.silu(ga) * gb
        f = jax.nn.sigmoid(jnp.einsum('btd,sd->bts', xn, Wf_w) + Wf_b)
        z = jnp.einsum('btd,sd->bts', xn, Wz_w) * jax.nn.sigmoid(jnp.einsum('btd,sd->bts', xn, Wzg_w))
        h = _linear_scan(f.astype(jnp.bfloat16), z.astype(jnp.bfloat16))
        gated = (out_gate.astype(jnp.bfloat16) * h).astype(jnp.float32)
        y = jnp.einsum('bts,ds->btd', gated, Wout_w) + Wout_b
        return y + residual

    def _L0_ffn_ref(hidden_states, Wr, br, Wg, Wu, Wd):
        import jax, jax.numpy as jnp
        import numpy as np
        D_MODEL = 256
        D_FF = 1024
        N_EXPERTS = 4
        B, S = (2, 256)
        b, s, d = hidden_states.shape
        x = hidden_states.reshape(-1, d)
        logits = x @ Wr + br
        probs = jax.nn.softmax(logits, axis=-1)
        top_w, top_idx = jax.lax.top_k(probs, 1)
        g = jnp.einsum('td,edf->tef', x, Wg)
        u = jnp.einsum('td,edf->tef', x, Wu)
        h = jax.nn.silu(g) * u
        y = jnp.einsum('tef,efd->ted', h, Wd)
        sel = jnp.take_along_axis(y, top_idx[:, :, None], axis=1)[:, 0]
        out = sel * top_w
        return out.reshape(b, s, d)

    def _L1_attn_ref(hidden_states, W_in, conv_w, conv_b, W_x, W_dt, b_dt, A_log, D, W_out, b_out):
        import jax, jax.numpy as jnp
        import numpy as np
        BATCH, L = (2, 128)
        D_MODEL, D_INNER, D_STATE, DT_RANK, K = (256, 512, 16, 128, 4)

        def _reference_tuple_inner(hidden_states, W_in, conv_w, conv_b, W_x, W_dt, b_dt, A_log, D, W_out, b_out):
            b, l, _ = hidden_states.shape
            xz = jnp.einsum('bld,ed->bel', hidden_states, W_in)
            x, z = jnp.split(xz, 2, axis=1)
            conv_state = x[:, :, -K:]
            xc = jax.lax.conv_general_dilated(x, conv_w[:, None, :], window_strides=(1,), padding=[(K - 1, 0)], feature_group_count=D_INNER, dimension_numbers=('NCH', 'OIH', 'NCH'))
            xc = jax.nn.silu(xc + conv_b[None, :, None])
            x_dbl = jnp.einsum('bdl,ed->ble', xc, W_x)
            dt, Bm, Cm = jnp.split(x_dbl, [DT_RANK, DT_RANK + D_STATE], axis=-1)
            dt = jnp.einsum('blr,dr->bdl', dt, W_dt)
            delta = jax.nn.softplus(dt + b_dt[None, :, None])
            A = -jnp.exp(A_log)

            def step(state, inp):
                d_t, b_t, c_t, u_t = inp
                dA = jnp.exp(d_t[..., None] * A)
                state = dA * state + (d_t * u_t)[..., None] * b_t[:, None, :]
                y_t = jnp.einsum('bdn,bn->bd', state, c_t)
                return (state, y_t)
            xs = (delta.transpose(2, 0, 1), Bm.transpose(1, 0, 2), Cm.transpose(1, 0, 2), xc.transpose(2, 0, 1))
            init = jnp.zeros((b, D_INNER, D_STATE), delta.dtype)
            last_state, ys = jax.lax.scan(step, init, xs)
            y = ys.transpose(1, 2, 0) + D[None, :, None] * xc
            y = y * jax.nn.silu(z)
            out = jnp.einsum('bdl,ed->ble', y, W_out) + b_out
            return (out, conv_state, last_state)
        return _reference_tuple_inner(hidden_states, W_in, conv_w, conv_b, W_x, W_dt, b_dt, A_log, D, W_out, b_out)[0]

    def _L1_ffn_ref(x, weight, bias):
        import jax, jax.numpy as jnp
        import numpy as np

        def binarize_weight(w):
            alpha = jnp.mean(jnp.abs(w), axis=tuple(range(1, w.ndim)), keepdims=True)
            bw = jnp.where(w >= 0, 1.0, -1.0) * alpha
            return jax.lax.stop_gradient(bw - w) + w
        bw = binarize_weight(weight)
        return jnp.einsum('bsi,oi->bso', x, bw) + bias
    x = L0_attn_x
    xn = _layernorm(x, axis=-1)
    s = _L0_attn_ref(xn, L0_attn_rms_w, L0_attn_Wf_w, L0_attn_Wf_b, L0_attn_Wzg_w, L0_attn_Wz_w, L0_attn_Wga_w, L0_attn_Wgb_w, L0_attn_Wout_w, L0_attn_Wout_b)
    g = _silu(_L0_ffn_ref(xn, L0_ffn_Wr, L0_ffn_br, L0_ffn_Wg, L0_ffn_Wu, L0_ffn_Wd))
    x = x + s * g
    xn = _layernorm(x, axis=-1)
    s = _L1_attn_ref(xn, L1_attn_W_in, L1_attn_conv_w, L1_attn_conv_b, L1_attn_W_x, L1_attn_W_dt, L1_attn_b_dt, L1_attn_A_log, L1_attn_D, L1_attn_W_out, L1_attn_b_out)
    g = _silu(_L1_ffn_ref(xn, L1_ffn_weight, L1_ffn_bias))
    x = x + s * g
    return x

_drawn_inputs = setup_inputs


def setup_inputs(seed=0):
    import zlib

    import numpy as np

    out = dict(_drawn_inputs(seed))
    spreads = {'L0_attn_rms_w': (1.0, 0.2), 'L0_ffn_br': (0.0, 0.1), 'L1_attn_D': (1.0, 0.2)}
    factors = {}
    for name, (base, spread) in spreads.items():
        noise = np.random.default_rng([zlib.crc32(name.encode()), seed]).standard_normal(out[name].shape)
        drawn = base * np.exp(spread * noise) if base else spread * noise
        out[name] = jnp.asarray(drawn.astype(out[name].dtype))
    for name, factor in factors.items():
        out[name] = (out[name] * factor).astype(out[name].dtype)
    return out
```

```python
from contextlib import ExitStack

import concourse.bass as bass
from concourse import mybir

P = 128
B, T, D = 2, 2048, 256
KB = D // P
TILES = B * T // P
TPC = 4
CH = TPC * P
CPB = T // CH
CHUNKS = B * CPB
TPB = T // P
S0 = 256
SB = S0 // P
NE, FF = 4, 1024
FB = FF // P
HALF = FF // 2
SLOTS = TILES + NE - 1
ROWS = SLOTS + 1
DI, DS, DR, KC = 512, 16, 128, 4
DB = DI // P
XR = DR + 2 * DS
EPS = 1e-5

F32 = mybir.dt.float32
BF16 = mybir.dt.bfloat16
I32 = mybir.dt.int32
U32 = mybir.dt.uint32
ALU = mybir.AluOpType
ACT = mybir.ActivationFunctionType
AX_X = mybir.AxisListType.X

PROJ_F, PROJ_ZG, PROJ_Z, PROJ_GA, PROJ_GB = range(5)
GROUPS = 2 + 2 + 8 + 1 + 1 + DB
G_XNT, G_GATE, G_IN, G_DT, G_BC, G_DELTA = 0, 2, 4, 12, 13, 14
STATE_BUFS = 2
DA_BUFS = 2


def build(nc, a, out):
    with ExitStack() as ctx:
        def sem(name):
            return ctx.enter_context(nc.semaphore(name))

        def sb(stack, name, shape, dt=F32):
            return stack.enter_context(nc.sbuf_tensor(name, shape, dt))

        sorted_x = nc.dram_tensor("sorted_x", (ROWS * P, D), F32).ap()
        sorted_y = nc.dram_tensor("sorted_y", (SLOTS * P, D), F32).ap()
        mixed = nc.dram_tensor("mixed", (P, TILES, D), F32).ap()

        ident = sb(ctx, "ident", [P, P])
        ones = sb(ctx, "ones", [P, P])
        w_in = sb(ctx, "w_in", [P, KB, 2 * DI])
        w_x = sb(ctx, "w_x", [P, DB, XR])
        w_dt = sb(ctx, "w_dt", [P, DI])
        w_out = sb(ctx, "w_out", [P, DB, D])
        bwT = sb(ctx, "bwT", [P, KB, D])
        bias1 = sb(ctx, "bias1", [1, 2, D])
        cols1 = sb(ctx, "cols1", [P, DB, KC + 3])
        negA = sb(ctx, "negA", [P, DB, DS])
        dest_u = sb(ctx, "dest_u", [P, TILES], U32)
        top_w = sb(ctx, "top_w", [P, TILES])
        idx4 = sb(ctx, "idx4", [P, TPC], U32)
        neg_half = sb(ctx, "neg_half", [P, TILES])

        l0 = ExitStack()
        x_sb = sb(l0, "x_sb", [P, TILES, D])
        w_g = sb(l0, "w_g", [P, NE * KB * FF])
        w_u = sb(l0, "w_u", [P, NE * KB * FF])
        w_d = sb(l0, "w_d", [P, NE * FB * D])
        w0 = sb(l0, "w0", [P, 5, KB, S0])
        wo_f = sb(l0, "wo_f", [P, SB, D])
        wo_b = sb(l0, "wo_b", [P, 3, SB, D], BF16)
        bias0 = sb(l0, "bias0", [1, D])
        cols0 = sb(l0, "cols0", [P, 2, 2])
        w_r = sb(l0, "w_r", [P, KB, NE])
        tri = sb(l0, "tri", [P, P])
        small = sb(l0, "small", [P, 2 * NE + TILES + SLOTS + 1])
        st0 = sb(l0, "st0", [P, TILES, 6])
        mean0 = sb(l0, "mean0", [P, TILES])
        var0 = sb(l0, "var0", [P, TILES])
        tmp0 = sb(l0, "tmp0", [P, 4, TILES])
        rstd0 = sb(l0, "rstd0", [P, TILES])
        rr0 = sb(l0, "rr0", [P, TILES])
        rt = sb(l0, "rt", [P, 8, TILES, NE])
        rs = sb(l0, "rs", [P, 8, TILES])
        eidf = sb(l0, "eidf", [1, SLOTS + 1, NE])
        eid = sb(l0, "eid", [1, SLOTS + 1], I32)
        xn_st = sb(l0, "xn_st", [P, TPC, D])
        xr_st = sb(l0, "xr_st", [P, TPC, D])
        xT = sb(l0, "xT", [P, KB, CH])
        f_sb = sb(l0, "f_sb", [P, SB, CH], BF16)
        z_sb = sb(l0, "z_sb", [P, SB, CH], BF16)
        og_sb = sb(l0, "og_sb", [P, SB, CH], BF16)
        h_sb = sb(l0, "h_sb", [P, SB, CH], BF16)
        gated = sb(l0, "gated", [P, SB, CH], BF16)
        carry0 = sb(l0, "carry0", [P, SB], BF16)
        sg_z = sb(l0, "sg_z", [P, SB, CH])
        sg_a = sb(l0, "sg_a", [P, SB, CH])
        mix_st = rt[:].rearrange("p k t e -> p (k t e)").rearrange("p (t d) -> p t d", d=D)
        xg = sb(l0, "xg", [P, 2, D])
        wo_r = xr_st[:, 0:SB, :]
        xgT = f_sb[:].bitcast(F32).rearrange("p s c -> p (s c)")[:, 0:KB * P].rearrange("p (k t) -> p k t", k=KB)
        silu_g, hid = sg_z, sg_a
        hidT = xT[:].rearrange("p k c -> p (k c)").rearrange("p (f t) -> p f t", t=P)
        ye = h_sb[:].bitcast(F32)
        bw_w, bw_t = gated[:].bitcast(F32), wo_f
        bw_a = sb(l0, "bw_a", [P, KB])
        l0.close()

        l1 = ExitStack()
        xpad = [sb(l1, f"xpad{b}", [P, DB, KC - 1 + CH]) for b in range(B)]
        z_silu = [sb(l1, f"z_silu{b}", [P, DB, CH]) for b in range(B)]
        xc = [sb(l1, f"xc{b}", [P, DB, CH]) for b in range(B)]
        delta = [sb(l1, f"delta{b}", [P, DB, CH]) for b in range(B)]
        du = [sb(l1, f"du{b}", [P, DB, CH]) for b in range(B)]
        bc_rows = [sb(l1, f"bc_rows{b}", [2 * DS, CH]) for b in range(B)]
        g_silu = [sb(l1, f"g_silu{b}", [P, TPC, D]) for b in range(B)]
        x1 = [sb(l1, f"x1_{b}", [P, TPC, D]) for b in range(B)]
        carry1 = [sb(l1, f"carry1_{b}", [P, DS, DB]) for b in range(B)]
        dbu = [sb(l1, f"dbu{i}", [P, DB, CH]) for i in range(2)]
        hst = [sb(l1, f"hst{i}", [P, DB, CH]) for i in range(STATE_BUFS)]
        c_bc = sb(l1, "c_bc", [P, 2, CH])
        soft = sb(l1, "soft", [P, DB, CH])
        y_fin = sb(l1, "y_fin", [P, DB, CH])
        yg = sb(l1, "yg", [P, TPC, D])
        mix1 = sb(l1, "mix1", [P, TPC, D])
        xn2T = sb(l1, "xn2T", [P, KB, CH])
        dt_sb = sb(l1, "dt_sb", [P, CH])
        o_st = sb(l1, "o_st", [P, TPC, D])
        st1 = sb(l1, "st1", [P, TPC, 6])
        ln1 = sb(l1, "ln1", [P, 8, TPC])
        l1.close()

        bank = [ctx.enter_context(nc.psum_tensor(f"bank{i}", [P, 512], F32)) for i in range(8)]

        ld_x = [sem(f"ld_x{i}") for i in range(2)]
        ld_small = sem("ld_small")
        ld_w0 = sem("ld_w0")
        ld_moe = sem("ld_moe")
        ld_w1 = sem("ld_w1")
        ld_bw = sem("ld_bw")
        zero_set = sem("zero_set")
        pool_passed = sem("pool_passed")
        zero_filled = sem("zero_filled")
        v0 = sem("v0")
        set_done = sem("set_done")
        stats_ready = sem("stats_ready")
        rstd_ready = sem("rstd_ready")
        xn_ready = sem("xn_ready")
        xn_turned = sem("xn_turned")
        xnT_ready = sem("xnT_ready")
        logits_ready = sem("logits_ready")
        shifted = sem("shifted")
        exp_ready = sem("exp_ready")
        onehot_ready = sem("onehot_ready")
        ranks_ready = sem("ranks_ready")
        st_ready = sem("st_ready")
        xr_turned = sem("xr_turned")
        xrT_ready = sem("xrT_ready")
        proj_ready = sem("proj_ready")
        sig_ready = sem("sig_ready")
        carry_set = sem("carry_set")
        v_l0 = sem("v_l0")
        gated_ready = sem("gated_ready")
        mix_ready = sem("mix_ready")
        mix_added = sem("mix_added")
        mix_stored = sem("mix_stored")
        scattered = sem("scattered")
        eid_ready = sem("eid_ready")
        xg_loaded = [sem(f"xg_loaded{i}") for i in range(2)]
        xg_turned = sem("xg_turned")
        xgT_ready = sem("xgT_ready")
        up_ready = sem("up_ready")
        silu_ready = sem("silu_ready")
        hid_ready = sem("hid_ready")
        hid_turned = sem("hid_turned")
        hidT_ready = sem("hidT_ready")
        down_ready = sem("down_ready")
        ye_ready = sem("ye_ready")
        ye_stored = [sem(f"ye_stored{i}") for i in range(2)]
        bw_ready = sem("bw_ready")
        bw_turned = sem("bw_turned")
        bwT_ready = sem("bwT_ready")
        layer0_done = sem("layer0_done")
        x_in = sem("x_in")
        idx_ready = sem("idx_ready")
        y_in = sem("y_in")
        y_silu = sem("y_silu")
        v_pre = sem("v_pre")
        var1_ready = sem("var1_ready")
        rstd1_ready = sem("rstd1_ready")
        xn2_ready = sem("xn2_ready")
        pre_full = sem("pre_full")
        pre_free = sem("pre_free")
        conv_ready = sem("conv_ready")
        xc_ready = sem("xc_ready")
        soft_ready = sem("soft_ready")
        a_pre = sem("a_pre")
        delta_ready = sem("delta_ready")
        du_ready = sem("du_ready")
        scan_set = sem("scan_set")
        bc_full = sem("bc_full")
        c_ready = sem("c_ready")
        dA_ready = sem("dA_ready")
        dbu_ready = sem("dbu_ready")
        scan_done = sem("scan_done")
        carry_done = sem("carry_done")
        hc_ready = sem("hc_ready")
        y_added = sem("y_added")
        skip_added = sem("skip_added")
        y_ready = sem("y_ready")
        out_full = sem("out_full")
        out_mul = sem("out_mul")
        out_ready = sem("out_ready")
        stored = sem("stored")

        block = ctx.enter_context(nc.Block())

        def wait_past(eng, semaphore, value):
            if not isinstance(value, int) or value > 0:
                eng.wait_ge(semaphore, value)

        @block.sync
        def _(sp):
            half = TILES // 2
            for i in range(2):
                for q in range(4):
                    lo = i * half + q * half // 4
                    sp.dma_start(x_sb[:, lo:lo + half // 4, :], a["x"][:, lo:lo + half // 4, :]).then_inc(ld_x[i], 16)
            for t, name in ((cols0, "cols0"), (w_r, "w_r"), (tri, "tri"), (small, "small"), (bias0, "bias0"),
                            (ident, "ident")):
                sp.dma_start(t[:], a[name]).then_inc(ld_small, 16)
            sp.dma_start(w0[:], a["w0"]).then_inc(ld_w0, 16)
            sp.dma_start(wo_f[:], a["wo"]).then_inc(ld_w0, 16)
            sp.wait_ge(zero_set, 1)
            for s in range(0, ROWS, TPC):
                sp.dma_start(sorted_x[s * P:(s + TPC) * P, :].rearrange("(n p) d -> p n d", p=P),
                             xn_st[:]).then_inc(zero_filled, 16)
            for t, name in ((w_g, "w_g"), (w_u, "w_u"), (w_d, "w_d")):
                sp.dma_start(t[:], a[name]).then_inc(ld_moe, 16)
            for t, name in ((w_in, "w_in"), (w_x, "w_x"), (w_dt, "w_dt"), (w_out, "w_out"), (bias1, "bias1"),
                            (cols1, "cols1"), (negA, "a_log")):
                sp.dma_start(t[:], a[name]).then_inc(ld_w1, 16)

            with sp.Fori(0, CHUNKS) as c:
                sp.wait_ge(mix_added, 2 * c + 2)
                sp.dma_start(mixed[:, bass.ds(c * TPC, TPC), :], mix_st).then_inc(mix_stored, 16)

            sp.dma_start(bw_w, a["bw_w"]).then_inc(ld_bw, 16)
            sp.wait_ge(scattered, 16 * TILES)

            def load(j, u):
                sp.dma_start(xg[:, u, :], sorted_x[bass.ds(j * P, P), :]).then_inc(xg_loaded[u], 16)

            def store(j, u):
                sp.wait_ge(ye_ready, j + 1)
                sp.dma_start(sorted_y[bass.ds(j * P, P), :], ye[:, u, :]).then_inc(ye_stored[u], 16)

            load(0, 0)
            load(1, 1)
            with sp.Fori(0, (SLOTS - 1) // 2) as jj:
                for u in range(2):
                    j = 2 * jj + u
                    sp.wait_ge(xg_turned, j + 1)
                    load(j + 2, u)
                    store(j, u)
            store(SLOTS - 1, 0)
            sp.wait_ge(mix_stored, 16 * CHUNKS)
            sp.wait_ge(ye_stored[0], 16 * ((SLOTS + 1) // 2))
            sp.wait_ge(ye_stored[1], 16 * (SLOTS // 2))
            sp.sem_inc(layer0_done, 1)
            sp.wait_ge(layer0_done, 5)

            def load_chunk(q, b, j):
                sp.dma_start(x1[b][:], a["x"][:, bass.ds(b * TPB + j * TPC, TPC), :]).then_inc(x_in, 16)
                sp.dma_start(mix1[:], mixed[:, bass.ds(b * TPB + j * TPC, TPC), :]).then_inc(x_in, 16)

            def store_chunk(q, b, j):
                sp.wait_ge(out_ready, 2 * q + 2)
                sp.dma_start(out[:, bass.ds(b * TPB + j * TPC, TPC), :], o_st[:]).then_inc(stored, 16)

            load_chunk(0, 0, 0)
            sp.wait_ge(xn2_ready, 1)
            load_chunk(1, 1, 0)
            with sp.Fori(0, CPB - 1) as j:
                for b in range(B):
                    q = B * j + b
                    store_chunk(q, b, j)
                    sp.wait_ge(xn2_ready, q + 2)
                    load_chunk(q + 2, b, j + 1)
            for b in range(B):
                store_chunk(B * (CPB - 1) + b, b, CPB - 1)
            sp.wait_ge(stored, 16 * CHUNKS)

        @block.gpsimd
        def _(pool):
            pool.memset(xn_st[:], 0.0).then_inc(zero_set, 1)
            pool.memset(neg_half[:], -0.5).then_inc(set_done, 1)
            pool.memset(ones[:], 1.0).then_inc(set_done, 1)
            pool.wait_ge(set_done, 2)
            for k, dst in enumerate((rstd0, rr0)):
                pool.wait_ge(stats_ready, k + 1)
                pool.tensor_tensor(dst[:], tmp0[:, k, :], neg_half[:], ALU.pow).then_inc(rstd_ready, 1)
            pool.wait_ge(zero_filled, 16 * (ROWS // TPC))
            with pool.Fori(0, CHUNKS) as c:
                pool.wait_ge(st_ready, c + 1)
                pool.sem_inc(pool_passed, 1)
                for i in range(TPC):
                    pool.indirect_dma_start(
                        sorted_x[:], bass.IndirectOffsetOnAxis(idx4[:, i:i + 1], 0), xn_st[:, i, :], None,
                    ).then_inc(scattered, 16)
            pool.wait_ge(scattered, 16 * TILES)
            pool.sem_inc(layer0_done, 1)
            pool.wait_ge(layer0_done, 5)

            def fetch_experts(q):
                pool.wait_ge(idx_ready, q + 1)
                wait_past(pool, pre_full, GROUPS * q)
                pool.sem_inc(pool_passed, 1)
                for i in range(TPC):
                    pool.indirect_dma_start(
                        yg[:, i, :], None, sorted_y[:], bass.IndirectOffsetOnAxis(idx4[:, i:i + 1], 0),
                    ).then_inc(y_in, 16)

            def rstd(q):
                pool.wait_ge(var1_ready, q + 1)
                pool.tensor_tensor(ln1[:, 5, :], ln1[:, 4, :], neg_half[:, 0:TPC], ALU.pow).then_inc(rstd1_ready, 1)

            def delta_and_du(q, b):
                for d in range(DB):
                    pool.wait_ge(soft_ready, 2 * q + 2)
                    pool.tensor_tensor(delta[b][:, d, :], delta[b][:, d, :], soft[:, d, :],
                                       ALU.add).then_inc(delta_ready, 1)
                for d in range(DB):
                    pool.wait_ge(delta_ready, DB * q + d + 1)
                    pool.tensor_tensor(du[b][:, d, :], delta[b][:, d, :], xc[b][:, d, :],
                                       ALU.mult).then_inc(du_ready, 1)

            def prepare(q, b, n):
                if n == 2:
                    fetch_experts(q)
                if n == 3:
                    rstd(q)
                if n == 14:
                    delta_and_du(q, b)

            def scan(q, b, ahead):
                for n in range(DS):
                    g = DS * q + n
                    pool.wait_ge(carry_done, g + 1)
                    pool.wait_ge(c_ready, g + 1)
                    h = hst[n % STATE_BUFS]
                    pool.tensor_tensor(h[:], h[:], c_bc[:, n % 2, :].unsqueeze(1).broadcast_to([P, DB, CH]),
                                       ALU.mult).then_inc(hc_ready, 1)
                    if ahead:
                        prepare(q + 1, 1 - b, n)

            pool.sem_inc(hc_ready, 2)
            for n in range(DS):
                prepare(0, 0, n)
            with pool.Fori(0, CPB - 1) as j:
                for b in range(B):
                    scan(B * j + b, b, True)
            scan(CHUNKS - 2, 0, True)
            scan(CHUNKS - 1, 1, False)

        @block.scalar
        def _(act):
            act.wait_ge(ld_small, 16 * 6)
            def turn_normed(c):
                for k in range(KB):
                    act.wait_ge(xn_turned, KB * c + k + 1)
                    act.copy(xT[:, k, :], bank[k][:]).then_inc(xnT_ready, 1)

            turn_normed(0)
            with act.Fori(1, CHUNKS) as c:
                turn_normed(c)
            act.wait_ge(shifted, 1)
            act.activation(rt[:, 2], rt[:, 1], ACT.Exp).then_inc(exp_ready, 1)

            def mixer(c):
                for k in range(KB):
                    act.wait_ge(xr_turned, KB * c + k + 1)
                    wait_past(act, proj_ready, 10 * c)
                    act.activation(xT[:, k, :], bank[k][:], ACT.Copy, scale=cols0[:, k, 0:1]).then_inc(xrT_ready, 1)
                for s in range(SB):
                    r = 10 * c + 5 * s
                    act.wait_ge(proj_ready, r + PROJ_F + 1)
                    wait_past(act, gated_ready, SB * c)
                    act.activation(f_sb[:, s, :], bank[2 + PROJ_F][:], ACT.Sigmoid,
                                   bias=cols0[:, s, 1:2]).then_inc(sig_ready, 1)
                    act.wait_ge(proj_ready, r + PROJ_ZG + 1)
                    act.activation(sg_z[:, s, :], bank[2 + PROJ_ZG][:], ACT.Sigmoid).then_inc(sig_ready, 1)
                    act.wait_ge(proj_ready, r + PROJ_GA + 1)
                    act.activation(sg_a[:, s, :], bank[2 + PROJ_GA][:], ACT.Sigmoid).then_inc(sig_ready, 1)

            mixer(0)
            with act.Fori(1, CHUNKS) as c:
                mixer(c)

            def turn_in(j):
                act.wait_ge(xg_turned, j + 1)
                act.copy(xgT, bank[0][:, 0:D]).then_inc(xgT_ready, 1)

            def gate(j, half):
                act.wait_ge(up_ready, 2 * j + half + 1)
                act.activation(silu_g[:, half, :], bank[1 + 2 * half][:], ACT.Silu).then_inc(silu_ready, 1)

            def turn_hidden(j, half):
                act.wait_ge(hid_turned, 2 * j + half + 1)
                act.copy(hidT[:, half * FB // 2:(half + 1) * FB // 2, :], bank[5 + half][:]).then_inc(hidT_ready, 1)

            turn_in(0)
            gate(0, 0)
            gate(0, 1)
            turn_hidden(0, 0)
            turn_in(1)
            with act.Fori(0, SLOTS - 1) as jj:
                j = jj + 1
                gate(j, 0)
                turn_hidden(j - 1, 1)
                gate(j, 1)
                turn_hidden(j, 0)
                turn_in(j + 1)
            turn_hidden(SLOTS - 1, 1)
            act.wait_ge(ld_w1, 16 * 7)
            act.activation(negA[:], negA[:], ACT.Exp).then_inc(a_pre, 1)
            act.wait_ge(a_pre, 1)
            act.mul(negA[:], negA[:], -1.0).then_inc(a_pre, 1)
            for k in range(KB):
                act.wait_ge(bw_turned, k + 1)
                act.copy(bwT[:, k, :], bank[6 + k][:, 0:D]).then_inc(bwT_ready, 1)
            act.wait_ge(a_pre, 2)
            act.wait_ge(bwT_ready, KB)
            act.sem_inc(layer0_done, 1)
            act.wait_ge(layer0_done, 5)

            M = bank[7]

            def take(q, m):
                act.wait_ge(pre_full, GROUPS * q + m + 1)

            def silu_experts(q, b, j):
                act.wait_ge(y_in, 64 * q + 64)
                for i in range(TPC):
                    act.activation(yg[:, i, :], yg[:, i, :], ACT.Silu,
                                   scale=top_w[:, bass.ds(b * TPB + j * TPC + i, 1)]).then_inc(y_silu, 1)

            def turn_xn2(q):
                for k in range(KB):
                    take(q, G_XNT + k)
                    act.copy(xn2T[:, k, :], M[:]).then_inc(pre_free, 1)

            def gates(q, b):
                for h in range(2):
                    take(q, G_GATE + h)
                    act.activation(g_silu[b][:, 2 * h:2 * h + 2, :], M[:], ACT.Silu).then_inc(pre_free, 1)

            def x_half(q, b):
                for d in range(DB):
                    take(q, G_IN + d)
                    act.wait_ge(v_pre, PRE_STEPS * q + PRE_HALO)
                    act.copy(xpad[b][:, d, KC - 1:], M[:]).then_inc(pre_free, 1)

            def z_half(q, b):
                for d in range(DB):
                    take(q, G_IN + DB + d)
                    act.activation(z_silu[b][:, d, :], M[:], ACT.Silu).then_inc(pre_free, 1)

            def silu_conv(q, b):
                for d in range(DB):
                    act.wait_ge(conv_ready, DB * q + d + 1)
                    act.activation(xc[b][:, d, :], soft[:, d, :], ACT.Silu,
                                   bias=cols1[:, d, KC:KC + 1]).then_inc(xc_ready, 1)

            def low_rank(q, b):
                take(q, G_DT)
                act.copy(dt_sb[:], M[:]).then_inc(pre_free, 1)
                take(q, G_BC)
                act.copy(bc_rows[b][:], M[0:2 * DS, :]).then_inc(pre_free, 1)

            def softplus(q, b):
                for d in range(DB):
                    take(q, G_DELTA + d)
                    act.activation(soft[:, d, :], M[:], ACT.Abs, bias=cols1[:, d, KC + 1:KC + 2]).then_inc(a_pre, 1)
                    act.activation(delta[b][:, d, :], M[:], ACT.Relu,
                                   bias=cols1[:, d, KC + 1:KC + 2]).then_inc(pre_free, 1)
                act.wait_ge(a_pre, 2 + DB * (q + 1))
                act.activation(soft[:], soft[:], ACT.Exp, scale=-1.0).then_inc(soft_ready, 1)
                act.wait_ge(soft_ready, 2 * q + 1)
                act.wait_ge(pre_free, GROUPS * (q + 1))
                act.activation(soft[:], soft[:], ACT.Ln, bias=ones[:, 0:1]).then_inc(soft_ready, 1)

            def prepare(q, b, j, n):
                if n == 3:
                    silu_experts(q, b, j)
                if n == 6:
                    turn_xn2(q)
                if n == 7:
                    gates(q, b)
                if n == 8:
                    x_half(q, b)
                if n == 10:
                    z_half(q, b)
                if n == 12:
                    silu_conv(q, b)
                if n == 13:
                    low_rank(q, b)
                if n == 14:
                    softplus(q, b)

            def scan(q, b, ahead):
                for n in range(DS):
                    g = DS * q + n
                    act.wait_ge(bc_full, 2 * g + 1)
                    act.wait_ge(hc_ready, g + 1)
                    act.copy(c_bc[:, n % 2, :], bank[6][:]).then_inc(c_ready, 1)
                    for d in range(DB):
                        u = DB * g + d
                        if n == 0:
                            act.wait_ge(delta_ready, DB * q + d + 1)
                        act.wait_ge(scan_done, u + 1)
                        act.activation(bank[4 + u_bank(d)][:], delta[b][:, d, :], ACT.Exp,
                                       scale=negA[:, d, n:n + 1]).then_inc(dA_ready, 1)
                    if ahead is not None:
                        prepare(q + 1, 1 - b, ahead, n)

            for n in range(DS):
                prepare(0, 0, 0, n)
            with act.Fori(0, CPB - 1) as j:
                for b in range(B):
                    scan(B * j + b, b, j + b)
            scan(CHUNKS - 2, 0, CPB - 1)
            scan(CHUNKS - 1, 1, None)

        @block.vector
        def _(v):
            steps = [0]

            def then(ins):
                steps[0] += 1
                ins.then_inc(v0, 1)
                v.wait_ge(v0, steps[0])

            for i in range(2):
                v.wait_ge(ld_x[i], 64)
                with v.Fori(0, TILES // 2) as t:
                    v.bn_stats(st0[:, bass.ds(t + i * TILES // 2, 1), :], x_sb[:, bass.ds(t + i * TILES // 2, 1), :]).then_inc(xn_ready, 1)
            v.wait_ge(xn_ready, TILES)
            me, qe, mo, qo = (st0[:, :, k] for k in (1, 2, 4, 5))
            then(v.tensor_tensor(mean0[:], me, mo, ALU.add))
            then(v.tensor_scalar(mean0[:], mean0[:], 0.5, None, ALU.mult))
            then(v.tensor_tensor(tmp0[:, 2, :], me, mo, ALU.subtract))
            then(v.scalar_tensor_tensor(tmp0[:, 2, :], tmp0[:, 2, :], 0.25, tmp0[:, 2, :], ALU.mult, ALU.mult))
            then(v.tensor_tensor(tmp0[:, 3, :], qe, qo, ALU.add))
            then(v.scalar_tensor_tensor(var0[:], tmp0[:, 3, :], 1.0 / D, tmp0[:, 2, :], ALU.mult, ALU.add))
            v.tensor_scalar(tmp0[:, 0, :], var0[:], EPS, None, ALU.add).then_inc(stats_ready, 1)
            v.wait_ge(rstd_ready, 1)
            then(v.tensor_tensor(tmp0[:, 2, :], rstd0[:], rstd0[:], ALU.mult))
            then(v.tensor_tensor(tmp0[:, 2, :], tmp0[:, 2, :], var0[:], ALU.mult))
            v.tensor_scalar(tmp0[:, 1, :], tmp0[:, 2, :], EPS, None, ALU.add).then_inc(stats_ready, 1)
            v.wait_ge(rstd_ready, 2)
            then(v.tensor_tensor(rr0[:], rr0[:], rstd0[:], ALU.mult))

            v.wait_ge(zero_filled, 16 * (ROWS // TPC))
            def normed_tiles(c):
                wait_past(v, xn_turned, KB * c)
                for i in range(TPC):
                    t = c * TPC + i
                    v.tensor_scalar(xn_st[:, i, :], x_sb[:, bass.ds(t, 1), :], mean0[:, bass.ds(t, 1)],
                                    rstd0[:, bass.ds(t, 1)], ALU.subtract, ALU.mult).then_inc(xn_ready, 1)

            normed_tiles(0)
            with v.Fori(1, CHUNKS) as c:
                normed_tiles(c)

            def per_tile(x):
                return x.unsqueeze(2).broadcast_to([P, TILES, NE])

            def per_expert(x):
                return x.unsqueeze(1).broadcast_to([P, TILES, NE])

            br, prio = small[:, 0:NE], small[:, NE:2 * NE]
            steps128 = small[:, 2 * NE:2 * NE + TILES]
            slot_no = small[0:1, 2 * NE + TILES:]
            logits, shift, ex, eq, oh, tot, cum = (rt[:, k] for k in range(7))
            v.wait_ge(logits_ready, CHUNKS)
            then(v.tensor_tensor(logits, bank[7][:, 0:TILES * NE].rearrange("p (t e) -> p t e", e=NE),
                                 per_expert(br), ALU.add))
            then(v.tensor_reduce(rs[:, 0, :], logits, AX_X, ALU.max))
            v.tensor_tensor(shift, logits, per_tile(rs[:, 0, :]), ALU.subtract).then_inc(shifted, 1)
            then(v.tensor_tensor(eq, logits, per_tile(rs[:, 0, :]), ALU.is_equal))
            then(v.tensor_tensor(eq, eq, per_expert(prio), ALU.mult))
            then(v.tensor_reduce(rs[:, 1, :], eq, AX_X, ALU.max))
            v.tensor_tensor(oh, eq, per_tile(rs[:, 1, :]), ALU.is_equal).then_inc(onehot_ready, 1)
            v.wait_ge(exp_ready, 1)
            then(v.tensor_reduce(rs[:, 2, :], ex, AX_X, ALU.add))
            then(v.reciprocal(top_w[:], rs[:, 2, :]))
            v.wait_ge(ranks_ready, 1)
            rank_ps = bank[6][:, 0:TILES * NE].rearrange("p (t e) -> p t e", e=NE)
            then(v.tensor_copy(tot, bank[6][:, TILES * NE:2 * TILES * NE]))
            then(v.memset(rs[:, 3, :], 1.0))
            for e in range(NE):
                then(v.tensor_tensor_scan(cum[:, :, e], rs[:, 3, :], tot[:, :, e], 0.0, ALU.mult, ALU.add))
            cnt = cum[:, TILES - 1, :]
            cmp = rt[:, 7].rearrange("p t e -> p (t e)").rearrange("p (e t) -> p e t", e=NE)
            then(v.tensor_tensor(cmp, cnt.unsqueeze(2).broadcast_to([P, NE, TILES]),
                                 steps128.unsqueeze(1).broadcast_to([P, NE, TILES]), ALU.is_gt))
            nt, end, start = rs[:, 4, 0:NE], rs[:, 5, 0:NE], rs[:, 6, 0:NE]
            then(v.tensor_reduce(nt, cmp, AX_X, ALU.add))
            then(v.tensor_tensor_scan(end, rs[:, 3, 0:NE], nt, 0.0, ALU.mult, ALU.add))
            then(v.tensor_tensor(start, end, nt, ALU.subtract))
            then(v.tensor_tensor(cum, cum, tot, ALU.subtract))
            then(v.tensor_tensor(cum, cum, rank_ps, ALU.add))
            then(v.scalar_tensor_tensor(cum, per_expert(start), float(P), cum, ALU.mult, ALU.add))
            then(v.tensor_tensor(cum, cum, oh, ALU.mult))
            then(v.tensor_reduce(rs[:, 7, :], cum, AX_X, ALU.add))
            then(v.tensor_copy(dest_u[:], rs[:, 7, :]))
            n_slot = SLOTS + 1
            ef = eidf[:, :, 0:NE - 1]
            then(v.tensor_tensor(ef, slot_no.unsqueeze(2).broadcast_to([1, n_slot, NE - 1]),
                                 start[0:1, 1:NE].unsqueeze(1).broadcast_to([1, n_slot, NE - 1]), ALU.is_ge))
            then(v.tensor_reduce(eidf[:, :, NE - 1], ef, AX_X, ALU.add))
            v.tensor_copy(eid[:], eidf[:, :, NE - 1]).then_inc(eid_ready, 1)

            v.wait_ge(ld_w0, 32)
            then(v.tensor_copy(wo_b[:, 0], wo_f[:]))
            then(v.tensor_tensor(wo_r, wo_f[:], wo_b[:, 0], ALU.subtract))
            then(v.tensor_copy(wo_b[:, 1], wo_r))
            then(v.tensor_tensor(wo_r, wo_r, wo_b[:, 1], ALU.subtract))
            then(v.tensor_copy(wo_b[:, 2], wo_r))

            def mixer(c, b):
                k = [0]

                def chain(ins):
                    k[0] += 1
                    ins.then_inc(v_l0, 1)
                    return c * L0_STEPS + k[0]

                wait_past(v, scattered, 64 * c)
                wait_past(v, mix_added, 2 * c)
                for i in range(TPC):
                    t = c * TPC + i
                    v.tensor_scalar(xn_st[:, i, :], x_sb[:, bass.ds(t, 1), :], mean0[:, bass.ds(t, 1)],
                                    rstd0[:, bass.ds(t, 1)], ALU.subtract, ALU.mult)
                    v.tensor_scalar(xr_st[:, i, :], x_sb[:, bass.ds(t, 1), :], mean0[:, bass.ds(t, 1)],
                                    rr0[:, bass.ds(t, 1)], ALU.subtract, ALU.mult)
                v.tensor_copy(idx4[:], dest_u[:, bass.ds(c * TPC, TPC)]).then_inc(st_ready, 1)
                for s in range(SB):
                    r = 10 * c + 5 * s
                    v.wait_ge(proj_ready, r + PROJ_Z + 1)
                    v.wait_ge(sig_ready, 6 * c + 3 * s + 2)
                    chain(v.tensor_tensor(z_sb[:, s, :], bank[2 + PROJ_Z][:], sg_z[:, s, :], ALU.mult))
                    v.wait_ge(sig_ready, 6 * c + 3 * s + 3)
                    w1 = chain(v.tensor_tensor(sg_a[:, s, :], bank[2 + PROJ_GA][:], sg_a[:, s, :], ALU.mult))
                    v.wait_ge(v_l0, w1)
                    v.wait_ge(proj_ready, r + PROJ_GB + 1)
                    w2 = chain(v.tensor_tensor(og_sb[:, s, :], bank[2 + PROJ_GB][:], sg_a[:, s, :], ALU.mult))
                    v.wait_ge(v_l0, w2)
                    v.wait_ge(carry_set, b + 1)
                    w3 = chain(v.tensor_tensor_scan(h_sb[:, s, :], f_sb[:, s, :], z_sb[:, s, :],
                                                    carry0[:, s:s + 1], ALU.mult, ALU.add))
                    v.wait_ge(v_l0, w3)
                    chain(v.tensor_copy(carry0[:, s:s + 1], h_sb[:, s, CH - 1:CH]))
                    v.tensor_tensor(gated[:, s, :], og_sb[:, s, :], h_sb[:, s, :],
                                    ALU.mult).then_inc(gated_ready, 1)
                assert k[0] == SB * L0_SB == L0_STEPS
                for h in range(2):
                    v.wait_ge(mix_ready, 2 * c + h + 1)
                    if h == 0:
                        wait_past(v, mix_stored, 16 * c)
                    v.tensor_tensor(mix_st[:, 2 * h:2 * h + 2, :],
                                    bank[7][:].rearrange("p (t d) -> p t d", d=D),
                                    xn_st[:, 2 * h:2 * h + 2, :], ALU.add).then_inc(mix_added, 1)

            for b in range(B):
                wait_past(v, gated_ready, SB * CPB * b)
                v.memset(carry0[:], 0.0).then_inc(carry_set, 1)
                mixer(CPB * b, b)
                with v.Fori(CPB * b + 1, CPB * (b + 1)) as c:
                    mixer(c, b)

            def hidden(j, half):
                v.wait_ge(silu_ready, 2 * j + half + 1)
                v.tensor_tensor(hid[:, half, :], silu_g[:, half, :], bank[2 + 2 * half][:],
                                ALU.mult).then_inc(hid_ready, 1)

            def result(j, u, waits):
                v.wait_ge(down_ready, j + 1)
                if waits is not None:
                    v.wait_ge(ye_stored[u], waits)
                v.tensor_copy(ye[:, u, :], bank[7][:, 0:D]).then_inc(ye_ready, 1)

            hidden(0, 0)
            hidden(0, 1)
            hidden(1, 0)
            hidden(1, 1)
            result(0, 0, None)
            hidden(2, 0)
            hidden(2, 1)
            result(1, 1, None)
            with v.Fori(0, (SLOTS - 3) // 2) as jj:
                for u in range(2):
                    j = 3 + 2 * jj + u
                    hidden(j, 0)
                    hidden(j, 1)
                    result(j - 1, u, 16 * (jj + 1))
            result(SLOTS - 1, (SLOTS - 1) % 2, 16 * ((SLOTS - 1) // 2))
            v.wait_ge(ld_bw, 16)
            then(v.tensor_reduce(bw_a[:], bw_w, AX_X, ALU.add, apply_absolute_value=True))
            then(v.tensor_scalar(bw_a[:], bw_a[:], 1.0 / D, None, ALU.mult))
            then(v.tensor_scalar(bw_t[:], bw_w, 0.0, None, ALU.is_ge))
            then(v.tensor_scalar(bw_t[:], bw_t[:], 2.0, -1.0, ALU.mult, ALU.add))
            for k in range(KB):
                then(v.scalar_tensor_tensor(bw_t[:, k, :], bw_t[:, k, :], bw_a[:, k:k + 1], bw_w[:, k, :],
                                            ALU.mult, ALU.subtract))
            v.tensor_tensor(bw_t[:], bw_t[:], bw_w, ALU.add).then_inc(bw_ready, 1)
            v.wait_ge(bw_ready, 1)
            v.sem_inc(layer0_done, 1)
            v.wait_ge(layer0_done, 5)

            for b in range(B):
                v.memset(carry1[b][:], 0.0).then_inc(scan_set, 1)
                v.memset(xpad[b][:], 0.0).then_inc(scan_set, 1)
            v.wait_ge(scan_set, 4)

            def at(q, step):
                return PRE_STEPS * q + step

            def places(q, b, j):
                wait_past(v, y_in, 64 * q)
                v.tensor_copy(idx4[:], dest_u[:, bass.ds(b * TPB + j * TPC, TPC)]).then_inc(idx_ready, 1)
                v.tensor_copy(xpad[b][:, :, 0:KC - 1], xpad[b][:, :, CH:CH + KC - 1]).then_inc(v_pre, 1)

            def residual(q, b):
                v.wait_ge(x_in, 32 * q + 32)
                v.wait_ge(y_silu, TPC * q + TPC)
                v.tensor_tensor(yg[:], yg[:], mix1[:], ALU.mult).then_inc(v_pre, 1)
                v.wait_ge(v_pre, at(q, 2))
                v.tensor_tensor(x1[b][:], x1[b][:], yg[:], ALU.add).then_inc(v_pre, 1)
                v.wait_ge(v_pre, at(q, 3))
                for i in range(TPC):
                    v.bn_stats(st1[:, i, :], x1[b][:, i, :]).then_inc(v_pre, 1)
                v.wait_ge(v_pre, at(q, 7))
                me, qe, mo, qo = (st1[:, :, k] for k in (1, 2, 4, 5))
                v.tensor_tensor(ln1[:, 0, :], me, mo, ALU.add)
                v.tensor_tensor(ln1[:, 1, :], me, mo, ALU.subtract)
                v.tensor_tensor(ln1[:, 2, :], qe, qo, ALU.add).then_inc(v_pre, 1)
                v.wait_ge(v_pre, at(q, 8))
                v.tensor_scalar(ln1[:, 3, :], ln1[:, 0, :], 0.5, None, ALU.mult)
                v.scalar_tensor_tensor(ln1[:, 1, :], ln1[:, 1, :], 0.25, ln1[:, 1, :], ALU.mult, ALU.mult)
                v.tensor_scalar(ln1[:, 2, :], ln1[:, 2, :], 1.0 / D, EPS, ALU.mult, ALU.add).then_inc(v_pre, 1)
                v.wait_ge(v_pre, at(q, 9))
                v.tensor_tensor(ln1[:, 4, :], ln1[:, 2, :], ln1[:, 1, :], ALU.add).then_inc(var1_ready, 1)

            def normed(q, b):
                v.wait_ge(rstd1_ready, q + 1)
                for i in range(TPC):
                    ins = v.tensor_scalar(yg[:, i, :], x1[b][:, i, :], ln1[:, 3, i:i + 1], ln1[:, 5, i:i + 1],
                                          ALU.subtract, ALU.mult)
                ins.then_inc(xn2_ready, 1)

            def conv(q, b, d):
                v.wait_ge(pre_free, GROUPS * q + G_IN + d + 1)
                if d == 0:
                    wait_past(v, delta_ready, DB * q)
                v.tensor_scalar(soft[:, d, :], xpad[b][:, d, 0:CH], cols1[:, d, 0:1], None,
                                ALU.mult).then_inc(v_pre, 1)
                for k in range(1, KC):
                    v.wait_ge(v_pre, at(q, 9 + (KC - 1) * d + k))
                    v.scalar_tensor_tensor(soft[:, d, :], xpad[b][:, d, k:k + CH], cols1[:, d, k:k + 1],
                                           soft[:, d, :], ALU.mult, ALU.add
                                           ).then_inc(v_pre if k < KC - 1 else conv_ready, 1)

            def prepare(q, b, j, n):
                if n == 1:
                    places(q, b, j)
                if n == 3:
                    residual(q, b)
                if n == 5:
                    normed(q, b)
                if 8 <= n < 8 + DB:
                    conv(q, b, n - 8)

            def finish(q, b):
                v.wait_ge(y_added, DS * q + DS + STATE_BUFS)
                wait_past(v, out_full, 2 * q)
                for d in range(DB):
                    v.scalar_tensor_tensor(y_fin[:, d, :], xc[b][:, d, :], cols1[:, d, KC + 2:KC + 3], bank[d][:],
                                           ALU.mult, ALU.add).then_inc(skip_added, 1)
                for d in range(DB):
                    v.wait_ge(skip_added, DB * q + d + 1)
                    v.tensor_tensor(y_fin[:, d, :], y_fin[:, d, :], z_silu[b][:, d, :],
                                    ALU.mult).then_inc(y_ready, 1)

            def result1(q, b):
                wait_past(v, stored, 16 * q)
                for h in range(2):
                    two = slice(2 * h, 2 * h + 2)
                    v.wait_ge(out_full, 2 * q + h + 1)
                    v.tensor_tensor(o_st[:, two, :], M2, g_silu[b][:, two, :], ALU.mult).then_inc(out_mul, 1)
                    v.wait_ge(out_mul, 2 * q + h + 1)
                    v.tensor_tensor(o_st[:, two, :], o_st[:, two, :], x1[b][:, two, :],
                                    ALU.add).then_inc(out_ready, 1)

            M2 = bank[7][:].rearrange("p (t d) -> p t d", d=D)

            def scan(q, b, ahead, before):
                for n in range(DS):
                    g = DS * q + n
                    if n == 0:
                        v.wait_ge(du_ready, DB * q + DB)
                    v.wait_ge(bc_full, 2 * g + 2)
                    v.tensor_tensor(dbu[n % 2][:], du[b][:],
                                    bank[6][:].unsqueeze(1).broadcast_to([P, DB, CH]), ALU.mult
                                    ).then_inc(dbu_ready, 1)
                    v.wait_ge(dbu_ready, g + 1)
                    h = hst[n % STATE_BUFS]
                    v.wait_ge(y_added, g + 1)
                    for d in range(DB):
                        u = DB * g + d
                        v.wait_ge(dA_ready, u + 1)
                        v.tensor_tensor_scan(h[:, d, :], bank[4 + u_bank(d)][:], dbu[n % 2][:, d, :],
                                             carry1[b][:, n, d:d + 1], ALU.mult, ALU.add).then_inc(scan_done, 1)
                    v.wait_ge(scan_done, DA_BUFS + DB * g + DB)
                    v.tensor_copy(carry1[b][:, n, :], h[:, :, CH - 1]).then_inc(carry_done, 1)
                    if n == 0 and before:
                        finish(q - 1, 1 - b)
                    if n == 1 and before:
                        result1(q - 1, 1 - b)
                    if ahead is not None:
                        prepare(q + 1, 1 - b, ahead, n)

            v.sem_inc(scan_done, DA_BUFS)
            for n in range(DS):
                prepare(0, 0, 0, n)
            scan(0, 0, 0, False)
            scan(1, 1, 1, True)
            with v.Fori(1, CPB - 1) as j:
                for b in range(B):
                    scan(B * j + b, b, j + b, True)
            scan(CHUNKS - 2, 0, CPB - 1, True)
            scan(CHUNKS - 1, 1, None, True)
            finish(CHUNKS - 1, 1)
            result1(CHUNKS - 1, 1)

        @block.tensor
        def _(pe):
            pe.wait_ge(ld_small, 16 * 6)
            def router(c):
                pe.wait_ge(xn_ready, TILES + TPC * c + TPC)
                wait_past(pe, xnT_ready, KB * c)
                for k in range(KB):
                    for i in range(TPC):
                        ins = pe.transpose(bank[k][:, i * P:(i + 1) * P], xn_st[:, i, k * P:(k + 1) * P], ident[:])
                    ins.then_inc(xn_turned, 1)
                pe.wait_ge(xnT_ready, KB * c + KB)
                for i in range(TPC):
                    for k in range(KB):
                        ins = pe.matmul(bank[7][:, bass.ds((c * TPC + i) * NE, NE)], xT[:, k, i * P:(i + 1) * P],
                                        w_r[:, k, :], start=(k == 0), stop=(k == KB - 1))
                ins.then_inc(logits_ready, 1)

            router(0)
            with pe.Fori(1, CHUNKS) as c:
                router(c)
            pe.wait_ge(onehot_ready, 1)
            pe.wait_ge(set_done, 2)
            n = TILES * NE
            oh = rt[:, 4].rearrange("p t e -> p (t e)")
            pe.matmul(bank[6][:, 0:n], tri[:], oh, start=True, stop=True)
            pe.matmul(bank[6][:, n:2 * n], ones[:], oh, start=True, stop=True).then_inc(ranks_ready, 1)

            pe.wait_ge(ld_w0, 32)
            def mixer(c):
                pe.wait_ge(st_ready, c + 1)
                for k in range(KB):
                    for i in range(TPC):
                        ins = pe.transpose(bank[k][:, i * P:(i + 1) * P], xr_st[:, i, k * P:(k + 1) * P], ident[:])
                    ins.then_inc(xr_turned, 1)
                pe.wait_ge(xrT_ready, KB * c + KB)
                for s in range(SB):
                    if s == 0:
                        wait_past(pe, gated_ready, SB * c)
                    for w in range(5):
                        if s > 0 and w == PROJ_F:
                            pe.wait_ge(sig_ready, 6 * c + 1)
                        if s > 0 and w == PROJ_ZG:
                            pe.wait_ge(sig_ready, 6 * c + 2)
                        if s > 0 and w == PROJ_Z:
                            pe.wait_ge(v_l0, L0_STEPS * c + 3)
                        for k in range(KB):
                            ins = pe.matmul(bank[2 + w][:], w0[:, w, k, s * P:(s + 1) * P], xT[:, k, :],
                                            start=(k == 0), stop=(k == KB - 1))
                        ins.then_inc(proj_ready, 1)
                pe.wait_ge(gated_ready, SB * c + SB)
                for h in range(2):
                    wait_past(pe, mix_added, 2 * c + h)
                    for i in range(2):
                        o = bank[7][:, i * D:(i + 1) * D]
                        pe.matmul(o, ones[0:1, :], bias0[:], start=True, stop=False)
                        t = (2 * h + i) * P
                        for s in range(SB):
                            for part in range(3):
                                ins = pe.matmul(o, gated[:, s, t:t + P], wo_b[:, part, s, :], start=False,
                                                stop=(s == SB - 1 and part == 2))
                    ins.then_inc(mix_ready, 1)

            mixer(0)
            with pe.Fori(1, CHUNKS) as c:
                mixer(c)

            pe.wait_ge(ld_moe, 48)
            pe.wait_ge(eid_ready, 1)
            pe.wait_ge(mix_added, 2 * CHUNKS)

            def turn_in(j, u, loads):
                pe.wait_ge(xg_loaded[u], 16 * loads)
                for k in range(KB):
                    ins = pe.transpose(bank[0][:, k * P:(k + 1) * P], xg[:, u, k * P:(k + 1) * P], ident[:])
                ins.then_inc(xg_turned, 1)

            def up(j, e, half):
                if half == 0:
                    pe.wait_ge(xgT_ready, j + 1)
                for n, w in enumerate((w_g, w_u)):
                    for k in range(KB):
                        ins = pe.matmul(bank[1 + 2 * half + n][:], xgT[:, k, :],
                                        w[:, bass.ds(e * (KB * FF) + (k * FF + half * HALF), HALF)],
                                        start=(k == 0), stop=(k == KB - 1))
                ins.then_inc(up_ready, 1)

            def turn_hidden(j, half):
                pe.wait_ge(hid_ready, 2 * j + half + 1)
                for i in range(FB // 2):
                    ins = pe.transpose(bank[5 + half][:, i * P:(i + 1) * P], hid[:, half, i * P:(i + 1) * P],
                                       ident[:])
                ins.then_inc(hid_turned, 1)

            def down(j, e):
                pe.wait_ge(hidT_ready, 2 * j + 2)
                wait_past(pe, ye_ready, j)
                for i in range(FB):
                    ins = pe.matmul(bank[7][:, 0:D], hidT[:, i, :], w_d[:, bass.ds(e * (FB * D) + i * D, D)],
                                    start=(i == 0), stop=(i == FB - 1))
                ins.then_inc(down_ready, 1)

            def expert(j):
                return pe.value_load(eid[0:1, bass.ds(j, 1)], min_val=0, max_val=NE - 1)

            turn_in(0, 0, 1)
            e0 = expert(0)
            up(0, e0, 0)
            up(0, e0, 1)
            turn_hidden(0, 0)
            turn_in(1, 1, 1)
            def pair(jj):
                for u in range(2):
                    j = 1 + 2 * jj + u
                    e = expert(j)
                    up(j, e, 0)
                    turn_hidden(j - 1, 1)
                    up(j, e, 1)
                    down(j - 1, expert(j - 1))
                    turn_hidden(j, 0)
                    turn_in(j + 1, u, jj + 2)

            pair(0)
            with pe.Fori(1, (SLOTS - 1) // 2) as jj:
                pair(jj)
            turn_hidden(SLOTS - 1, 1)
            down(SLOTS - 1, expert(SLOTS - 1))
            pe.wait_ge(bw_ready, 1)
            pe.wait_ge(ye_ready, SLOTS)
            for k in range(KB):
                for o in range(KB):
                    ins = pe.transpose(bank[6 + k][:, o * P:(o + 1) * P], bw_t[:, o, k * P:(k + 1) * P], ident[:])
                ins.then_inc(bw_turned, 1)
            pe.wait_ge(bwT_ready, KB)
            pe.sem_inc(layer0_done, 1)
            pe.wait_ge(layer0_done, 5)

            M = bank[7]

            def group(q, m):
                wait_past(pe, pre_free, GROUPS * q + m)

            def turn_xn2(q):
                pe.wait_ge(xn2_ready, q + 1)
                for k in range(KB):
                    group(q, G_XNT + k)
                    for i in range(TPC):
                        ins = pe.transpose(M[:, i * P:(i + 1) * P], yg[:, i, k * P:(k + 1) * P], ident[:])
                    ins.then_inc(pre_full, 1)

            def gates(q):
                for h in range(2):
                    group(q, G_GATE + h)
                    for i in range(2):
                        o, t = M[:, i * D:(i + 1) * D], (2 * h + i) * P
                        pe.matmul(o, ones[0:1, :], bias1[:, 0, :], start=True, stop=False)
                        for k in range(KB):
                            ins = pe.matmul(o, xn2T[:, k, t:t + P], bwT[:, k, :], start=False, stop=(k == KB - 1))
                    ins.then_inc(pre_full, 1)

            def in_proj(q, first, n):
                for e in range(first, first + n):
                    group(q, G_IN + e)
                    for k in range(KB):
                        ins = pe.matmul(M[:], w_in[:, k, e * P:(e + 1) * P], xn2T[:, k, :],
                                        start=(k == 0), stop=(k == KB - 1))
                    ins.then_inc(pre_full, 1)

            def low_rank(q, b):
                pe.wait_ge(xc_ready, DB * q + DB)
                for m, (lo, n) in ((G_DT, (0, DR)), (G_BC, (DR, 2 * DS))):
                    group(q, m)
                    for d in range(DB):
                        ins = pe.matmul(M[0:n, :], w_x[:, d, lo:lo + n], xc[b][:, d, :], start=(d == 0),
                                        stop=(d == DB - 1))
                    ins.then_inc(pre_full, 1)

            def dt(q):
                for d in range(DB):
                    group(q, G_DELTA + d)
                    pe.matmul(M[:], w_dt[:, d * P:(d + 1) * P], dt_sb[:], start=True, stop=True).then_inc(pre_full, 1)

            def prepare(q, b, n):
                if n == 5:
                    turn_xn2(q)
                if n == 6:
                    gates(q)
                if n == 7:
                    in_proj(q, 0, DB)
                if n == 9:
                    in_proj(q, DB, DB)
                if n == 12:
                    low_rank(q, b)
                if n == 13:
                    dt(q)

            def spread(q, b, n):
                g = DS * q + n
                for k, row in enumerate((DS + n, n)):
                    if k == 0:
                        if n == 0:
                            pe.wait_ge(pre_free, GROUPS * q + G_BC + 1)
                        wait_past(pe, dbu_ready, g)
                    else:
                        pe.wait_ge(c_ready, g + 1)
                    pe.matmul(bank[6][:], ident[0:2 * DS, row:row + 1].broadcast_to([2 * DS, P]), bc_rows[b][:],
                              start=True, stop=True).then_inc(bc_full, 1)

            def add_up(q, n):
                g = DS * q + n
                pe.wait_ge(hc_ready, 2 + g + 1)
                if n == 0:
                    wait_past(pe, skip_added, DB * q)
                for d in range(DB):
                    ins = pe.matmul(bank[d][:], ident[:], hst[n % STATE_BUFS][:, d, :], start=(n == 0),
                                    stop=(n == DS - 1))
                ins.then_inc(y_added, 1)

            def out_proj(q, prepared):
                pe.wait_ge(y_ready, DB * q + DB)
                for h in range(2):
                    if h == 0:
                        pe.wait_ge(pre_free, GROUPS * prepared)
                    wait_past(pe, out_mul, 2 * q + h)
                    for i in range(2):
                        o, t = M[:, i * D:(i + 1) * D], (2 * h + i) * P
                        pe.matmul(o, ones[0:1, :], bias1[:, 1, :], start=True, stop=False)
                        for d in range(DB):
                            ins = pe.matmul(o, y_fin[:, d, t:t + P], w_out[:, d, :], start=False,
                                            stop=(d == DB - 1))
                    ins.then_inc(out_full, 1)

            def scan(q, b, ahead, before):
                for n in range(DS):
                    if n == 0:
                        spread(q, b, 0)
                    if n + 1 < DS:
                        spread(q, b, n + 1)
                    add_up(q, n)
                    if n == 1 and before:
                        out_proj(q - 1, q + 1)
                        pe.wait_ge(out_mul, 2 * q)
                    if ahead:
                        prepare(q + 1, 1 - b, n)

            pe.sem_inc(y_added, STATE_BUFS)
            for n in range(DS):
                prepare(0, 0, n)
            scan(0, 0, True, False)
            scan(1, 1, True, True)
            with pe.Fori(1, CPB - 1) as j:
                for b in range(B):
                    scan(B * j + b, b, True, True)
            scan(CHUNKS - 2, 0, True, True)
            scan(CHUNKS - 1, 1, False, True)
            out_proj(CHUNKS - 1, CHUNKS)


L0_SB = 5
L0_STEPS = SB * L0_SB
PRE_HALO = 1
PRE_STEPS = 9 + DB * (KC - 1)


def u_bank(d):
    return d % DA_BUFS


def kernel(L0_attn_x, L0_attn_rms_w, L0_attn_Wf_w, L0_attn_Wf_b, L0_attn_Wzg_w, L0_attn_Wz_w, L0_attn_Wga_w,
           L0_attn_Wgb_w, L0_attn_Wout_w, L0_attn_Wout_b, L0_ffn_Wr, L0_ffn_br, L0_ffn_Wg, L0_ffn_Wu, L0_ffn_Wd,
           L1_attn_W_in, L1_attn_conv_w, L1_attn_conv_b, L1_attn_W_x, L1_attn_W_dt, L1_attn_b_dt, L1_attn_A_log,
           L1_attn_D, L1_attn_W_out, L1_attn_b_out, L1_ffn_weight, L1_ffn_bias):
    import numpy as np
    import concourse.bacc as bacc
    from concourse.bass_utils import run_bass_kernel_spmd

    def rows(w):
        w = np.asarray(w)
        return np.swapaxes(w.reshape(w.shape[0] // P, P, *w.shape[1:]), 0, 1)

    def spread(r):
        r = np.asarray(r)
        return np.broadcast_to(r, (P, *r.shape))

    wt = [rows(np.asarray(w).T) for w in (L0_attn_Wf_w, L0_attn_Wzg_w, L0_attn_Wz_w, L0_attn_Wga_w, L0_attn_Wgb_w)]
    experts = [np.stack([rows(np.asarray(w)[e]) for e in range(NE)], 1).reshape(P, -1)
               for w in (L0_ffn_Wg, L0_ffn_Wu, L0_ffn_Wd)]
    consts = np.concatenate([np.arange(NE, 0, -1), P * np.arange(TILES), np.arange(SLOTS + 1)]).astype(np.float32)
    arrays = {
        "x": rows(np.asarray(L0_attn_x).reshape(B * T, D)),
        "cols0": np.stack([rows(L0_attn_rms_w), rows(L0_attn_Wf_b)], 2),
        "w_r": rows(L0_ffn_Wr),
        "tri": np.triu(np.ones((P, P), np.float32), 1),
        "small": np.concatenate([spread(L0_ffn_br), spread(consts)], 1),
        "bias0": np.asarray(L0_attn_Wout_b).reshape(1, D),
        "ident": np.eye(P, dtype=np.float32),
        "w0": np.stack(wt, 1),
        "wo": rows(np.asarray(L0_attn_Wout_w).T),
        "w_g": experts[0], "w_u": experts[1], "w_d": experts[2],
        "w_in": rows(np.asarray(L1_attn_W_in).T),
        "w_x": rows(np.asarray(L1_attn_W_x).T),
        "w_dt": np.asarray(L1_attn_W_dt).T,
        "w_out": rows(np.asarray(L1_attn_W_out).T),
        "bias1": np.stack([np.asarray(L1_ffn_bias), np.asarray(L1_attn_b_out)])[None],
        "cols1": np.concatenate([rows(L1_attn_conv_w)] + [rows(c)[:, :, None] for c in
                                (L1_attn_conv_b, L1_attn_b_dt, L1_attn_D)], 2),
        "a_log": rows(L1_attn_A_log),
        "bw_w": rows(L1_ffn_weight),
    }
    nc = bacc.Bacc("TRN2", target_bir_lowering=False, num_devices=1)
    ins, aps = {}, {}
    for name, x in arrays.items():
        x = np.ascontiguousarray(x)
        ins[f"in_{name}"] = x
        aps[name] = nc.dram_tensor(f"in_{name}", x.shape, mybir.dt.from_np(x.dtype), kind="ExternalInput").ap()
    out = nc.dram_tensor("out_0", (P, TILES, D), F32, kind="ExternalOutput").ap()
    build(nc, aps, out)
    r = run_bass_kernel_spmd(nc, [ins], core_ids=[0])
    got = r.results[0]["out_0"]
    return np.ascontiguousarray(np.swapaxes(got, 0, 1)).reshape(B, T, D)
```

```python
from contextlib import ExitStack

import concourse.bass as bass
from concourse import mybir

P = 128
B, T, D = 2, 2048, 256
KB = D // P
TILES = B * T // P
TPC = 4
CH = TPC * P
CPB = T // CH
CHUNKS = B * CPB
TPB = T // P
S0 = 256
SB = S0 // P
NE, FF = 4, 1024
FB = FF // P
HALF = FF // 2
SLOTS = TILES + NE - 1
ROWS = SLOTS + 1
DI, DS, DR, KC = 512, 16, 128, 4
DB = DI // P
XR = DR + 2 * DS
EPS = 1e-5

F32 = mybir.dt.float32
F32R = mybir.dt.float32r
BF16 = mybir.dt.bfloat16
I32 = mybir.dt.int32
U32 = mybir.dt.uint32
ALU = mybir.AluOpType
ACT = mybir.ActivationFunctionType
AX_X = mybir.AxisListType.X

PROJ_F, PROJ_ZG, PROJ_Z, PROJ_GA, PROJ_GB = range(5)
G_XNT, G_X, G_OUT, G_Z01, G_DT, G_BC, G_DELTA, G_Z23, G_GATE, GROUPS = 0, 2, 6, 8, 10, 11, 12, 16, 18, 20
STATE_BUFS = 4
LAG = 2
SPLIT = 32
DA_BUFS = DB


def build(nc, a, out):
    with ExitStack() as ctx:
        def sem(name):
            return ctx.enter_context(nc.semaphore(name))

        def sb(stack, name, shape, dt=F32):
            return stack.enter_context(nc.sbuf_tensor(name, shape, dt))

        sorted_x = nc.dram_tensor("sorted_x", (ROWS * P, D), F32).ap()
        sorted_y = nc.dram_tensor("sorted_y", (SLOTS * P, D), F32).ap()
        c_rows = nc.dram_tensor("c_rows", (CHUNKS, DS, CH), F32).ap()
        mixed = nc.dram_tensor("mixed", (P, TILES, D), F32).ap()

        ident = sb(ctx, "ident", [P, P])
        ones = sb(ctx, "ones", [P, P])
        w_in = sb(ctx, "w_in", [P, KB, 2 * DI])
        w_x = sb(ctx, "w_x", [P, DB, DR + SPLIT + DS])
        pick = sb(ctx, "pick", [2 * SPLIT, DS], F32R)
        w_dt = sb(ctx, "w_dt", [P, DI])
        w_out = sb(ctx, "w_out", [P, DB, D])
        bwT = sb(ctx, "bwT", [P, KB, D])
        bias1 = sb(ctx, "bias1", [1, 2, D])
        cols1 = sb(ctx, "cols1", [P, DB, KC + 3])
        negA = sb(ctx, "negA", [P, DB, DS])
        dest_u = sb(ctx, "dest_u", [P, TILES], U32)
        top_w = sb(ctx, "top_w", [P, TILES])
        idx4 = sb(ctx, "idx4", [P, TPC], U32)
        neg_half = sb(ctx, "neg_half", [P, TILES])

        l0 = ExitStack()
        x_sb = sb(l0, "x_sb", [P, TILES, D])
        w_g = sb(l0, "w_g", [P, NE * KB * FF])
        w_u = sb(l0, "w_u", [P, NE * KB * FF])
        w_d = sb(l0, "w_d", [P, NE * FB * D])
        w0 = sb(l0, "w0", [P, 5, KB, S0])
        wo_f = sb(l0, "wo_f", [P, SB, D])
        wo_b = sb(l0, "wo_b", [P, 3, SB, D], BF16)
        bias0 = sb(l0, "bias0", [1, D])
        cols0 = sb(l0, "cols0", [P, 2, 2])
        w_r = sb(l0, "w_r", [P, KB, NE])
        tri = sb(l0, "tri", [P, P])
        small = sb(l0, "small", [P, 2 * NE + TILES + SLOTS + 1])
        st0 = sb(l0, "st0", [P, TILES, 6])
        mean0 = sb(l0, "mean0", [P, TILES])
        var0 = sb(l0, "var0", [P, TILES])
        tmp0 = sb(l0, "tmp0", [P, 4, TILES])
        rstd0 = sb(l0, "rstd0", [P, TILES])
        rr0 = sb(l0, "rr0", [P, TILES])
        rt = sb(l0, "rt", [P, 8, TILES, NE])
        rs = sb(l0, "rs", [P, 8, TILES])
        eidf = sb(l0, "eidf", [1, SLOTS + 1, NE])
        eid = sb(l0, "eid", [1, SLOTS + 1], I32)
        xn_st = sb(l0, "xn_st", [P, TPC, D])
        xr_st = sb(l0, "xr_st", [P, TPC, D])
        xT = sb(l0, "xT", [P, KB, CH])
        f_sb = sb(l0, "f_sb", [P, SB, CH], BF16)
        z_sb = sb(l0, "z_sb", [P, SB, CH], BF16)
        og_sb = sb(l0, "og_sb", [P, SB, CH], BF16)
        h_sb = sb(l0, "h_sb", [P, SB, CH], BF16)
        gated = sb(l0, "gated", [P, SB, CH], BF16)
        carry0 = sb(l0, "carry0", [P, SB], BF16)
        sg_z = sb(l0, "sg_z", [P, SB, CH])
        sg_a = sb(l0, "sg_a", [P, SB, CH])
        mix_st = rt[:].rearrange("p k t e -> p (k t e)").rearrange("p (t d) -> p t d", d=D)
        xg = sb(l0, "xg", [P, 2, D])
        zeros = sg_a[:].rearrange("p s c -> p (s c)").rearrange("p (t d) -> p t d", d=D)
        normed_st, normedT = [xn_st, xr_st], [xT, sg_z]
        wo_r = xr_st[:, 0:SB, :]
        xgT = f_sb[:].bitcast(F32).rearrange("p s c -> p (s c)")[:, 0:KB * P].rearrange("p (k t) -> p k t", k=KB)
        silu_g, hid = sg_z, sg_a
        hidT = xT[:].rearrange("p k c -> p (k c)").rearrange("p (f t) -> p f t", t=P)
        ye = h_sb[:].bitcast(F32)
        bw_w, bw_t = gated[:].bitcast(F32), wo_f
        bw_a = sb(l0, "bw_a", [P, KB])
        pick_f = sb(l0, "pick_f", [2 * SPLIT, DS])
        l0.close()

        l1 = ExitStack()
        xpad = sb(l1, "xpad", [P, DB, KC - 1 + CH])
        halo = [sb(l1, f"halo{b}", [P, DB, KC - 1]) for b in range(B)]
        z_silu = sb(l1, "z_silu", [P, DB, CH])
        xc = [sb(l1, f"xc{b}", [P, DB, CH]) for b in range(B)]
        delta = [sb(l1, f"delta{b}", [P, DB, CH]) for b in range(B)]
        du = [sb(l1, f"du{b}", [P, DB, CH]) for b in range(B)]
        bc_rows = sb(l1, "bc_rows", [2 * DS, CH])
        b_split = [sb(l1, f"b_split{b}", [2 * SPLIT, CH], F32R) for b in range(B)]
        g_silu = sb(l1, "g_silu", [P, TPC, D])
        x1 = [sb(l1, f"x1_{b}", [P, TPC, D]) for b in range(B)]
        carry1 = [sb(l1, f"carry1_{b}", [P, DS, DB]) for b in range(B)]
        dbu = [sb(l1, f"dbu{i}", [P, DB, CH]) for i in range(2)]
        hst = [sb(l1, f"hst{i}", [P, DB, CH]) for i in range(STATE_BUFS)]
        c_bc = sb(l1, "c_bc", [P, STATE_BUFS, CH])
        soft = sb(l1, "soft", [P, DB, CH])
        y_fin = sb(l1, "y_fin", [P, DB, CH])
        yg = sb(l1, "yg", [P, TPC, D])
        dA = sb(l1, "dA", [P, DA_BUFS, CH])
        x_ld = soft[:, 0:2, :].rearrange("p a c -> p (a c)").rearrange("p (t d) -> p t d", d=D)
        mix1 = soft[:, 2:4, :].rearrange("p a c -> p (a c)").rearrange("p (t d) -> p t d", d=D)
        xn2T = [sb(l1, f"xn2T{b}", [P, KB, CH]) for b in range(B)]
        dt_sb = sb(l1, "dt_sb", [P, CH])
        o_st = sb(l1, "o_st", [P, TPC, D])
        st1 = sb(l1, "st1", [P, TPC, 6])
        ln1 = sb(l1, "ln1", [P, 8, TPC])
        l1.close()

        bank = [ctx.enter_context(nc.psum_tensor(f"bank{i}", [P, 512], F32)) for i in range(8)]

        ld_x = [sem(f"ld_x{i}") for i in range(2)]
        ld_small = sem("ld_small")
        ld_w0 = sem("ld_w0")
        ld_moe = sem("ld_moe")
        ld_w1 = sem("ld_w1")
        ld_bw = sem("ld_bw")
        zero_set = sem("zero_set")
        pool_passed = sem("pool_passed")
        sp_passed = sem("sp_passed")
        zero_filled = sem("zero_filled")
        v0 = sem("v0")
        set_done = sem("set_done")
        stats_ready = sem("stats_ready")
        rstd_ready = sem("rstd_ready")
        xn_ready = sem("xn_ready")
        xn_turned = sem("xn_turned")
        xnT_ready = sem("xnT_ready")
        logits_ready = sem("logits_ready")
        shifted = sem("shifted")
        exp_ready = sem("exp_ready")
        onehot_ready = sem("onehot_ready")
        ranks_ready = sem("ranks_ready")
        st_ready = sem("st_ready")
        xr_ready = sem("xr_ready")
        xr_turned = sem("xr_turned")
        xrT_ready = sem("xrT_ready")
        proj_ready = sem("proj_ready")
        sig_ready = sem("sig_ready")
        carry_set = sem("carry_set")
        v_l0 = sem("v_l0")
        gated_ready = sem("gated_ready")
        mix_ready = sem("mix_ready")
        mix_added = sem("mix_added")
        mix_stored = sem("mix_stored")
        scattered = sem("scattered")
        eid_ready = sem("eid_ready")
        xg_loaded = [sem(f"xg_loaded{i}") for i in range(2)]
        xg_turned = sem("xg_turned")
        xgT_ready = sem("xgT_ready")
        up_ready = sem("up_ready")
        silu_ready = sem("silu_ready")
        hid_ready = sem("hid_ready")
        hid_turned = sem("hid_turned")
        hidT_ready = sem("hidT_ready")
        down_ready = sem("down_ready")
        ye_ready = sem("ye_ready")
        ye_stored = [sem(f"ye_stored{i}") for i in range(2)]
        bw_ready = sem("bw_ready")
        bw_turned = sem("bw_turned")
        bwT_ready = sem("bwT_ready")
        layer0_done = sem("layer0_done")
        x_in = sem("x_in")
        idx_ready = sem("idx_ready")
        y_in = sem("y_in")
        y_silu = sem("y_silu")
        v_pre = sem("v_pre")
        var1_ready = sem("var1_ready")
        rstd1_ready = sem("rstd1_ready")
        xn2_ready = sem("xn2_ready")
        m_full = sem("m_full")
        m_free = sem("m_free")
        x1_kept = sem("x1_kept")
        tap_ready = sem("tap_ready")
        conv_ready = sem("conv_ready")
        xc_ready = sem("xc_ready")
        soft_ready = sem("soft_ready")
        a_pre = sem("a_pre")
        delta_ready = sem("delta_ready")
        du_ready = sem("du_ready")
        scan_set = sem("scan_set")
        b_spread = sem("b_spread")
        b_high = sem("b_high")
        pick_ready = sem("pick_ready")
        c_stored = sem("c_stored")
        c_loaded = [sem(f"c_loaded{i}") for i in range(2)]
        dA_ready = sem("dA_ready")
        dbu_ready = sem("dbu_ready")
        scan_done = sem("scan_done")
        carry_done = sem("carry_done")
        hc_ready = sem("hc_ready")
        y_added = sem("y_added")
        gates_ready = sem("gates_ready")
        skip_added = sem("skip_added")
        y_ready = sem("y_ready")
        out_mul = sem("out_mul")
        out_ready = sem("out_ready")
        stored = sem("stored")

        def shared(g):
            return bank[6 + g % 2]

        def group(turn, g):
            return GROUPS * (turn + 1) + g

        block = ctx.enter_context(nc.Block())

        def wait_past(eng, semaphore, value):
            if not isinstance(value, int) or value > 0:
                eng.wait_ge(semaphore, value)

        @block.sync
        def _(sp):
            half = TILES // 2
            for i in range(2):
                for q in range(4):
                    lo = i * half + q * half // 4
                    sp.dma_start(x_sb[:, lo:lo + half // 4, :], a["x"][:, lo:lo + half // 4, :]).then_inc(ld_x[i], 16)
            for t, name in ((cols0, "cols0"), (w_r, "w_r"), (tri, "tri"), (small, "small"), (bias0, "bias0"),
                            (ident, "ident")):
                sp.dma_start(t[:], a[name]).then_inc(ld_small, 16)
            sp.dma_start(w0[:], a["w0"]).then_inc(ld_w0, 16)
            sp.dma_start(wo_f[:], a["wo"]).then_inc(ld_w0, 16)
            sp.wait_ge(zero_set, 1)
            for s in range(0, ROWS, TPC):
                sp.dma_start(sorted_x[s * P:(s + TPC) * P, :].rearrange("(n p) d -> p n d", p=P),
                             zeros).then_inc(zero_filled, 16)
            for t, name in ((w_g, "w_g"), (w_u, "w_u"), (w_d, "w_d")):
                sp.dma_start(t[:], a[name]).then_inc(ld_moe, 16)
            for t, name in ((w_in, "w_in"), (w_x, "w_x"), (w_dt, "w_dt"), (w_out, "w_out"), (bias1, "bias1"),
                            (cols1, "cols1"), (negA, "a_log"), (pick_f, "pick")):
                sp.dma_start(t[:], a[name]).then_inc(ld_w1, 16)

            with sp.Fori(0, CHUNKS) as c:
                sp.wait_ge(mix_added, 2 * c + 2)
                sp.dma_start(mixed[:, bass.ds(c * TPC, TPC), :], mix_st).then_inc(mix_stored, 16)

            sp.dma_start(bw_w, a["bw_w"]).then_inc(ld_bw, 16)
            sp.wait_ge(scattered, 16 * TILES)

            def load(j, u):
                sp.dma_start(xg[:, u, :], sorted_x[bass.ds(j * P, P), :]).then_inc(xg_loaded[u], 16)

            def store(j, u):
                sp.wait_ge(ye_ready, j + 1)
                sp.dma_start(sorted_y[bass.ds(j * P, P), :], ye[:, u, :]).then_inc(ye_stored[u], 16)

            load(0, 0)
            load(1, 1)
            with sp.Fori(0, (SLOTS - 1) // 2) as jj:
                for u in range(2):
                    j = 2 * jj + u
                    sp.wait_ge(xg_turned, j + 1)
                    load(j + 2, u)
                    store(j, u)
            store(SLOTS - 1, 0)
            sp.wait_ge(mix_stored, 16 * CHUNKS)
            sp.wait_ge(ye_stored[0], 16 * ((SLOTS + 1) // 2))
            sp.wait_ge(ye_stored[1], 16 * (SLOTS // 2))
            sp.sem_inc(layer0_done, 1)
            sp.wait_ge(layer0_done, 5)

            def load_chunk(q, b, j):
                wait_past(sp, delta_ready, DB * q)
                sp.sem_inc(sp_passed, 1)
                sp.dma_start(x_ld, a["x"][:, bass.ds(b * TPB + j * TPC, TPC), :]).then_inc(x_in, 16)
                sp.dma_start(mix1, mixed[:, bass.ds(b * TPB + j * TPC, TPC), :]).then_inc(x_in, 16)

            def store_chunk(q, b, j):
                sp.wait_ge(out_ready, 2 * q + 2)
                sp.sem_inc(sp_passed, 1)
                sp.dma_start(out[:, bass.ds(b * TPB + j * TPC, TPC), :], o_st[:]).then_inc(stored, 16)

            def store_c(q):
                sp.wait_ge(m_free, group(q - 1, G_BC) + 1)
                sp.sem_inc(sp_passed, 1)
                sp.dma_start(c_rows[bass.ds(q, 1), :, :], bc_rows[DS:2 * DS, :]).then_inc(c_stored, 16)

            def load_c(q, m):
                if m == 0:
                    sp.wait_ge(c_stored, 16 * q + 16)
                    sp.sem_inc(sp_passed, 1)
                if m < 2:
                    wait_past(sp, hc_ready, DS * q + 2 * m - 2 if not isinstance(q, int) or q > 0 else 0)
                else:
                    sp.wait_ge(hc_ready, DS * q + 2 * m - 2)
                sp.sem_inc(sp_passed, 1)
                slot = 2 * m % STATE_BUFS
                src = c_rows[bass.ds(q, 1), 2 * m:2 * m + 2, :].broadcast_to([P, 2, CH])
                sp.dma_start(c_bc[:, slot:slot + 2, :], src).then_inc(c_loaded[m % 2], 16)

            def scan(q, b, j, ahead, before):
                for m in range(DS // 2):
                    load_c(q, m)
                    if m == 0 and ahead is not None:
                        load_chunk(q + 1, 1 - b, ahead)
                    if m == 5 and before:
                        store_chunk(q - 1, 1 - b, before[0])
                    if m == 6 and ahead is not None:
                        store_c(q + 1)

            load_chunk(0, 0, 0)
            store_c(0)
            scan(0, 0, 0, 0, None)
            scan(1, 1, 0, 1, (0,))
            with sp.Fori(1, CPB - 1) as j:
                for b in range(B):
                    scan(B * j + b, b, j, j + b, (j - 1 + b,))
            scan(CHUNKS - 2, 0, CPB - 1, CPB - 1, (CPB - 2,))
            scan(CHUNKS - 1, 1, CPB - 1, None, (CPB - 1,))
            store_chunk(CHUNKS - 1, 1, CPB - 1)
            sp.wait_ge(stored, 16 * CHUNKS)

        @block.gpsimd
        def _(pool):
            pool.memset(zeros, 0.0).then_inc(zero_set, 1)
            pool.memset(neg_half[:], -0.5).then_inc(set_done, 1)
            pool.memset(ones[:], 1.0).then_inc(set_done, 1)
            pool.wait_ge(set_done, 2)
            for k, dst in enumerate((rstd0, rr0)):
                pool.wait_ge(stats_ready, k + 1)
                pool.tensor_tensor(dst[:], tmp0[:, k, :], neg_half[:], ALU.pow).then_inc(rstd_ready, 1)
            pool.wait_ge(zero_filled, 16 * (ROWS // TPC))
            with pool.Fori(0, CHUNKS) as c:
                pool.wait_ge(st_ready, c + 1)
                pool.sem_inc(pool_passed, 1)
                for i in range(TPC):
                    pool.indirect_dma_start(
                        sorted_x[:], bass.IndirectOffsetOnAxis(idx4[:, i:i + 1], 0), xn_st[:, i, :], None,
                    ).then_inc(scattered, 16)
            pool.wait_ge(scattered, 16 * TILES)
            pool.sem_inc(layer0_done, 1)
            pool.wait_ge(layer0_done, 5)

            def fetch_experts(q):
                pool.wait_ge(idx_ready, q + 1)
                wait_past(pool, x1_kept, q)
                pool.sem_inc(pool_passed, 1)
                for i in range(TPC):
                    pool.indirect_dma_start(
                        yg[:, i, :], None, sorted_y[:], bass.IndirectOffsetOnAxis(idx4[:, i:i + 1], 0),
                    ).then_inc(y_in, 16)

            def rstd(q):
                pool.wait_ge(var1_ready, q + 1)
                pool.tensor_tensor(ln1[:, 5, :], ln1[:, 4, :], neg_half[:, 0:TPC], ALU.pow).then_inc(rstd1_ready, 1)

            def make_delta(q, b, d):
                pool.wait_ge(soft_ready, 2 * q + 2)
                pool.tensor_tensor(delta[b][:, d, :], delta[b][:, d, :], soft[:, d, :],
                                   ALU.add).then_inc(delta_ready, 1)

            def make_du(q, b, d):
                pool.wait_ge(delta_ready, DB * q + d + 1)
                pool.tensor_tensor(du[b][:, d, :], delta[b][:, d, :], xc[b][:, d, :],
                                   ALU.mult).then_inc(du_ready, 1)

            def prepare(q, b, n):
                if n == 0:
                    rstd(q)
                if n == 11:
                    make_delta(q, b, 0)
                    make_delta(q, b, 1)
                    make_du(q, b, 0)
                if n == 12:
                    make_delta(q, b, 2)
                    make_du(q, b, 1)
                    make_delta(q, b, 3)
                if n == 13:
                    make_du(q, b, 2)
                    make_du(q, b, 3)

            def scan(q, b, ahead, fetch):
                for n in range(DS):
                    g = DS * q + n
                    pool.wait_ge(carry_done, g + 1)
                    pool.wait_ge(c_loaded[n // 2 % 2], 64 * q + 16 * (n // 4 + 1))
                    h = hst[n % STATE_BUFS]
                    c = c_bc[:, n % STATE_BUFS, :].unsqueeze(1).broadcast_to([P, DB, CH])
                    pool.tensor_tensor(h[:], h[:], c, ALU.mult).then_inc(hc_ready, 1)
                    if ahead:
                        prepare(q + 1, 1 - b, n)
                    if n == 14 and fetch:
                        fetch_experts(q + 2)

            fetch_experts(0)
            for n in range(DS):
                prepare(0, 0, n)
            fetch_experts(1)
            with pool.Fori(0, CPB - 1) as j:
                for b in range(B):
                    scan(B * j + b, b, True, True)
            scan(CHUNKS - 2, 0, True, False)
            scan(CHUNKS - 1, 1, False, False)

        @block.scalar
        def _(act):
            act.wait_ge(ld_small, 16 * 6)
            def turn_normed(c, u):
                wait_past(act, logits_ready, c - 1)
                for k in range(KB):
                    act.wait_ge(xn_turned, KB * c + k + 1)
                    act.copy(normedT[u][:, k, :], bank[2 * u + k][:]).then_inc(xnT_ready, 1)

            turn_normed(0, 0)
            turn_normed(1, 1)
            with act.Fori(1, CHUNKS // 2) as pair:
                for u in range(2):
                    turn_normed(2 * pair + u, u)
            act.wait_ge(shifted, 1)
            act.activation(rt[:, 2], rt[:, 1], ACT.Exp).then_inc(exp_ready, 1)

            def turn_inputs(c):
                for k in range(KB):
                    act.wait_ge(xr_turned, KB * c + k + 1)
                    wait_past(act, proj_ready, 10 * c)
                    act.activation(xT[:, k, :], bank[k][:], ACT.Copy, scale=cols0[:, k, 0:1]).then_inc(xrT_ready, 1)

            def mixer(c, ahead):
                for s in range(SB):
                    r = 10 * c + 5 * s
                    act.wait_ge(proj_ready, r + PROJ_F + 1)
                    wait_past(act, gated_ready, SB * c)
                    act.activation(f_sb[:, s, :], bank[2 + PROJ_F][:], ACT.Sigmoid,
                                   bias=cols0[:, s, 1:2]).then_inc(sig_ready, 1)
                    act.wait_ge(proj_ready, r + PROJ_ZG + 1)
                    act.activation(sg_z[:, s, :], bank[2 + PROJ_ZG][:], ACT.Sigmoid).then_inc(sig_ready, 1)
                    act.wait_ge(proj_ready, r + PROJ_GA + 1)
                    act.activation(sg_a[:, s, :], bank[2 + PROJ_GA][:], ACT.Sigmoid).then_inc(sig_ready, 1)
                if ahead:
                    turn_inputs(c + 1)

            act.wait_ge(zero_filled, 16 * (ROWS // TPC))
            turn_inputs(0)
            mixer(0, True)
            with act.Fori(1, CHUNKS - 1) as c:
                mixer(c, True)
            mixer(CHUNKS - 1, False)

            def turn_in(j):
                act.wait_ge(xg_turned, j + 1)
                act.copy(xgT, bank[0][:, 0:D]).then_inc(xgT_ready, 1)

            def gate(j, half):
                act.wait_ge(up_ready, 2 * j + half + 1)
                act.activation(silu_g[:, half, :], bank[1 + 2 * half][:], ACT.Silu).then_inc(silu_ready, 1)

            def turn_hidden(j, half):
                act.wait_ge(hid_turned, 2 * j + half + 1)
                act.copy(hidT[:, half * FB // 2:(half + 1) * FB // 2, :], bank[5 + half][:]).then_inc(hidT_ready, 1)

            turn_in(0)
            gate(0, 0)
            gate(0, 1)
            turn_in(1)
            turn_hidden(0, 0)
            with act.Fori(0, SLOTS - 1) as jj:
                j = jj + 1
                gate(j, 0)
                turn_hidden(j - 1, 1)
                gate(j, 1)
                turn_in(j + 1)
                turn_hidden(j, 0)
            turn_hidden(SLOTS - 1, 1)
            act.wait_ge(ld_w1, 16 * 8)
            act.activation(negA[:], negA[:], ACT.Exp).then_inc(a_pre, 1)
            act.wait_ge(a_pre, 1)
            act.mul(negA[:], negA[:], -1.0).then_inc(a_pre, 1)
            for k in range(KB):
                act.wait_ge(bw_turned, k + 1)
                act.copy(bwT[:, k, :], bank[6 + k][:, 0:D]).then_inc(bwT_ready, 1)
            act.wait_ge(a_pre, 2)
            act.wait_ge(bwT_ready, KB)
            act.sem_inc(layer0_done, 1)
            act.wait_ge(layer0_done, 5)


            def take(turn, g):
                act.wait_ge(m_full, group(turn, g) + 1)
                return shared(g)

            def silus(q, b, j, prepares, gates):
                if prepares:
                    act.wait_ge(y_in, 64 * (q + 1) + 64)
                    for i in range(TPC):
                        act.activation(yg[:, i, :], yg[:, i, :], ACT.Silu,
                                       scale=top_w[:, bass.ds((1 - b) * TPB + j * TPC + i, 1)]).then_inc(y_silu, 1)
                if gates:
                    act.wait_ge(m_free, group(q - 1, G_GATE) + 2)
                    act.activation(z_silu[:], z_silu[:], ACT.Silu).then_inc(gates_ready, 1)
                    act.activation(g_silu[:], g_silu[:], ACT.Silu).then_inc(gates_ready, 1)

            def turn_xn2(t, b, k):
                M = take(t, G_XNT + k)
                act.copy(xn2T[b][:, k, :], M[:]).then_inc(m_free, 1)

            def x_half(t, d):
                M = take(t, G_X + d)
                act.wait_ge(v_pre, PRE_STEPS * (t + 1) + PRE_HALO)
                act.copy(xpad[:, d, KC - 1:], M[:]).then_inc(m_free, 1)
                act.wait_ge(m_free, group(t, G_X + d) + 1)
                act.activation(soft[:, d, :], xpad[:, d, 0:CH], ACT.Copy, scale=cols1[:, d, 0:1]).then_inc(tap_ready, 1)

            def raw_out(t, h):
                M = take(t, G_OUT + h)
                if h == 0:
                    wait_past(act, stored, 16 * (t - 1))
                act.copy(o_st[:, 2 * h:2 * h + 2, :], M[:]).then_inc(m_free, 1)

            def z_half(t, d):
                M = take(t, (G_Z01 if d < 2 else G_Z23 - 2) + d)
                if d == 0:
                    wait_past(act, y_ready, DB * t)
                act.copy(z_silu[:, d, :], M[:]).then_inc(m_free, 1)

            def gate_half(t, h):
                M = take(t, G_GATE + h)
                if h == 0:
                    wait_past(act, out_mul, 2 * t)
                act.copy(g_silu[:, 2 * h:2 * h + 2, :], M[:]).then_inc(m_free, 1)

            def silu_conv(q, b):
                for d in range(DB):
                    act.wait_ge(conv_ready, DB * q + d + 1)
                    act.activation(xc[b][:, d, :], soft[:, d, :], ACT.Silu,
                                   bias=cols1[:, d, KC:KC + 1]).then_inc(xc_ready, 1)

            def dt_rows(t):
                M = take(t, G_DT)
                act.copy(dt_sb[:], M[:]).then_inc(m_free, 1)

            def bc(t, b):
                M = take(t, G_BC)
                act.copy(bc_rows[:], M[0:2 * DS, :])
                act.copy(b_split[b][0:DS, :], M[0:DS, :])
                act.copy(b_split[b][SPLIT:SPLIT + DS, :], M[SPLIT:SPLIT + DS, :]).then_inc(b_high, 1)

            def softplus(t, b, d):
                if d == 0:
                    act.wait_ge(m_free, group(t, G_BC) + 1)
                M = take(t, G_DELTA + d)
                act.activation(soft[:, d, :], M[:], ACT.Abs, bias=cols1[:, d, KC + 1:KC + 2]).then_inc(a_pre, 1)
                act.activation(delta[b][:, d, :], M[:], ACT.Relu,
                               bias=cols1[:, d, KC + 1:KC + 2]).then_inc(m_free, 1)

            def log_part(q):
                act.wait_ge(a_pre, 2 + DB * (q + 1))
                act.activation(soft[:], soft[:], ACT.Exp, scale=-1.0).then_inc(soft_ready, 1)
                act.wait_ge(soft_ready, 2 * q + 1)
                act.activation(soft[:], soft[:], ACT.Ln, bias=ones[:, 0:1]).then_inc(soft_ready, 1)

            def slot(t, b, k, prepares, gates, before):
                if prepares:
                    if k in (6, 7):
                        turn_xn2(t, 1 - b, k - 6)
                    if 8 <= k < 8 + DB:
                        x_half(t, k - 8)
                    if k == 14:
                        silu_conv(t + 1, 1 - b)
                    if k == 16:
                        dt_rows(t)
                    if k == 17:
                        bc(t, 1 - b)
                    if 19 <= k < 19 + DB:
                        softplus(t, 1 - b, k - 19)
                    if k == 23:
                        log_part(t + 1)
                if before and k in (12, 13):
                    raw_out(t, k - 12)
                if gates:
                    if k in (14, 15):
                        z_half(t, k - 14)
                    if k in (23, 24):
                        z_half(t, k - 21)
                    if k in (25, 26):
                        gate_half(t, k - 25)

            def scan(q, b, j, before):
                ahead = j is not None
                for n in range(DS):
                    g = DS * q + n
                    for d in range(DB):
                        u = DB * g + d
                        if n == 0:
                            act.wait_ge(delta_ready, DB * q + d + 1)
                        act.wait_ge(scan_done, u + 1)
                        act.activation(dA[:, d, :], delta[b][:, d, :], ACT.Exp,
                                       scale=negA[:, d, n:n + 1]).then_inc(dA_ready, 1)
                        if d == 1:
                            slot(q, b, 2 * n, ahead, True, before)
                    slot(q, b, 2 * n + 1, ahead, True, before)
                    if n == 0:
                        silus(q, b, j, ahead, before)

            silus(-1, 1, 0, True, False)
            for k in range(2 * DS):
                slot(-1, 1, k, True, False, False)
            scan(0, 0, 0, False)
            scan(1, 1, 1, True)
            with act.Fori(1, CPB - 1) as j:
                for b in range(B):
                    scan(B * j + b, b, j + b, True)
            scan(CHUNKS - 2, 0, CPB - 1, True)
            scan(CHUNKS - 1, 1, None, True)
            silus(CHUNKS, 0, None, False, True)
            for h in range(2):
                raw_out(CHUNKS, h)

        @block.vector
        def _(v):
            steps = [0]

            def then(ins):
                steps[0] += 1
                ins.then_inc(v0, 1)
                v.wait_ge(v0, steps[0])

            for i in range(2):
                v.wait_ge(ld_x[i], 64)
                with v.Fori(0, TILES // 2) as t:
                    v.bn_stats(st0[:, bass.ds(t + i * TILES // 2, 1), :], x_sb[:, bass.ds(t + i * TILES // 2, 1), :]).then_inc(xn_ready, 1)
            v.wait_ge(xn_ready, TILES)
            me, qe, mo, qo = (st0[:, :, k] for k in (1, 2, 4, 5))
            then(v.tensor_tensor(mean0[:], me, mo, ALU.add))
            then(v.tensor_scalar(mean0[:], mean0[:], 0.5, None, ALU.mult))
            then(v.tensor_tensor(tmp0[:, 2, :], me, mo, ALU.subtract))
            then(v.scalar_tensor_tensor(tmp0[:, 2, :], tmp0[:, 2, :], 0.25, tmp0[:, 2, :], ALU.mult, ALU.mult))
            then(v.tensor_tensor(tmp0[:, 3, :], qe, qo, ALU.add))
            then(v.scalar_tensor_tensor(var0[:], tmp0[:, 3, :], 1.0 / D, tmp0[:, 2, :], ALU.mult, ALU.add))
            v.tensor_scalar(tmp0[:, 0, :], var0[:], EPS, None, ALU.add).then_inc(stats_ready, 1)
            v.wait_ge(rstd_ready, 1)
            then(v.tensor_tensor(tmp0[:, 2, :], rstd0[:], rstd0[:], ALU.mult))
            then(v.tensor_tensor(tmp0[:, 2, :], tmp0[:, 2, :], var0[:], ALU.mult))
            v.tensor_scalar(tmp0[:, 1, :], tmp0[:, 2, :], EPS, None, ALU.add).then_inc(stats_ready, 1)
            v.wait_ge(rstd_ready, 2)
            then(v.tensor_tensor(rr0[:], rr0[:], rstd0[:], ALU.mult))

            def normed_tiles(c, u):
                wait_past(v, xn_turned, KB * (c - 1))
                for i in range(TPC):
                    t = c * TPC + i
                    v.tensor_scalar(normed_st[u][:, i, :], x_sb[:, bass.ds(t, 1), :], mean0[:, bass.ds(t, 1)],
                                    rstd0[:, bass.ds(t, 1)], ALU.subtract, ALU.mult).then_inc(xn_ready, 1)

            normed_tiles(0, 0)
            normed_tiles(1, 1)
            with v.Fori(1, CHUNKS // 2) as pair:
                for u in range(2):
                    normed_tiles(2 * pair + u, u)

            def per_tile(x):
                return x.unsqueeze(2).broadcast_to([P, TILES, NE])

            def per_expert(x):
                return x.unsqueeze(1).broadcast_to([P, TILES, NE])

            br, prio = small[:, 0:NE], small[:, NE:2 * NE]
            steps128 = small[:, 2 * NE:2 * NE + TILES]
            slot_no = small[0:1, 2 * NE + TILES:]
            logits, shift, ex, eq, oh, tot, cum = (rt[:, k] for k in range(7))
            v.wait_ge(logits_ready, CHUNKS)
            then(v.tensor_tensor(logits, bank[7][:, 0:TILES * NE].rearrange("p (t e) -> p t e", e=NE),
                                 per_expert(br), ALU.add))
            then(v.tensor_reduce(rs[:, 0, :], logits, AX_X, ALU.max))
            v.tensor_tensor(shift, logits, per_tile(rs[:, 0, :]), ALU.subtract).then_inc(shifted, 1)
            then(v.tensor_tensor(eq, logits, per_tile(rs[:, 0, :]), ALU.is_equal))
            then(v.tensor_tensor(eq, eq, per_expert(prio), ALU.mult))
            then(v.tensor_reduce(rs[:, 1, :], eq, AX_X, ALU.max))
            v.tensor_tensor(oh, eq, per_tile(rs[:, 1, :]), ALU.is_equal).then_inc(onehot_ready, 1)
            v.wait_ge(exp_ready, 1)
            then(v.tensor_reduce(rs[:, 2, :], ex, AX_X, ALU.add))
            then(v.reciprocal(top_w[:], rs[:, 2, :]))
            v.wait_ge(ranks_ready, 1)
            rank_ps = bank[6][:, 0:TILES * NE].rearrange("p (t e) -> p t e", e=NE)
            then(v.tensor_copy(tot, bank[6][:, TILES * NE:2 * TILES * NE]))
            then(v.memset(rs[:, 3, :], 1.0))
            for e in range(NE):
                then(v.tensor_tensor_scan(cum[:, :, e], rs[:, 3, :], tot[:, :, e], 0.0, ALU.mult, ALU.add))
            cnt = cum[:, TILES - 1, :]
            cmp = rt[:, 7].rearrange("p t e -> p (t e)").rearrange("p (e t) -> p e t", e=NE)
            then(v.tensor_tensor(cmp, cnt.unsqueeze(2).broadcast_to([P, NE, TILES]),
                                 steps128.unsqueeze(1).broadcast_to([P, NE, TILES]), ALU.is_gt))
            nt, end, start = rs[:, 4, 0:NE], rs[:, 5, 0:NE], rs[:, 6, 0:NE]
            then(v.tensor_reduce(nt, cmp, AX_X, ALU.add))
            then(v.tensor_tensor_scan(end, rs[:, 3, 0:NE], nt, 0.0, ALU.mult, ALU.add))
            then(v.tensor_tensor(start, end, nt, ALU.subtract))
            then(v.tensor_tensor(cum, cum, tot, ALU.subtract))
            then(v.tensor_tensor(cum, cum, rank_ps, ALU.add))
            then(v.scalar_tensor_tensor(cum, per_expert(start), float(P), cum, ALU.mult, ALU.add))
            then(v.tensor_tensor(cum, cum, oh, ALU.mult))
            then(v.tensor_reduce(rs[:, 7, :], cum, AX_X, ALU.add))
            then(v.tensor_copy(dest_u[:], rs[:, 7, :]))
            n_slot = SLOTS + 1
            ef = eidf[:, :, 0:NE - 1]
            then(v.tensor_tensor(ef, slot_no.unsqueeze(2).broadcast_to([1, n_slot, NE - 1]),
                                 start[0:1, 1:NE].unsqueeze(1).broadcast_to([1, n_slot, NE - 1]), ALU.is_ge))
            then(v.tensor_reduce(eidf[:, :, NE - 1], ef, AX_X, ALU.add))
            v.tensor_copy(eid[:], eidf[:, :, NE - 1]).then_inc(eid_ready, 1)

            v.wait_ge(ld_w0, 32)
            then(v.tensor_copy(wo_b[:, 0], wo_f[:]))
            then(v.tensor_tensor(wo_r, wo_f[:], wo_b[:, 0], ALU.subtract))
            then(v.tensor_copy(wo_b[:, 1], wo_r))
            then(v.tensor_tensor(wo_r, wo_r, wo_b[:, 1], ALU.subtract))
            then(v.tensor_copy(wo_b[:, 2], wo_r))

            def scaled_tiles(c):
                wait_past(v, xr_turned, KB * c)
                for i in range(TPC):
                    t = c * TPC + i
                    ins = v.tensor_scalar(xr_st[:, i, :], x_sb[:, bass.ds(t, 1), :], mean0[:, bass.ds(t, 1)],
                                          rr0[:, bass.ds(t, 1)], ALU.subtract, ALU.mult)
                ins.then_inc(xr_ready, 1)

            def mixer(c, b, ahead):
                k = [0]

                def chain(ins):
                    k[0] += 1
                    ins.then_inc(v_l0, 1)
                    return c * L0_STEPS + k[0]

                wait_past(v, scattered, 64 * c)
                wait_past(v, mix_added, 2 * c)
                for i in range(TPC):
                    t = c * TPC + i
                    v.tensor_scalar(xn_st[:, i, :], x_sb[:, bass.ds(t, 1), :], mean0[:, bass.ds(t, 1)],
                                    rstd0[:, bass.ds(t, 1)], ALU.subtract, ALU.mult)
                v.tensor_copy(idx4[:], dest_u[:, bass.ds(c * TPC, TPC)]).then_inc(st_ready, 1)
                for s in range(SB):
                    r = 10 * c + 5 * s
                    v.wait_ge(proj_ready, r + PROJ_Z + 1)
                    v.wait_ge(sig_ready, 6 * c + 3 * s + 2)
                    chain(v.tensor_tensor(z_sb[:, s, :], bank[2 + PROJ_Z][:], sg_z[:, s, :], ALU.mult))
                    v.wait_ge(sig_ready, 6 * c + 3 * s + 3)
                    w1 = chain(v.tensor_tensor(sg_a[:, s, :], bank[2 + PROJ_GA][:], sg_a[:, s, :], ALU.mult))
                    v.wait_ge(v_l0, w1)
                    v.wait_ge(proj_ready, r + PROJ_GB + 1)
                    w2 = chain(v.tensor_tensor(og_sb[:, s, :], bank[2 + PROJ_GB][:], sg_a[:, s, :], ALU.mult))
                    v.wait_ge(v_l0, w2)
                    v.wait_ge(carry_set, b + 1)
                    w3 = chain(v.tensor_tensor_scan(h_sb[:, s, :], f_sb[:, s, :], z_sb[:, s, :],
                                                    carry0[:, s:s + 1], ALU.mult, ALU.add))
                    v.wait_ge(v_l0, w3)
                    chain(v.tensor_copy(carry0[:, s:s + 1], h_sb[:, s, CH - 1:CH]))
                    v.tensor_tensor(gated[:, s, :], og_sb[:, s, :], h_sb[:, s, :],
                                    ALU.mult).then_inc(gated_ready, 1)
                    if s == 0 and ahead:
                        scaled_tiles(c + 1)
                assert k[0] == SB * L0_SB == L0_STEPS
                for h in range(2):
                    v.wait_ge(mix_ready, 2 * c + h + 1)
                    if h == 0:
                        wait_past(v, mix_stored, 16 * c)
                    v.tensor_tensor(mix_st[:, 2 * h:2 * h + 2, :],
                                    bank[7][:].rearrange("p (t d) -> p t d", d=D),
                                    xn_st[:, 2 * h:2 * h + 2, :], ALU.add).then_inc(mix_added, 1)

            scaled_tiles(0)
            for b in range(B):
                wait_past(v, gated_ready, SB * CPB * b)
                v.memset(carry0[:], 0.0).then_inc(carry_set, 1)
                mixer(CPB * b, b, True)
                last = b == B - 1
                with v.Fori(CPB * b + 1, CPB * (b + 1) - last) as c:
                    mixer(c, b, True)
                if last:
                    mixer(CHUNKS - 1, b, False)

            def hidden(j, half):
                v.wait_ge(silu_ready, 2 * j + half + 1)
                v.tensor_tensor(hid[:, half, :], silu_g[:, half, :], bank[2 + 2 * half][:],
                                ALU.mult).then_inc(hid_ready, 1)

            def result(j, u, waits):
                v.wait_ge(down_ready, j + 1)
                if waits is not None:
                    v.wait_ge(ye_stored[u], waits)
                v.tensor_copy(ye[:, u, :], bank[7][:, 0:D]).then_inc(ye_ready, 1)

            hidden(0, 0)
            hidden(0, 1)
            hidden(1, 0)
            hidden(1, 1)
            result(0, 0, None)
            hidden(2, 0)
            hidden(2, 1)
            result(1, 1, None)
            with v.Fori(0, (SLOTS - 3) // 2) as jj:
                for u in range(2):
                    j = 3 + 2 * jj + u
                    hidden(j, 0)
                    hidden(j, 1)
                    result(j - 1, u, 16 * (jj + 1))
            result(SLOTS - 1, (SLOTS - 1) % 2, 16 * ((SLOTS - 1) // 2))
            v.wait_ge(ld_bw, 16)
            then(v.tensor_reduce(bw_a[:], bw_w, AX_X, ALU.add, apply_absolute_value=True))
            then(v.tensor_scalar(bw_a[:], bw_a[:], 1.0 / D, None, ALU.mult))
            then(v.tensor_scalar(bw_t[:], bw_w, 0.0, None, ALU.is_ge))
            then(v.tensor_scalar(bw_t[:], bw_t[:], 2.0, -1.0, ALU.mult, ALU.add))
            for k in range(KB):
                then(v.scalar_tensor_tensor(bw_t[:, k, :], bw_t[:, k, :], bw_a[:, k:k + 1], bw_w[:, k, :],
                                            ALU.mult, ALU.subtract))
            v.tensor_tensor(bw_t[:], bw_t[:], bw_w, ALU.add).then_inc(bw_ready, 1)
            v.wait_ge(ld_w1, 16 * 8)
            v.tensor_copy(pick[:], pick_f[:]).then_inc(pick_ready, 1)
            v.wait_ge(pick_ready, 1)
            v.wait_ge(bw_ready, 1)
            v.sem_inc(layer0_done, 1)
            v.wait_ge(layer0_done, 5)

            for b in range(B):
                v.memset(carry1[b][:], 0.0).then_inc(scan_set, 1)
                v.memset(halo[b][:], 0.0).then_inc(scan_set, 1)
                v.memset(b_split[b][:].bitcast(F32), 0.0).then_inc(scan_set, 1)
            v.wait_ge(scan_set, 6)

            def at(q, step):
                return PRE_STEPS * q + step

            def places(q, b, j):
                wait_past(v, y_in, 64 * q)
                v.tensor_copy(idx4[:], dest_u[:, bass.ds(b * TPB + j * TPC, TPC)]).then_inc(idx_ready, 1)

            def residual(q, b):
                v.tensor_copy(xpad[:, :, 0:KC - 1], halo[b][:]).then_inc(v_pre, 1)
                v.wait_ge(x_in, 32 * q + 32)
                v.wait_ge(y_silu, TPC * q + TPC)
                v.tensor_tensor(yg[:], yg[:], mix1, ALU.mult).then_inc(v_pre, 1)
                v.wait_ge(v_pre, at(q, 2))
                v.tensor_tensor(yg[:], x_ld, yg[:], ALU.add).then_inc(v_pre, 1)
                v.wait_ge(v_pre, at(q, 3))
                for i in range(TPC):
                    v.bn_stats(st1[:, i, :], yg[:, i, :]).then_inc(v_pre, 1)
                v.wait_ge(v_pre, at(q, 7))
                me, qe, mo, qo = (st1[:, :, k] for k in (1, 2, 4, 5))
                v.tensor_tensor(ln1[:, 0, :], me, mo, ALU.add)
                v.tensor_tensor(ln1[:, 1, :], me, mo, ALU.subtract)
                v.tensor_tensor(ln1[:, 2, :], qe, qo, ALU.add).then_inc(v_pre, 1)
                v.wait_ge(v_pre, at(q, 8))
                v.tensor_scalar(ln1[:, 3, :], ln1[:, 0, :], 0.5, None, ALU.mult)
                v.scalar_tensor_tensor(ln1[:, 1, :], ln1[:, 1, :], 0.25, ln1[:, 1, :], ALU.mult, ALU.mult)
                v.tensor_scalar(ln1[:, 2, :], ln1[:, 2, :], 1.0 / D, EPS, ALU.mult, ALU.add).then_inc(v_pre, 1)
                v.wait_ge(v_pre, at(q, 9))
                v.tensor_tensor(ln1[:, 4, :], ln1[:, 2, :], ln1[:, 1, :], ALU.add).then_inc(var1_ready, 1)

            def normed(q):
                v.wait_ge(rstd1_ready, q + 1)
                for i in range(TPC):
                    ins = v.tensor_scalar(x_ld[:, i, :], yg[:, i, :], ln1[:, 3, i:i + 1], ln1[:, 5, i:i + 1],
                                          ALU.subtract, ALU.mult)
                ins.then_inc(xn2_ready, 1)

            def conv(q, b, d):
                v.wait_ge(tap_ready, DB * q + d + 1)
                for k in range(1, KC):
                    v.wait_ge(v_pre, at(q, 9 + (KC - 2) * d + k - 1))
                    v.scalar_tensor_tensor(soft[:, d, :], xpad[:, d, k:k + CH], cols1[:, d, k:k + 1],
                                           soft[:, d, :], ALU.mult, ALU.add
                                           ).then_inc(v_pre if k < KC - 1 else conv_ready, 1)

            def low_part(q, b):
                v.wait_ge(b_high, q + 1)
                low = b_split[b][SPLIT:SPLIT + DS, :]
                v.tensor_tensor(low, shared(G_BC)[SPLIT:SPLIT + DS, :], low.bitcast(F32),
                                ALU.subtract).then_inc(m_free, 1)

            def keep_x1(q, b):
                wait_past(v, out_ready, 2 * (q - 1))
                v.tensor_copy(x1[b][:], yg[:]).then_inc(x1_kept, 1)

            def slot(q, b, k, ahead, before):
                if ahead:
                    if k == 2:
                        residual(q + 1, 1 - b)
                    if k == 4:
                        normed(q + 1)
                    if 11 <= k < 11 + DB:
                        conv(q + 1, 1 - b, k - 11)
                    if k == 15:
                        v.tensor_copy(halo[1 - b][:], xpad[:, :, CH:CH + KC - 1])
                    if k == 17:
                        low_part(q + 1, 1 - b)
                if before:
                    if k == 2:
                        finish(q - 1, 1 - b)
                    if k == 15:
                        result1(q - 1, 1 - b)
                if ahead and k == 16:
                    keep_x1(q + 1, 1 - b)

            def finish(q, b):
                v.wait_ge(y_added, DS * q + DS + STATE_BUFS)
                v.wait_ge(gates_ready, 2 * q + 2)
                wait_past(v, m_free, group(q, G_OUT) + 2 if not isinstance(q, int) or q > 0 else 0)
                for d in range(DB):
                    v.scalar_tensor_tensor(y_fin[:, d, :], xc[b][:, d, :], cols1[:, d, KC + 2:KC + 3], bank[d][:],
                                           ALU.mult, ALU.add).then_inc(skip_added, 1)
                for d in range(DB):
                    v.wait_ge(skip_added, DB * q + d + 1)
                    v.tensor_tensor(y_fin[:, d, :], y_fin[:, d, :], z_silu[:, d, :], ALU.mult).then_inc(y_ready, 1)

            def result1(q, b):
                for h in range(2):
                    two = slice(2 * h, 2 * h + 2)
                    v.wait_ge(m_free, group(q + 1, G_OUT + h) + 1)
                    v.tensor_tensor(o_st[:, two, :], o_st[:, two, :], g_silu[:, two, :], ALU.mult).then_inc(out_mul, 1)
                    v.wait_ge(out_mul, 2 * q + h + 1)
                    v.tensor_tensor(o_st[:, two, :], o_st[:, two, :], x1[b][:, two, :],
                                    ALU.add).then_inc(out_ready, 1)

            def scan(q, b, ahead, before, fetch_j):
                def inputs(n):
                    v.wait_ge(b_spread, DS * q + n + 1)
                    v.tensor_tensor(dbu[n % 2][:], du[b][:],
                                    bank[4 + n % 2][:].unsqueeze(1).broadcast_to([P, DB, CH]), ALU.mult
                                    ).then_inc(dbu_ready, 1)

                v.wait_ge(du_ready, DB * q + DB)
                inputs(0)
                for n in range(DS):
                    g = DS * q + n
                    if n + 1 < DS:
                        inputs(n + 1)
                    slot(q, b, 2 * n, ahead, before)
                    v.wait_ge(dbu_ready, g + 1)
                    h = hst[n % STATE_BUFS]
                    v.wait_ge(y_added, g + 1)
                    for d in range(DB):
                        u = DB * g + d
                        v.wait_ge(dA_ready, u + 1)
                        v.tensor_tensor_scan(h[:, d, :], dA[:, d, :], dbu[n % 2][:, d, :],
                                             carry1[b][:, n, d:d + 1], ALU.mult, ALU.add).then_inc(scan_done, 1)
                    v.wait_ge(scan_done, DA_BUFS + DB * g + DB)
                    v.tensor_copy(carry1[b][:, n, :], h[:, :, CH - 1]).then_inc(carry_done, 1)
                    slot(q, b, 2 * n + 1, ahead, before)
                    if n == 9 and fetch_j is not None:
                        places(q + 2, b, fetch_j)

            v.sem_inc(scan_done, DA_BUFS)
            places(0, 0, 0)
            for k in range(2 * DS):
                slot(-1, 1, k, True, False)
            places(1, 1, 0)
            scan(0, 0, True, False, 1)
            scan(1, 1, True, True, 1)
            with v.Fori(1, CPB - 1) as j:
                for b in range(B):
                    scan(B * j + b, b, True, True, j + 1)
            scan(CHUNKS - 2, 0, True, True, None)
            scan(CHUNKS - 1, 1, False, True, None)
            finish(CHUNKS - 1, 1)
            result1(CHUNKS - 1, 1)

        @block.tensor
        def _(pe):
            pe.wait_ge(ld_small, 16 * 6)
            def turn_normed(c, u):
                pe.wait_ge(xn_ready, TILES + TPC * c + TPC)
                wait_past(pe, xnT_ready, KB * (c - 1))
                for k in range(KB):
                    for i in range(TPC):
                        ins = pe.transpose(bank[2 * u + k][:, i * P:(i + 1) * P],
                                           normed_st[u][:, i, k * P:(k + 1) * P], ident[:])
                    ins.then_inc(xn_turned, 1)

            def logits(c, u):
                pe.wait_ge(xnT_ready, KB * c + KB)
                for i in range(TPC):
                    for k in range(KB):
                        ins = pe.matmul(bank[7][:, bass.ds((c * TPC + i) * NE, NE)], normedT[u][:, k, i * P:(i + 1) * P],
                                        w_r[:, k, :], start=(k == 0), stop=(k == KB - 1))
                ins.then_inc(logits_ready, 1)

            turn_normed(0, 0)
            turn_normed(1, 1)
            logits(0, 0)
            with pe.Fori(1, CHUNKS // 2) as pair:
                turn_normed(2 * pair, 0)
                logits(2 * pair - 1, 1)
                turn_normed(2 * pair + 1, 1)
                logits(2 * pair, 0)
            logits(CHUNKS - 1, 1)
            pe.wait_ge(onehot_ready, 1)
            pe.wait_ge(set_done, 2)
            n = TILES * NE
            oh = rt[:, 4].rearrange("p t e -> p (t e)")
            pe.matmul(bank[6][:, 0:n], tri[:], oh, start=True, stop=True)
            pe.matmul(bank[6][:, n:2 * n], ones[:], oh, start=True, stop=True).then_inc(ranks_ready, 1)

            pe.wait_ge(ld_w0, 32)

            def turn_inputs(c):
                pe.wait_ge(xr_ready, c + 1)
                for k in range(KB):
                    for i in range(TPC):
                        ins = pe.transpose(bank[k][:, i * P:(i + 1) * P], xr_st[:, i, k * P:(k + 1) * P], ident[:])
                    ins.then_inc(xr_turned, 1)

            def mixer(c, ahead):
                pe.wait_ge(xrT_ready, KB * c + KB)
                for s in range(SB):
                    if s == 0:
                        wait_past(pe, gated_ready, SB * c)
                    for w in range(5):
                        if s > 0 and w == PROJ_F:
                            pe.wait_ge(sig_ready, 6 * c + 1)
                        if s > 0 and w == PROJ_ZG:
                            pe.wait_ge(sig_ready, 6 * c + 2)
                        if s > 0 and w == PROJ_Z:
                            pe.wait_ge(v_l0, L0_STEPS * c + 3)
                        for k in range(KB):
                            ins = pe.matmul(bank[2 + w][:], w0[:, w, k, s * P:(s + 1) * P], xT[:, k, :],
                                            start=(k == 0), stop=(k == KB - 1))
                        ins.then_inc(proj_ready, 1)
                if ahead:
                    turn_inputs(c + 1)
                pe.wait_ge(gated_ready, SB * c + SB)
                for h in range(2):
                    wait_past(pe, mix_added, 2 * c + h)
                    for i in range(2):
                        o = bank[7][:, i * D:(i + 1) * D]
                        pe.matmul(o, ones[0:1, :], bias0[:], start=True, stop=False)
                        t = (2 * h + i) * P
                        for s in range(SB):
                            for part in range(3):
                                ins = pe.matmul(o, gated[:, s, t:t + P], wo_b[:, part, s, :], start=False,
                                                stop=(s == SB - 1 and part == 2))
                    ins.then_inc(mix_ready, 1)

            turn_inputs(0)
            mixer(0, True)
            with pe.Fori(1, CHUNKS - 1) as c:
                mixer(c, True)
            mixer(CHUNKS - 1, False)

            pe.wait_ge(ld_moe, 48)
            pe.wait_ge(eid_ready, 1)
            pe.wait_ge(mix_added, 2 * CHUNKS)

            def turn_in(j, u, loads):
                pe.wait_ge(xg_loaded[u], 16 * loads)
                for k in range(KB):
                    ins = pe.transpose(bank[0][:, k * P:(k + 1) * P], xg[:, u, k * P:(k + 1) * P], ident[:])
                ins.then_inc(xg_turned, 1)

            def up(j, e, half):
                if half == 0:
                    pe.wait_ge(xgT_ready, j + 1)
                for n, w in enumerate((w_g, w_u)):
                    for k in range(KB):
                        ins = pe.matmul(bank[1 + 2 * half + n][:], xgT[:, k, :],
                                        w[:, bass.ds(e * (KB * FF) + (k * FF + half * HALF), HALF)],
                                        start=(k == 0), stop=(k == KB - 1))
                ins.then_inc(up_ready, 1)

            def turn_hidden(j, half):
                pe.wait_ge(hid_ready, 2 * j + half + 1)
                for i in range(FB // 2):
                    ins = pe.transpose(bank[5 + half][:, i * P:(i + 1) * P], hid[:, half, i * P:(i + 1) * P],
                                       ident[:])
                ins.then_inc(hid_turned, 1)

            def down(j, e):
                pe.wait_ge(hidT_ready, 2 * j + 2)
                wait_past(pe, ye_ready, j)
                for i in range(FB):
                    ins = pe.matmul(bank[7][:, 0:D], hidT[:, i, :], w_d[:, bass.ds(e * (FB * D) + i * D, D)],
                                    start=(i == 0), stop=(i == FB - 1))
                ins.then_inc(down_ready, 1)

            def expert(j):
                return pe.value_load(eid[0:1, bass.ds(j, 1)], min_val=0, max_val=NE - 1)

            turn_in(0, 0, 1)
            e0 = expert(0)
            up(0, e0, 0)
            up(0, e0, 1)
            turn_in(1, 1, 1)
            turn_hidden(0, 0)
            def pair(jj):
                for u in range(2):
                    j = 1 + 2 * jj + u
                    e = expert(j)
                    up(j, e, 0)
                    turn_hidden(j - 1, 1)
                    up(j, e, 1)
                    turn_in(j + 1, u, jj + 2)
                    down(j - 1, expert(j - 1))
                    turn_hidden(j, 0)

            pair(0)
            with pe.Fori(1, (SLOTS - 1) // 2) as jj:
                pair(jj)
            turn_hidden(SLOTS - 1, 1)
            down(SLOTS - 1, expert(SLOTS - 1))
            pe.wait_ge(bw_ready, 1)
            pe.wait_ge(ye_ready, SLOTS)
            for k in range(KB):
                for o in range(KB):
                    ins = pe.transpose(bank[6 + k][:, o * P:(o + 1) * P], bw_t[:, o, k * P:(k + 1) * P], ident[:])
                ins.then_inc(bw_turned, 1)
            pe.wait_ge(bwT_ready, KB)
            pe.sem_inc(layer0_done, 1)
            pe.wait_ge(layer0_done, 5)


            def claim(turn, g):
                wait_past(pe, m_free, group(turn, g) - 1)
                return shared(g)

            def skip(turn, g, n):
                wait_past(pe, m_free, group(turn, g))
                pe.sem_inc(m_full, n)
                pe.sem_inc(m_free, n)

            def turn_xn2(t, k):
                pe.wait_ge(xn2_ready, t + 2)
                M = claim(t, G_XNT + k)
                for i in range(TPC):
                    ins = pe.transpose(M[:, i * P:(i + 1) * P], x_ld[:, i, k * P:(k + 1) * P], ident[:])
                ins.then_inc(m_full, 1)

            def in_proj(t, b, e, g):
                M = claim(t, g)
                for k in range(KB):
                    ins = pe.matmul(M[:], w_in[:, k, e * P:(e + 1) * P], xn2T[b][:, k, :],
                                    start=(k == 0), stop=(k == KB - 1))
                ins.then_inc(m_full, 1)

            def x_half(t, b, d):
                if d == 0:
                    pe.wait_ge(m_free, group(t, G_XNT) + 2)
                in_proj(t, b, d, G_X + d)

            def z_half(t, b, d):
                in_proj(t, b, DB + d, (G_Z01 if d < 2 else G_Z23 - 2) + d)

            def gate_half(t, b, h):
                M = claim(t, G_GATE + h)
                for i in range(2):
                    o, r = M[:, i * D:(i + 1) * D], (2 * h + i) * P
                    pe.matmul(o, ones[0:1, :], bias1[:, 0, :], start=True, stop=False)
                    for k in range(KB):
                        ins = pe.matmul(o, xn2T[b][:, k, r:r + P], bwT[:, k, :], start=False, stop=(k == KB - 1))
                ins.then_inc(m_full, 1)

            def low_rank(t, b, g, lo, n):
                pe.wait_ge(xc_ready, DB * (t + 1) + DB)
                M = claim(t, g)
                for d in range(DB):
                    ins = pe.matmul(M[0:n, :], w_x[:, d, lo:lo + n], xc[b][:, d, :], start=(d == 0),
                                    stop=(d == DB - 1))
                ins.then_inc(m_full, 1)

            def dt(t, d):
                M = claim(t, G_DELTA + d)
                pe.matmul(M[:], w_dt[:, d * P:(d + 1) * P], dt_sb[:], start=True, stop=True).then_inc(m_full, 1)

            def out_proj(t, h):
                pe.wait_ge(y_ready, DB * t)
                M = claim(t, G_OUT + h)
                for i in range(2):
                    o, r = M[:, i * D:(i + 1) * D], (2 * h + i) * P
                    pe.matmul(o, ones[0:1, :], bias1[:, 1, :], start=True, stop=False)
                    for d in range(DB):
                        ins = pe.matmul(o, y_fin[:, d, r:r + P], w_out[:, d, :], start=False,
                                        stop=(d == DB - 1))
                ins.then_inc(m_full, 1)

            def slot(t, b, k, prepares, gates, before):
                if prepares:
                    if k in (5, 6):
                        turn_xn2(t, k - 5)
                    if 7 <= k < 7 + DB:
                        x_half(t, 1 - b, k - 7)
                    if k == 15:
                        low_rank(t, 1 - b, G_DT, 0, DR)
                    if k == 16:
                        low_rank(t, 1 - b, G_BC, DR, SPLIT + DS)
                    if 18 <= k < 18 + DB:
                        dt(t, k - 18)
                elif k in (5, 15):
                    skip(t, *((G_XNT, G_OUT - G_XNT) if k == 5 else (G_DT, G_Z23 - G_DT)))
                if before and k in (11, 12):
                    out_proj(t, k - 11)
                if not before and k == 11:
                    skip(t, G_OUT, 2)
                if gates:
                    if k in (13, 14):
                        z_half(t, b, k - 13)
                    if k in (22, 23):
                        z_half(t, b, k - 20)
                    if k in (24, 25):
                        gate_half(t, b, k - 24)
                elif k in (13, 22):
                    skip(t, *((G_Z01, 2) if k == 13 else (G_Z23, 4)))

            def spread(q, b, n):
                g = DS * q + n
                if n == 0:
                    pe.wait_ge(m_free, group(q - 1, G_BC) + 1)
                wait_past(pe, dbu_ready, g - 1)
                pe.matmul(bank[4 + n % 2][:], pick[:, n:n + 1].broadcast_to([2 * SPLIT, P]), b_split[b][:],
                          start=True, stop=True).then_inc(b_spread, 1)

            def add_up(q, n, blocks):
                g = DS * q + n
                if blocks[0] == 0:
                    pe.wait_ge(hc_ready, g + 1)
                    if n == 0:
                        wait_past(pe, skip_added, DB * q)
                for d in blocks:
                    ins = pe.matmul(bank[d][:], ident[:], hst[n % STATE_BUFS][:, d, :], start=(n == 0),
                                    stop=(n == DS - 1))
                if blocks[-1] == DB - 1:
                    ins.then_inc(y_added, 1)

            def scan(q, b, ahead, before):
                for n in range(DS):
                    if n == 0:
                        spread(q, b, 0)
                        spread(q, b, 1)
                    if n + 2 < DS:
                        spread(q, b, n + 2)
                    for half in range(2):
                        slot(q, b, 2 * n + half, ahead, True, before)
                        blocks = range(half * DB // 2, (half + 1) * DB // 2)
                        if n >= LAG:
                            add_up(q, n - LAG, blocks)
                        elif before:
                            add_up(q - 1, DS + n - LAG, blocks)

            pe.sem_inc(y_added, STATE_BUFS)
            for k in range(2 * DS):
                slot(-1, 1, k, True, False, False)
            scan(0, 0, True, False)
            scan(1, 1, True, True)
            with pe.Fori(1, CPB - 1) as j:
                for b in range(B):
                    scan(B * j + b, b, True, True)
            scan(CHUNKS - 2, 0, True, True)
            scan(CHUNKS - 1, 1, False, True)
            for n in range(DS - LAG, DS):
                add_up(CHUNKS - 1, n, range(DB))
            skip(CHUNKS, G_XNT, G_OUT - G_XNT)
            for h in range(2):
                out_proj(CHUNKS, h)


L0_SB = 5
L0_STEPS = SB * L0_SB
PRE_HALO = 1
PRE_STEPS = 9 + DB * (KC - 2)


def kernel(L0_attn_x, L0_attn_rms_w, L0_attn_Wf_w, L0_attn_Wf_b, L0_attn_Wzg_w, L0_attn_Wz_w, L0_attn_Wga_w,
           L0_attn_Wgb_w, L0_attn_Wout_w, L0_attn_Wout_b, L0_ffn_Wr, L0_ffn_br, L0_ffn_Wg, L0_ffn_Wu, L0_ffn_Wd,
           L1_attn_W_in, L1_attn_conv_w, L1_attn_conv_b, L1_attn_W_x, L1_attn_W_dt, L1_attn_b_dt, L1_attn_A_log,
           L1_attn_D, L1_attn_W_out, L1_attn_b_out, L1_ffn_weight, L1_ffn_bias):
    import numpy as np
    import concourse.bacc as bacc
    from concourse.bass_utils import run_bass_kernel_spmd

    def rows(w):
        w = np.asarray(w)
        return np.swapaxes(w.reshape(w.shape[0] // P, P, *w.shape[1:]), 0, 1)

    def spread(r):
        r = np.asarray(r)
        return np.broadcast_to(r, (P, *r.shape))

    wt = [rows(np.asarray(w).T) for w in (L0_attn_Wf_w, L0_attn_Wzg_w, L0_attn_Wz_w, L0_attn_Wga_w, L0_attn_Wgb_w)]
    experts = [np.stack([rows(np.asarray(w)[e]) for e in range(NE)], 1).reshape(P, -1)
               for w in (L0_ffn_Wg, L0_ffn_Wu, L0_ffn_Wd)]
    consts = np.concatenate([np.arange(NE, 0, -1), P * np.arange(TILES), np.arange(SLOTS + 1)]).astype(np.float32)
    w_xT = np.asarray(L1_attn_W_x).T
    w_xT = np.concatenate([w_xT, w_xT[:, DR:DR + DS]], 1)
    arrays = {
        "x": rows(np.asarray(L0_attn_x).reshape(B * T, D)),
        "cols0": np.stack([rows(L0_attn_rms_w), rows(L0_attn_Wf_b)], 2),
        "w_r": rows(L0_ffn_Wr),
        "tri": np.triu(np.ones((P, P), np.float32), 1),
        "small": np.concatenate([spread(L0_ffn_br), spread(consts)], 1),
        "bias0": np.asarray(L0_attn_Wout_b).reshape(1, D),
        "ident": np.eye(P, dtype=np.float32),
        "w0": np.stack(wt, 1),
        "wo": rows(np.asarray(L0_attn_Wout_w).T),
        "w_g": experts[0], "w_u": experts[1], "w_d": experts[2],
        "w_in": rows(np.asarray(L1_attn_W_in).T),
        "w_x": rows(w_xT),
        "pick": np.kron(np.ones((2, 1)), np.eye(SPLIT, DS)).astype(np.float32),
        "w_dt": np.asarray(L1_attn_W_dt).T,
        "w_out": rows(np.asarray(L1_attn_W_out).T),
        "bias1": np.stack([np.asarray(L1_ffn_bias), np.asarray(L1_attn_b_out)])[None],
        "cols1": np.concatenate([rows(L1_attn_conv_w)] + [rows(c)[:, :, None] for c in
                                (L1_attn_conv_b, L1_attn_b_dt, L1_attn_D)], 2),
        "a_log": rows(L1_attn_A_log),
        "bw_w": rows(L1_ffn_weight),
    }
    nc = bacc.Bacc("TRN2", target_bir_lowering=False, num_devices=1)
    ins, aps = {}, {}
    for name, x in arrays.items():
        x = np.ascontiguousarray(x)
        ins[f"in_{name}"] = x
        aps[name] = nc.dram_tensor(f"in_{name}", x.shape, mybir.dt.from_np(x.dtype), kind="ExternalInput").ap()
    out = nc.dram_tensor("out_0", (P, TILES, D), F32, kind="ExternalOutput").ap()
    build(nc, aps, out)
    r = run_bass_kernel_spmd(nc, [ins], core_ids=[0])
    got = r.results[0]["out_0"]
    return np.ascontiguousarray(np.swapaxes(got, 0, 1)).reshape(B, T, D)
```

```python
from contextlib import ExitStack

import concourse.bass as bass
from concourse import mybir

P = 128
B, T, D = 2, 2048, 256
KB = D // P
TILES = B * T // P
TPC = 4
CH = TPC * P
CPB = T // CH
CHUNKS = B * CPB
TPB = T // P
S0 = 256
SB = S0 // P
NE, FF = 4, 1024
FB = FF // P
HALF = FF // 2
SLOTS = TILES + NE - 1
ROWS = SLOTS + 1
DI, DS, DR, KC = 512, 16, 128, 4
DB = DI // P
XR = DR + 2 * DS
EPS = 1e-5
PARTS = 3
B_MIX, B_GATE, B_OUT = range(3)

F32 = mybir.dt.float32
F32R = mybir.dt.float32r
BF16 = mybir.dt.bfloat16
I32 = mybir.dt.int32
U32 = mybir.dt.uint32
ALU = mybir.AluOpType
ACT = mybir.ActivationFunctionType
AX_X = mybir.AxisListType.X

PROJ_F, PROJ_ZG, PROJ_Z, PROJ_GA, PROJ_GB = range(5)
G_XNT, G_X, G_OUT, G_DT, G_BC, G_DELTA, G_Z, G_GATE, GROUPS = 0, 2, 6, 8, 9, 10, 14, 18, 20
STATE_BUFS = 4
LAG = 2
SPLIT = 32
DA_BUFS = DB


def build(nc, a, out):
    with ExitStack() as ctx:
        def sem(name):
            return ctx.enter_context(nc.semaphore(name))

        def sb(stack, name, shape, dt=F32):
            return stack.enter_context(nc.sbuf_tensor(name, shape, dt))

        sorted_x = nc.dram_tensor("sorted_x", (ROWS * P, D), F32).ap()
        sorted_y = nc.dram_tensor("sorted_y", (SLOTS * P, D), F32).ap()
        c_rows = nc.dram_tensor("c_rows", (CHUNKS, DS, CH), F32).ap()
        mixed = nc.dram_tensor("mixed", (P, TILES, D), F32).ap()

        ident = sb(ctx, "ident", [P, P])
        ones = sb(ctx, "ones", [P, P])
        w_in = sb(ctx, "w_in", [P, KB, 2 * DI])
        w_x = sb(ctx, "w_x", [P, DB, DR + SPLIT + DS])
        pick = sb(ctx, "pick", [2 * SPLIT, DS], F32R)
        w_dt = sb(ctx, "w_dt", [P, DI])
        w_out = sb(ctx, "w_out", [P, DB, D])
        bwT = sb(ctx, "bwT", [P, KB, D])
        bias_b = sb(ctx, "bias_b", [PARTS, 3, D], BF16)
        ones_b = sb(ctx, "ones_b", [PARTS, P], BF16)
        cols1 = sb(ctx, "cols1", [P, DB, KC + 3])
        negA = sb(ctx, "negA", [P, DB, DS])
        dest_u = sb(ctx, "dest_u", [P, TILES], U32)
        top_w = sb(ctx, "top_w", [P, TILES])
        idx4 = sb(ctx, "idx4", [P, TPC], U32)
        neg_half = sb(ctx, "neg_half", [P, TILES])

        l0 = ExitStack()
        x_sb = sb(l0, "x_sb", [P, TILES, D])
        w_g = sb(l0, "w_g", [P, NE * KB * FF])
        w_u = sb(l0, "w_u", [P, NE * KB * FF])
        w_d = sb(l0, "w_d", [P, NE * FB * D])
        w0 = sb(l0, "w0", [P, 5, KB, S0])
        wo_f = sb(l0, "wo_f", [P, SB, D])
        wo_b = sb(l0, "wo_b", [P, 3, SB, D], BF16)
        bias_f = sb(l0, "bias_f", [PARTS, 3 * D + PARTS])
        cols0 = sb(l0, "cols0", [P, 2, 2])
        w_r = sb(l0, "w_r", [P, KB, NE])
        tri = sb(l0, "tri", [P, P])
        small = sb(l0, "small", [P, 2 * NE + TILES + SLOTS + 1])
        st0 = sb(l0, "st0", [P, TILES, 6])
        mean0 = sb(l0, "mean0", [P, TILES])
        var0 = sb(l0, "var0", [P, TILES])
        tmp0 = sb(l0, "tmp0", [P, 4, TILES])
        rstd0 = sb(l0, "rstd0", [P, TILES])
        rr0 = sb(l0, "rr0", [P, TILES])
        rt = sb(l0, "rt", [P, 8, TILES, NE])
        rs = sb(l0, "rs", [P, 8, TILES])
        eidf = sb(l0, "eidf", [1, SLOTS + 1, NE])
        eid = sb(l0, "eid", [1, SLOTS + 1], I32)
        xn_st = sb(l0, "xn_st", [P, TPC, D])
        xr_st = sb(l0, "xr_st", [P, TPC, D])
        xT = sb(l0, "xT", [P, KB, CH])
        f_sb = sb(l0, "f_sb", [P, SB, CH], BF16)
        z_sb = sb(l0, "z_sb", [P, SB, CH], BF16)
        og_sb = sb(l0, "og_sb", [P, SB, CH], BF16)
        h_sb = sb(l0, "h_sb", [P, SB, CH], BF16)
        gated = sb(l0, "gated", [P, SB, CH], BF16)
        carry0 = sb(l0, "carry0", [P, SB], BF16)
        sg_z = sb(l0, "sg_z", [P, SB, CH])
        sg_a = sb(l0, "sg_a", [P, SB, CH])
        mix_st = rt[:].rearrange("p k t e -> p (k t e)").rearrange("p (t d) -> p t d", d=D)
        zeros = sg_a[:].rearrange("p s c -> p (s c)").rearrange("p (t d) -> p t d", d=D)
        normed_st, normedT = [xn_st, xr_st], [xT, sg_z]
        wo_r = f_sb[:].bitcast(F32).rearrange("p s c -> p (s c)").rearrange("p (s d) -> p s d", s=SB)
        xgT = f_sb[:].bitcast(F32).rearrange("p s c -> p (s c)")[:, 0:KB * P].rearrange("p (k t) -> p k t", k=KB)
        silu_g, hid = sg_z, sg_a
        xg = og_sb[:].bitcast(F32)
        hidT = xT[:].rearrange("p k c -> p (k c)").rearrange("p (f t) -> p f t", t=P)
        ye = h_sb[:].bitcast(F32)
        bw_w, bw_t = gated[:].bitcast(F32), wo_f
        bw_a = sb(l0, "bw_a", [P, KB])
        pick_f = sb(l0, "pick_f", [2 * SPLIT, DS])
        l0.close()

        l1 = ExitStack()
        xpad = sb(l1, "xpad", [P, DB, KC - 1 + CH])
        halo = [sb(l1, f"halo{b}", [P, DB, KC - 1]) for b in range(B)]
        z_silu = sb(l1, "z_silu", [P, DB, CH])
        xc = [sb(l1, f"xc{b}", [P, DB, CH]) for b in range(B)]
        delta = [sb(l1, f"delta{b}", [P, DB, CH]) for b in range(B)]
        du = [sb(l1, f"du{b}", [P, DB, CH]) for b in range(B)]
        bc_rows = sb(l1, "bc_rows", [2 * DS, CH])
        b_split = [sb(l1, f"b_split{b}", [2 * SPLIT, CH], F32R) for b in range(B)]
        g_silu = sb(l1, "g_silu", [P, TPC, D])
        x1 = [sb(l1, f"x1_{b}", [P, TPC, D]) for b in range(B)]
        carry1 = [sb(l1, f"carry1_{b}", [P, DS, DB]) for b in range(B)]
        dbu = [sb(l1, f"dbu{i}", [P, DB, CH]) for i in range(2)]
        hst = [sb(l1, f"hst{i}", [P, DB, CH]) for i in range(STATE_BUFS)]
        c_bc = sb(l1, "c_bc", [P, STATE_BUFS, CH])
        soft = sb(l1, "soft", [P, DB, CH])
        y_fin = sb(l1, "y_fin", [P, DB, CH])
        yg = sb(l1, "yg", [P, TPC, D])
        dA = sb(l1, "dA", [P, DA_BUFS, CH])
        x_ld = soft[:, 0:2, :].rearrange("p a c -> p (a c)").rearrange("p (t d) -> p t d", d=D)
        mix1 = soft[:, 2:4, :].rearrange("p a c -> p (a c)").rearrange("p (t d) -> p t d", d=D)
        xn2T = [sb(l1, f"xn2T{b}", [P, KB, CH]) for b in range(B)]
        dt_sb = sb(l1, "dt_sb", [P, CH])
        o_st = sb(l1, "o_st", [P, TPC, D])
        st1 = sb(l1, "st1", [P, TPC, 6])
        ln1 = sb(l1, "ln1", [P, 8, TPC])
        l1.close()

        bank = [ctx.enter_context(nc.psum_tensor(f"bank{i}", [P, 512], F32)) for i in range(8)]

        ld_x = [sem(f"ld_x{i}") for i in range(2)]
        ld_small = sem("ld_small")
        ld_w0 = sem("ld_w0")
        ld_moe = sem("ld_moe")
        ld_w1 = sem("ld_w1")
        ld_bw = sem("ld_bw")
        zero_set = sem("zero_set")
        pool_passed = sem("pool_passed")
        sp_passed = sem("sp_passed")
        zero_filled = sem("zero_filled")
        v0 = sem("v0")
        set_done = sem("set_done")
        stats_ready = sem("stats_ready")
        rstd_ready = sem("rstd_ready")
        tile_stats = sem("tile_stats")
        xn_ready = sem("xn_ready")
        xn_turned = sem("xn_turned")
        xnT_ready = sem("xnT_ready")
        logits_ready = sem("logits_ready")
        shifted = sem("shifted")
        exp_ready = sem("exp_ready")
        onehot_ready = sem("onehot_ready")
        ranks_ready = sem("ranks_ready")
        split_ready = sem("split_ready")
        st_ready = sem("st_ready")
        xr_ready = sem("xr_ready")
        xr_turned = sem("xr_turned")
        xrT_ready = sem("xrT_ready")
        proj_ready = sem("proj_ready")
        sig_ready = sem("sig_ready")
        carry_set = sem("carry_set")
        v_l0 = sem("v_l0")
        gated_ready = sem("gated_ready")
        mix_ready = sem("mix_ready")
        mix_added = sem("mix_added")
        mix_stored = sem("mix_stored")
        scattered = sem("scattered")
        eid_ready = sem("eid_ready")
        xg_loaded = [sem(f"xg_loaded{i}") for i in range(2)]
        xg_turned = sem("xg_turned")
        xgT_ready = sem("xgT_ready")
        up_ready = sem("up_ready")
        silu_ready = sem("silu_ready")
        hid_ready = sem("hid_ready")
        hid_turned = sem("hid_turned")
        hidT_ready = sem("hidT_ready")
        down_ready = sem("down_ready")
        ye_ready = sem("ye_ready")
        ye_stored = [sem(f"ye_stored{i}") for i in range(2)]
        bw_ready = sem("bw_ready")
        bw_turned = sem("bw_turned")
        bwT_ready = sem("bwT_ready")
        layer0_done = sem("layer0_done")
        x_in = sem("x_in")
        idx_ready = sem("idx_ready")
        y_in = sem("y_in")
        y_silu = sem("y_silu")
        v_pre = sem("v_pre")
        var1_ready = sem("var1_ready")
        rstd1_ready = sem("rstd1_ready")
        xn2_ready = sem("xn2_ready")
        m_full = sem("m_full")
        m_free = sem("m_free")
        x1_kept = sem("x1_kept")
        tap_ready = sem("tap_ready")
        conv_ready = sem("conv_ready")
        xc_ready = sem("xc_ready")
        soft_ready = sem("soft_ready")
        a_pre = sem("a_pre")
        delta_ready = sem("delta_ready")
        du_ready = sem("du_ready")
        scan_set = sem("scan_set")
        b_spread = sem("b_spread")
        b_high = sem("b_high")
        pick_ready = sem("pick_ready")
        c_stored = sem("c_stored")
        c_loaded = [sem(f"c_loaded{i}") for i in range(2)]
        dA_ready = sem("dA_ready")
        dbu_ready = sem("dbu_ready")
        scan_done = sem("scan_done")
        carry_done = sem("carry_done")
        hc_ready = sem("hc_ready")
        y_added = sem("y_added")
        gates_ready = sem("gates_ready")
        skip_added = sem("skip_added")
        y_ready = sem("y_ready")
        out_mul = sem("out_mul")
        out_ready = sem("out_ready")
        stored = sem("stored")

        def shared(g):
            return bank[6 + g % 2]

        def group(turn, g):
            return GROUPS * (turn + 1) + g

        block = ctx.enter_context(nc.Block())

        def wait_past(eng, semaphore, value):
            if not isinstance(value, int) or value > 0:
                eng.wait_ge(semaphore, value)

        @block.sync
        def _(sp):
            half = TILES // 2
            for i in range(2):
                for q in range(4):
                    lo = i * half + q * half // 4
                    sp.dma_start(x_sb[:, lo:lo + half // 4, :], a["x"][:, lo:lo + half // 4, :]).then_inc(ld_x[i], 16)
            for t, name in ((cols0, "cols0"), (w_r, "w_r"), (tri, "tri"), (small, "small"), (bias_f, "bias_f"),
                            (ident, "ident")):
                sp.dma_start(t[:], a[name]).then_inc(ld_small, 16)
            sp.dma_start(w0[:], a["w0"]).then_inc(ld_w0, 16)
            sp.dma_start(wo_f[:], a["wo"]).then_inc(ld_w0, 16)
            sp.wait_ge(zero_set, 1)
            for s in range(0, ROWS, TPC):
                sp.dma_start(sorted_x[s * P:(s + TPC) * P, :].rearrange("(n p) d -> p n d", p=P),
                             zeros).then_inc(zero_filled, 16)
            for t, name in ((w_g, "w_g"), (w_u, "w_u"), (w_d, "w_d")):
                sp.dma_start(t[:], a[name]).then_inc(ld_moe, 16)
            for t, name in ((w_in, "w_in"), (w_x, "w_x"), (w_dt, "w_dt"), (w_out, "w_out"),
                            (cols1, "cols1"), (negA, "a_log"), (pick_f, "pick")):
                sp.dma_start(t[:], a[name]).then_inc(ld_w1, 16)

            with sp.Fori(0, CHUNKS) as c:
                sp.wait_ge(mix_added, 2 * c + 2)
                sp.dma_start(mixed[:, bass.ds(c * TPC, TPC), :], mix_st).then_inc(mix_stored, 16)

            sp.wait_ge(mix_ready, 2 * CHUNKS)
            sp.dma_start(bw_w, a["bw_w"]).then_inc(ld_bw, 16)
            sp.wait_ge(scattered, 16 * TILES)

            def load(j, u):
                sp.dma_start(xg[:, u, :], sorted_x[bass.ds(j * P, P), :]).then_inc(xg_loaded[u], 16)

            def store(j, u):
                sp.wait_ge(ye_ready, j + 1)
                sp.dma_start(sorted_y[bass.ds(j * P, P), :], ye[:, u, :]).then_inc(ye_stored[u], 16)

            load(0, 0)
            load(1, 1)
            with sp.Fori(0, (SLOTS - 1) // 2) as jj:
                for u in range(2):
                    j = 2 * jj + u
                    sp.wait_ge(xg_turned, j + 1)
                    load(j + 2, u)
                    store(j, u)
            store(SLOTS - 1, 0)
            sp.wait_ge(mix_stored, 16 * CHUNKS)
            sp.wait_ge(ye_stored[0], 16 * ((SLOTS + 1) // 2))
            sp.wait_ge(ye_stored[1], 16 * (SLOTS // 2))
            sp.sem_inc(layer0_done, 1)
            sp.wait_ge(layer0_done, 5)

            def load_chunk(q, b, j):
                wait_past(sp, delta_ready, q)
                sp.sem_inc(sp_passed, 1)
                sp.dma_start(x_ld, a["x"][:, bass.ds(b * TPB + j * TPC, TPC), :]).then_inc(x_in, 16)
                sp.dma_start(mix1, mixed[:, bass.ds(b * TPB + j * TPC, TPC), :]).then_inc(x_in, 16)

            def store_chunk(q, b, j):
                sp.wait_ge(out_ready, 2 * q + 2)
                sp.sem_inc(sp_passed, 1)
                sp.dma_start(out[:, bass.ds(b * TPB + j * TPC, TPC), :], o_st[:]).then_inc(stored, 16)

            def store_c(q):
                sp.wait_ge(m_free, group(q - 1, G_BC) + 1)
                sp.sem_inc(sp_passed, 1)
                sp.dma_start(c_rows[bass.ds(q, 1), :, :], bc_rows[DS:2 * DS, :]).then_inc(c_stored, 16)

            def load_c(q, m):
                if m == 0:
                    sp.wait_ge(c_stored, 16 * q + 16)
                    sp.sem_inc(sp_passed, 1)
                if m < 2:
                    wait_past(sp, hc_ready, DS * q + 2 * m - 2 if not isinstance(q, int) or q > 0 else 0)
                else:
                    sp.wait_ge(hc_ready, DS * q + 2 * m - 2)
                sp.sem_inc(sp_passed, 1)
                slot = 2 * m % STATE_BUFS
                src = c_rows[bass.ds(q, 1), 2 * m:2 * m + 2, :].broadcast_to([P, 2, CH])
                sp.dma_start(c_bc[:, slot:slot + 2, :], src).then_inc(c_loaded[m % 2], 16)

            def scan(q, b, j, ahead, before):
                for m in range(DS // 2):
                    load_c(q, m)
                    if m == 0 and ahead is not None:
                        load_chunk(q + 1, 1 - b, ahead)
                    if m == 5 and before:
                        store_chunk(q - 1, 1 - b, before[0])
                    if m == 6 and ahead is not None:
                        store_c(q + 1)

            load_chunk(0, 0, 0)
            store_c(0)
            scan(0, 0, 0, 0, None)
            scan(1, 1, 0, 1, (0,))
            with sp.Fori(1, CPB - 1) as j:
                for b in range(B):
                    scan(B * j + b, b, j, j + b, (j - 1 + b,))
            scan(CHUNKS - 2, 0, CPB - 1, CPB - 1, (CPB - 2,))
            scan(CHUNKS - 1, 1, CPB - 1, None, (CPB - 1,))
            store_chunk(CHUNKS - 1, 1, CPB - 1)
            sp.wait_ge(stored, 16 * CHUNKS)

        @block.gpsimd
        def _(pool):
            pool.memset(zeros, 0.0).then_inc(zero_set, 1)
            pool.memset(neg_half[:], -0.5).then_inc(set_done, 1)
            pool.memset(ones[:], 1.0).then_inc(set_done, 1)
            pool.memset(ones_b[:], 1.0).then_inc(set_done, 1)
            pool.wait_ge(set_done, 3)
            first, second = slice(0, TILES // 2), slice(TILES // 2, TILES)
            for k, (dst, src, part) in enumerate(((rstd0, 0, first), (rstd0, 0, second), (rr0, 1, slice(0, TILES)))):
                pool.wait_ge(stats_ready, k + 1)
                pool.tensor_tensor(dst[:, part], tmp0[:, src, part], neg_half[:, part],
                                   ALU.pow).then_inc(rstd_ready, 1)
            pool.wait_ge(zero_filled, 16 * (ROWS // TPC))
            with pool.Fori(0, CHUNKS) as c:
                pool.wait_ge(st_ready, c + 1)
                pool.sem_inc(pool_passed, 1)
                for i in range(TPC):
                    pool.indirect_dma_start(
                        sorted_x[:], bass.IndirectOffsetOnAxis(idx4[:, i:i + 1], 0), xn_st[:, i, :], None,
                    ).then_inc(scattered, 16)
            pool.wait_ge(scattered, 16 * TILES)
            pool.sem_inc(layer0_done, 1)
            pool.wait_ge(layer0_done, 5)

            def fetch_experts(q):
                pool.wait_ge(idx_ready, q + 1)
                wait_past(pool, x1_kept, q)
                pool.sem_inc(pool_passed, 1)
                for i in range(TPC):
                    pool.indirect_dma_start(
                        yg[:, i, :], None, sorted_y[:], bass.IndirectOffsetOnAxis(idx4[:, i:i + 1], 0),
                    ).then_inc(y_in, 16)

            def rstd(q):
                pool.wait_ge(var1_ready, q + 1)
                pool.tensor_tensor(ln1[:, 5, :], ln1[:, 4, :], neg_half[:, 0:TPC], ALU.pow).then_inc(rstd1_ready, 1)

            def make_du(q, b):
                pool.wait_ge(delta_ready, q + 1)
                pool.tensor_tensor(du[b][:], delta[b][:], xc[b][:], ALU.mult).then_inc(du_ready, 1)

            def gate_y(q):
                pool.wait_ge(gates_ready, 2 * q + 2)
                for d in range(DB):
                    pool.wait_ge(skip_added, DB * q + d + 1)
                    pool.tensor_tensor(y_fin[:, d, :], y_fin[:, d, :], z_silu[:, d, :], ALU.mult).then_inc(y_ready, 1)

            def result(q, b, h):
                two = slice(2 * h, 2 * h + 2)
                pool.wait_ge(m_free, group(q + 1, G_OUT + h) + 1)
                pool.tensor_tensor(o_st[:, two, :], o_st[:, two, :], g_silu[:, two, :], ALU.mult).then_inc(out_mul, 1)
                pool.wait_ge(out_mul, 2 * q + h + 1)
                pool.tensor_tensor(o_st[:, two, :], o_st[:, two, :], x1[b][:, two, :], ALU.add).then_inc(out_ready, 1)

            def prepare(q, b, n):
                if n == 0:
                    rstd(q)
                if n == 12:
                    make_du(q, b)

            def scan(q, b, ahead, fetch, before):
                for n in range(DS):
                    g = DS * q + n
                    if n == 2 and before:
                        gate_y(q - 1)
                    pool.wait_ge(carry_done, g + 1)
                    pool.wait_ge(c_loaded[n // 2 % 2], 64 * q + 16 * (n // 4 + 1))
                    h = hst[n % STATE_BUFS]
                    c = c_bc[:, n % STATE_BUFS, :].unsqueeze(1).broadcast_to([P, DB, CH])
                    pool.tensor_tensor(h[:], h[:], c, ALU.mult).then_inc(hc_ready, 1)
                    if n in (6, 7) and before:
                        result(q - 1, 1 - b, n - 6)
                    if ahead:
                        prepare(q + 1, 1 - b, n)
                    if n == 11 and fetch:
                        fetch_experts(q + 2)

            fetch_experts(0)
            rstd(0)
            fetch_experts(1)
            scan(0, 0, True, True, False)
            scan(1, 1, True, True, True)
            with pool.Fori(1, CPB - 1) as j:
                for b in range(B):
                    scan(B * j + b, b, True, True, True)
            scan(CHUNKS - 2, 0, True, False, True)
            scan(CHUNKS - 1, 1, False, False, True)

        @block.scalar
        def _(act):
            act.wait_ge(ld_small, 16 * 6)
            def turn_normed(c, u):
                wait_past(act, logits_ready, c - 1)
                for k in range(KB):
                    act.wait_ge(xn_turned, KB * c + k + 1)
                    act.copy(normedT[u][:, k, :], bank[2 * u + k][:]).then_inc(xnT_ready, 1)

            turn_normed(0, 0)
            turn_normed(1, 1)
            with act.Fori(1, CHUNKS // 2) as pair:
                for u in range(2):
                    turn_normed(2 * pair + u, u)
            act.wait_ge(shifted, 1)
            act.activation(rt[:, 2], rt[:, 1], ACT.Exp).then_inc(exp_ready, 1)

            def turn_inputs(c):
                for k in range(KB):
                    act.wait_ge(xr_turned, KB * c + k + 1)
                    wait_past(act, proj_ready, 10 * c)
                    act.activation(xT[:, k, :], bank[k][:], ACT.Copy, scale=cols0[:, k, 0:1]).then_inc(xrT_ready, 1)

            def mixer(c, ahead):
                for s in range(SB):
                    r = 10 * c + 5 * s
                    act.wait_ge(proj_ready, r + PROJ_F + 1)
                    wait_past(act, gated_ready, SB * c)
                    act.activation(f_sb[:, s, :], bank[2 + PROJ_F][:], ACT.Sigmoid,
                                   bias=cols0[:, s, 1:2]).then_inc(sig_ready, 1)
                    act.wait_ge(proj_ready, r + PROJ_ZG + 1)
                    act.activation(sg_z[:, s, :], bank[2 + PROJ_ZG][:], ACT.Sigmoid).then_inc(sig_ready, 1)
                    act.wait_ge(proj_ready, r + PROJ_GA + 1)
                    act.activation(sg_a[:, s, :], bank[2 + PROJ_GA][:], ACT.Sigmoid).then_inc(sig_ready, 1)
                if ahead:
                    turn_inputs(c + 1)

            act.wait_ge(zero_filled, 16 * (ROWS // TPC))
            turn_inputs(0)
            mixer(0, True)
            with act.Fori(1, CHUNKS - 1) as c:
                mixer(c, True)
            mixer(CHUNKS - 1, False)

            def turn_in(j):
                act.wait_ge(xg_turned, j + 1)
                act.copy(xgT, bank[0][:, 0:D]).then_inc(xgT_ready, 1)

            def gate(j, half):
                act.wait_ge(up_ready, 2 * j + half + 1)
                act.activation(silu_g[:, half, :], bank[1 + 2 * half][:], ACT.Silu).then_inc(silu_ready, 1)

            def turn_hidden(j, half):
                act.wait_ge(hid_turned, 2 * j + half + 1)
                act.copy(hidT[:, half * FB // 2:(half + 1) * FB // 2, :], bank[5 + half][:]).then_inc(hidT_ready, 1)

            act.wait_ge(ld_w1, 16 * 7)
            act.activation(negA[:], negA[:], ACT.Exp).then_inc(a_pre, 1)
            act.wait_ge(a_pre, 1)
            act.mul(negA[:], negA[:], -1.0).then_inc(a_pre, 1)
            turn_in(0)
            gate(0, 0)
            gate(0, 1)
            act.wait_ge(bw_turned, 1)
            act.copy(bwT[:], bank[7][:].rearrange("p (k o) -> p k o", k=KB)).then_inc(bwT_ready, 1)
            turn_in(1)
            turn_hidden(0, 0)
            with act.Fori(0, SLOTS - 1) as jj:
                j = jj + 1
                gate(j, 0)
                turn_hidden(j - 1, 1)
                gate(j, 1)
                turn_in(j + 1)
                turn_hidden(j, 0)
            turn_hidden(SLOTS - 1, 1)
            act.wait_ge(a_pre, 2)
            act.wait_ge(bwT_ready, 1)
            act.sem_inc(layer0_done, 1)
            act.wait_ge(layer0_done, 5)


            def take(turn, g):
                act.wait_ge(m_full, group(turn, g) + 1)
                return shared(g)

            def silus(q, b, j, prepares, gates):
                if prepares:
                    act.wait_ge(y_in, 64 * (q + 1) + 64)
                    for i in range(TPC):
                        act.activation(yg[:, i, :], yg[:, i, :], ACT.Silu,
                                       scale=top_w[:, bass.ds((1 - b) * TPB + j * TPC + i, 1)]).then_inc(y_silu, 1)
                if gates:
                    act.wait_ge(m_free, group(q - 1, G_GATE) + 2)
                    act.activation(z_silu[:], z_silu[:], ACT.Silu).then_inc(gates_ready, 1)
                    act.activation(g_silu[:], g_silu[:], ACT.Silu).then_inc(gates_ready, 1)

            def turn_xn2(t, b, k):
                M = take(t, G_XNT + k)
                act.copy(xn2T[b][:, k, :], M[:]).then_inc(m_free, 1)

            def x_half(t, d):
                M = take(t, G_X + d)
                act.wait_ge(v_pre, PRE_STEPS * (t + 1) + PRE_HALO)
                act.copy(xpad[:, d, KC - 1:], M[:]).then_inc(m_free, 1)
                act.wait_ge(m_free, group(t, G_X + d) + 1)
                act.activation(soft[:, d, :], xpad[:, d, 0:CH], ACT.Copy, scale=cols1[:, d, 0:1]).then_inc(tap_ready, 1)

            def raw_out(t, h):
                M = take(t, G_OUT + h)
                if h == 0:
                    wait_past(act, stored, 16 * (t - 1))
                act.copy(o_st[:, 2 * h:2 * h + 2, :], M[:]).then_inc(m_free, 1)

            def z_half(t, d):
                M = take(t, G_Z + d)
                if d == 0:
                    wait_past(act, y_ready, DB * t)
                act.copy(z_silu[:, d, :], M[:]).then_inc(m_free, 1)

            def gate_half(t, h):
                M = take(t, G_GATE + h)
                if h == 0:
                    wait_past(act, out_mul, 2 * t)
                act.copy(g_silu[:, 2 * h:2 * h + 2, :], M[:]).then_inc(m_free, 1)

            def silu_conv(q, b):
                for d in range(DB):
                    act.wait_ge(conv_ready, DB * q + d + 1)
                    act.activation(xc[b][:, d, :], soft[:, d, :], ACT.Silu,
                                   bias=cols1[:, d, KC:KC + 1]).then_inc(xc_ready, 1)

            def dt_rows(t):
                M = take(t, G_DT)
                act.copy(dt_sb[:], M[:]).then_inc(m_free, 1)

            def bc(t, b):
                M = take(t, G_BC)
                act.copy(bc_rows[:], M[0:2 * DS, :])
                act.copy(b_split[b][0:DS, :], M[0:DS, :])
                act.copy(b_split[b][SPLIT:SPLIT + DS, :], M[SPLIT:SPLIT + DS, :]).then_inc(b_high, 1)

            def softplus(t, b, d):
                if d == 0:
                    act.wait_ge(m_free, group(t, G_BC) + 1)
                M = take(t, G_DELTA + d)
                act.activation(soft[:, d, :], M[:], ACT.Abs, bias=cols1[:, d, KC + 1:KC + 2]).then_inc(a_pre, 1)
                act.activation(delta[b][:, d, :], M[:], ACT.Relu,
                               bias=cols1[:, d, KC + 1:KC + 2]).then_inc(m_free, 1)
                act.wait_ge(a_pre, 2 + 2 * (DB * (t + 1) + d) + 1)
                act.activation(soft[:, d, :], soft[:, d, :], ACT.Exp, scale=-1.0).then_inc(a_pre, 1)

            def log_part(q):
                act.wait_ge(a_pre, 2 + 2 * DB * (q + 1))
                act.activation(soft[:], soft[:], ACT.Ln, bias=ones[:, 0:1]).then_inc(soft_ready, 1)

            def slot(t, b, k, prepares, gates, before):
                if prepares:
                    if k in (6, 7):
                        turn_xn2(t, 1 - b, k - 6)
                    if 8 <= k < 8 + DB:
                        x_half(t, k - 8)
                    if k == 14:
                        silu_conv(t + 1, 1 - b)
                    if k == 16:
                        dt_rows(t)
                    if k == 17:
                        bc(t, 1 - b)
                    if 19 <= k < 19 + DB:
                        softplus(t, 1 - b, k - 19)
                    if k == 23:
                        log_part(t + 1)
                if before and k in (12, 13):
                    raw_out(t, k - 12)
                if gates:
                    if 23 <= k < 23 + DB:
                        z_half(t, k - 23)
                    if k in (27, 28):
                        gate_half(t, k - 27)

            def scan(q, b, j, before):
                ahead = j is not None
                for n in range(DS):
                    g = DS * q + n
                    for d in range(DB):
                        u = DB * g + d
                        if n == 0 and d == 0:
                            act.wait_ge(delta_ready, q + 1)
                        act.wait_ge(scan_done, u + 1)
                        act.activation(dA[:, d, :], delta[b][:, d, :], ACT.Exp,
                                       scale=negA[:, d, n:n + 1]).then_inc(dA_ready, 1)
                        if d == 1:
                            slot(q, b, 2 * n, ahead, True, before)
                    slot(q, b, 2 * n + 1, ahead, True, before)
                    if n == 0:
                        silus(q, b, j, ahead, before)

            silus(-1, 1, 0, True, False)
            for k in range(2 * DS):
                slot(-1, 1, k, True, False, False)
            scan(0, 0, 0, False)
            scan(1, 1, 1, True)
            with act.Fori(1, CPB - 1) as j:
                for b in range(B):
                    scan(B * j + b, b, j + b, True)
            scan(CHUNKS - 2, 0, CPB - 1, True)
            scan(CHUNKS - 1, 1, None, True)
            silus(CHUNKS, 0, None, False, True)
            for h in range(2):
                raw_out(CHUNKS, h)

        @block.vector
        def _(v):
            steps = [0]

            def then(ins):
                steps[0] += 1
                ins.then_inc(v0, 1)
                v.wait_ge(v0, steps[0])

            def statistics(i):
                lo = i * TILES // 2
                part = slice(lo, lo + TILES // 2)
                v.wait_ge(ld_x[i], 64)
                with v.Fori(0, TILES // 2 // TPC) as c:
                    for k in range(TPC):
                        t = c * TPC + k + lo
                        v.bn_stats(st0[:, bass.ds(t, 1), :], x_sb[:, bass.ds(t, 1), :]).then_inc(tile_stats, 1)
                v.wait_ge(tile_stats, lo + TILES // 2)
                me, qe, mo, qo = (st0[:, part, k] for k in (1, 2, 4, 5))
                mean, var = mean0[:, part], var0[:, part]
                diff, sq = tmp0[:, 2, part], tmp0[:, 3, part]
                then(v.tensor_tensor(mean, me, mo, ALU.add))
                then(v.tensor_scalar(mean, mean, 0.5, None, ALU.mult))
                then(v.tensor_tensor(diff, me, mo, ALU.subtract))
                then(v.scalar_tensor_tensor(diff, diff, 0.25, diff, ALU.mult, ALU.mult))
                then(v.tensor_tensor(sq, qe, qo, ALU.add))
                then(v.scalar_tensor_tensor(var, sq, 1.0 / D, diff, ALU.mult, ALU.add))
                v.tensor_scalar(tmp0[:, 0, part], var, EPS, None, ALU.add).then_inc(stats_ready, 1)

            def normed_tiles(c, u):
                wait_past(v, xn_turned, KB * (c - 1))
                for i in range(TPC):
                    t = c * TPC + i
                    v.tensor_scalar(normed_st[u][:, i, :], x_sb[:, bass.ds(t, 1), :], mean0[:, bass.ds(t, 1)],
                                    rstd0[:, bass.ds(t, 1)], ALU.subtract, ALU.mult).then_inc(xn_ready, 1)

            statistics(0)
            v.wait_ge(rstd_ready, 1)
            normed_tiles(0, 0)
            normed_tiles(1, 1)
            statistics(1)
            normed_tiles(2, 0)
            normed_tiles(3, 1)
            v.wait_ge(rstd_ready, 2)
            then(v.tensor_tensor(tmp0[:, 2, :], rstd0[:], rstd0[:], ALU.mult))
            then(v.tensor_tensor(tmp0[:, 2, :], tmp0[:, 2, :], var0[:], ALU.mult))
            v.tensor_scalar(tmp0[:, 1, :], tmp0[:, 2, :], EPS, None, ALU.add).then_inc(stats_ready, 1)
            with v.Fori(CHUNKS // 4, CHUNKS // 2) as pair:
                for u in range(2):
                    normed_tiles(2 * pair + u, u)
            v.wait_ge(rstd_ready, 3)
            then(v.tensor_tensor(rr0[:], rr0[:], rstd0[:], ALU.mult))

            v.wait_ge(ld_w0, 32)
            then(v.tensor_copy(wo_b[:, 0], wo_f[:]))
            then(v.tensor_tensor(wo_r, wo_f[:], wo_b[:, 0], ALU.subtract))
            then(v.tensor_copy(wo_b[:, 1], wo_r))
            then(v.tensor_tensor(wo_r, wo_r, wo_b[:, 1], ALU.subtract))
            v.tensor_copy(wo_b[:, 2], wo_r).then_inc(split_ready, 1)
            v.wait_ge(ld_small, 16 * 6)
            biases, own = bias_f[:, 0:3 * D], bias_f[:, 3 * D:]
            parts = [t[0:PARTS].rearrange("p s c -> p (s c)")[:, 0:3 * D] for t in (gated, og_sb, h_sb)]
            for k in range(PARTS):
                then(v.tensor_copy(parts[k], biases))
                if k < PARTS - 1:
                    then(v.tensor_tensor(biases, biases, parts[k], ALU.subtract))
            then(v.tensor_scalar(biases, parts[0], own[:, 0:1], None, ALU.mult))
            then(v.scalar_tensor_tensor(biases, parts[1], own[:, 1:2], biases, ALU.mult, ALU.add))
            v.scalar_tensor_tensor(bias_b[:].rearrange("p b d -> p (b d)"), parts[2], own[:, 2:3], biases,
                                   ALU.mult, ALU.add).then_inc(split_ready, 1)

            def scaled_tiles(c):
                if isinstance(c, int) and c == 0:
                    v.wait_ge(xn_turned, KB * CHUNKS)
                wait_past(v, xr_turned, KB * c)
                for i in range(TPC):
                    t = c * TPC + i
                    ins = v.tensor_scalar(xr_st[:, i, :], x_sb[:, bass.ds(t, 1), :], mean0[:, bass.ds(t, 1)],
                                          rr0[:, bass.ds(t, 1)], ALU.subtract, ALU.mult)
                ins.then_inc(xr_ready, 1)

            def per_tile(x):
                return x.unsqueeze(2).broadcast_to([P, TILES, NE])

            def per_expert(x):
                return x.unsqueeze(1).broadcast_to([P, TILES, NE])

            br, prio = small[:, 0:NE], small[:, NE:2 * NE]
            steps128 = small[:, 2 * NE:2 * NE + TILES]
            slot_no = small[0:1, 2 * NE + TILES:]
            logits, shift, ex, eq, oh, tot, cum = (rt[:, k] for k in range(7))
            v.wait_ge(logits_ready, CHUNKS)
            then(v.tensor_tensor(logits, bank[7][:, 0:TILES * NE].rearrange("p (t e) -> p t e", e=NE),
                                 per_expert(br), ALU.add))
            then(v.tensor_reduce(rs[:, 0, :], logits, AX_X, ALU.max))
            v.tensor_tensor(shift, logits, per_tile(rs[:, 0, :]), ALU.subtract).then_inc(shifted, 1)
            then(v.tensor_tensor(eq, logits, per_tile(rs[:, 0, :]), ALU.is_equal))
            then(v.tensor_tensor(eq, eq, per_expert(prio), ALU.mult))
            then(v.tensor_reduce(rs[:, 1, :], eq, AX_X, ALU.max))
            v.tensor_tensor(oh, eq, per_tile(rs[:, 1, :]), ALU.is_equal).then_inc(onehot_ready, 1)
            scaled_tiles(0)
            v.wait_ge(exp_ready, 1)
            then(v.tensor_reduce(rs[:, 2, :], ex, AX_X, ALU.add))
            then(v.reciprocal(top_w[:], rs[:, 2, :]))
            v.wait_ge(ranks_ready, 1)
            rank_ps = bank[7][:, TILES * NE:2 * TILES * NE].rearrange("p (t e) -> p t e", e=NE)
            then(v.tensor_copy(tot, bank[7][:, 2 * TILES * NE:3 * TILES * NE]))
            then(v.memset(rs[:, 3, :], 1.0))
            for e in range(NE):
                then(v.tensor_tensor_scan(cum[:, :, e], rs[:, 3, :], tot[:, :, e], 0.0, ALU.mult, ALU.add))
            cnt = cum[:, TILES - 1, :]
            cmp = rt[:, 7].rearrange("p t e -> p (t e)").rearrange("p (e t) -> p e t", e=NE)
            then(v.tensor_tensor(cmp, cnt.unsqueeze(2).broadcast_to([P, NE, TILES]),
                                 steps128.unsqueeze(1).broadcast_to([P, NE, TILES]), ALU.is_gt))
            nt, end, start = rs[:, 4, 0:NE], rs[:, 5, 0:NE], rs[:, 6, 0:NE]
            then(v.tensor_reduce(nt, cmp, AX_X, ALU.add))
            then(v.tensor_tensor_scan(end, rs[:, 3, 0:NE], nt, 0.0, ALU.mult, ALU.add))
            then(v.tensor_tensor(start, end, nt, ALU.subtract))
            then(v.tensor_tensor(cum, cum, tot, ALU.subtract))
            then(v.tensor_tensor(cum, cum, rank_ps, ALU.add))
            then(v.scalar_tensor_tensor(cum, per_expert(start), float(P), cum, ALU.mult, ALU.add))
            then(v.tensor_tensor(cum, cum, oh, ALU.mult))
            then(v.tensor_reduce(rs[:, 7, :], cum, AX_X, ALU.add))
            then(v.tensor_copy(dest_u[:], rs[:, 7, :]))
            n_slot = SLOTS + 1
            ef = eidf[:, :, 0:NE - 1]
            then(v.tensor_tensor(ef, slot_no.unsqueeze(2).broadcast_to([1, n_slot, NE - 1]),
                                 start[0:1, 1:NE].unsqueeze(1).broadcast_to([1, n_slot, NE - 1]), ALU.is_ge))
            then(v.tensor_reduce(eidf[:, :, NE - 1], ef, AX_X, ALU.add))
            v.tensor_copy(eid[:], eidf[:, :, NE - 1]).then_inc(eid_ready, 1)

            def mixer(c, b, ahead):
                k = [0]

                def chain(ins):
                    k[0] += 1
                    ins.then_inc(v_l0, 1)
                    return c * L0_STEPS + k[0]

                wait_past(v, scattered, 64 * c)
                wait_past(v, mix_added, 2 * c)
                for i in range(TPC):
                    t = c * TPC + i
                    v.tensor_scalar(xn_st[:, i, :], x_sb[:, bass.ds(t, 1), :], mean0[:, bass.ds(t, 1)],
                                    rstd0[:, bass.ds(t, 1)], ALU.subtract, ALU.mult)
                v.tensor_copy(idx4[:], dest_u[:, bass.ds(c * TPC, TPC)]).then_inc(st_ready, 1)
                for s in range(SB):
                    r = 10 * c + 5 * s
                    v.wait_ge(proj_ready, r + PROJ_Z + 1)
                    v.wait_ge(sig_ready, 6 * c + 3 * s + 2)
                    w1 = chain(v.tensor_tensor(z_sb[:, s, :], bank[2 + PROJ_Z][:], sg_z[:, s, :], ALU.mult))
                    v.wait_ge(v_l0, w1)
                    v.wait_ge(carry_set, b + 1)
                    w2 = chain(v.tensor_tensor_scan(h_sb[:, s, :], f_sb[:, s, :], z_sb[:, s, :],
                                                    carry0[:, s:s + 1], ALU.mult, ALU.add))
                    v.wait_ge(v_l0, w2)
                    chain(v.tensor_copy(carry0[:, s:s + 1], h_sb[:, s, CH - 1:CH]))
                    v.wait_ge(sig_ready, 6 * c + 3 * s + 3)
                    w4 = chain(v.tensor_tensor(sg_a[:, s, :], bank[2 + PROJ_GA][:], sg_a[:, s, :], ALU.mult))
                    v.wait_ge(v_l0, w4)
                    v.wait_ge(proj_ready, r + PROJ_GB + 1)
                    w5 = chain(v.tensor_tensor(og_sb[:, s, :], bank[2 + PROJ_GB][:], sg_a[:, s, :], ALU.mult))
                    v.wait_ge(v_l0, w5)
                    v.tensor_tensor(gated[:, s, :], og_sb[:, s, :], h_sb[:, s, :],
                                    ALU.mult).then_inc(gated_ready, 1)
                    if s == 0 and ahead:
                        scaled_tiles(c + 1)
                assert k[0] == SB * L0_SB == L0_STEPS
                for h in range(2):
                    v.wait_ge(mix_ready, 2 * c + h + 1)
                    if h == 0:
                        wait_past(v, mix_stored, 16 * c)
                    v.tensor_tensor(mix_st[:, 2 * h:2 * h + 2, :],
                                    bank[7 - h][:].rearrange("p (t d) -> p t d", d=D),
                                    xn_st[:, 2 * h:2 * h + 2, :], ALU.add).then_inc(mix_added, 1)

            for b in range(B):
                wait_past(v, gated_ready, SB * CPB * b)
                v.memset(carry0[:], 0.0).then_inc(carry_set, 1)
                mixer(CPB * b, b, True)
                last = b == B - 1
                with v.Fori(CPB * b + 1, CPB * (b + 1) - last) as c:
                    mixer(c, b, True)
                if last:
                    mixer(CHUNKS - 1, b, False)

            v.wait_ge(ld_bw, 16)
            then(v.tensor_reduce(bw_a[:], bw_w, AX_X, ALU.add, apply_absolute_value=True))
            then(v.tensor_scalar(bw_a[:], bw_a[:], 1.0 / D, None, ALU.mult))
            then(v.tensor_scalar(bw_t[:], bw_w, 0.0, None, ALU.is_ge))
            then(v.tensor_scalar(bw_t[:], bw_t[:], 2.0, -1.0, ALU.mult, ALU.add))
            for k in range(KB):
                then(v.scalar_tensor_tensor(bw_t[:, k, :], bw_t[:, k, :], bw_a[:, k:k + 1], bw_w[:, k, :],
                                            ALU.mult, ALU.subtract))
            v.tensor_tensor(bw_t[:], bw_t[:], bw_w, ALU.add).then_inc(bw_ready, 1)
            v.wait_ge(ld_w1, 16 * 7)
            v.tensor_copy(pick[:], pick_f[:]).then_inc(pick_ready, 1)

            def hidden(j, half):
                v.wait_ge(silu_ready, 2 * j + half + 1)
                v.tensor_tensor(hid[:, half, :], silu_g[:, half, :], bank[2 + 2 * half][:],
                                ALU.mult).then_inc(hid_ready, 1)

            def result(j, u, waits):
                v.wait_ge(down_ready, j + 1)
                if waits is not None:
                    v.wait_ge(ye_stored[u], waits)
                v.tensor_copy(ye[:, u, :], bank[7][:, 0:D]).then_inc(ye_ready, 1)

            hidden(0, 0)
            hidden(0, 1)
            hidden(1, 0)
            hidden(1, 1)
            result(0, 0, None)
            hidden(2, 0)
            hidden(2, 1)
            result(1, 1, None)
            with v.Fori(0, (SLOTS - 3) // 2) as jj:
                for u in range(2):
                    j = 3 + 2 * jj + u
                    hidden(j, 0)
                    hidden(j, 1)
                    result(j - 1, u, 16 * (jj + 1))
            result(SLOTS - 1, (SLOTS - 1) % 2, 16 * ((SLOTS - 1) // 2))
            v.wait_ge(pick_ready, 1)
            v.wait_ge(bw_ready, 1)
            v.sem_inc(layer0_done, 1)
            v.wait_ge(layer0_done, 5)

            for b in range(B):
                v.memset(carry1[b][:], 0.0).then_inc(scan_set, 1)
                v.memset(halo[b][:], 0.0).then_inc(scan_set, 1)
                v.memset(b_split[b][:].bitcast(F32), 0.0).then_inc(scan_set, 1)
            v.wait_ge(scan_set, 6)

            def at(q, step):
                return PRE_STEPS * q + step

            def places(q, b, j):
                wait_past(v, y_in, 64 * q)
                v.tensor_copy(idx4[:], dest_u[:, bass.ds(b * TPB + j * TPC, TPC)]).then_inc(idx_ready, 1)

            def residual(q, b):
                v.tensor_copy(xpad[:, :, 0:KC - 1], halo[b][:]).then_inc(v_pre, 1)
                v.wait_ge(x_in, 32 * q + 32)
                v.wait_ge(y_silu, TPC * q + TPC)
                v.tensor_tensor(yg[:], yg[:], mix1, ALU.mult).then_inc(v_pre, 1)
                v.wait_ge(v_pre, at(q, 2))
                v.tensor_tensor(yg[:], x_ld, yg[:], ALU.add).then_inc(v_pre, 1)
                v.wait_ge(v_pre, at(q, 3))
                for i in range(TPC):
                    v.bn_stats(st1[:, i, :], yg[:, i, :]).then_inc(v_pre, 1)
                v.wait_ge(v_pre, at(q, 7))
                me, qe, mo, qo = (st1[:, :, k] for k in (1, 2, 4, 5))
                v.tensor_tensor(ln1[:, 0, :], me, mo, ALU.add)
                v.tensor_tensor(ln1[:, 1, :], me, mo, ALU.subtract)
                v.tensor_tensor(ln1[:, 2, :], qe, qo, ALU.add).then_inc(v_pre, 1)
                v.wait_ge(v_pre, at(q, 8))
                v.tensor_scalar(ln1[:, 3, :], ln1[:, 0, :], 0.5, None, ALU.mult)
                v.scalar_tensor_tensor(ln1[:, 1, :], ln1[:, 1, :], 0.25, ln1[:, 1, :], ALU.mult, ALU.mult)
                v.tensor_scalar(ln1[:, 2, :], ln1[:, 2, :], 1.0 / D, EPS, ALU.mult, ALU.add).then_inc(v_pre, 1)
                v.wait_ge(v_pre, at(q, 9))
                v.tensor_tensor(ln1[:, 4, :], ln1[:, 2, :], ln1[:, 1, :], ALU.add).then_inc(var1_ready, 1)

            def normed(q):
                v.wait_ge(rstd1_ready, q + 1)
                for i in range(TPC):
                    ins = v.tensor_scalar(x_ld[:, i, :], yg[:, i, :], ln1[:, 3, i:i + 1], ln1[:, 5, i:i + 1],
                                          ALU.subtract, ALU.mult)
                ins.then_inc(xn2_ready, 1)

            def conv(q, b, pair):
                for k in range(1, KC):
                    for i in range(2):
                        d = 2 * pair + i
                        if k == 1:
                            v.wait_ge(tap_ready, DB * q + d + 1)
                        else:
                            v.wait_ge(v_pre, at(q, 9 + 2 * ((KC - 2) * pair + k - 2) + i + 1))
                        v.scalar_tensor_tensor(soft[:, d, :], xpad[:, d, k:k + CH], cols1[:, d, k:k + 1],
                                               soft[:, d, :], ALU.mult, ALU.add
                                               ).then_inc(v_pre if k < KC - 1 else conv_ready, 1)

            def low_part(q, b):
                v.wait_ge(b_high, q + 1)
                low = b_split[b][SPLIT:SPLIT + DS, :]
                v.tensor_tensor(low, shared(G_BC)[SPLIT:SPLIT + DS, :], low.bitcast(F32),
                                ALU.subtract).then_inc(m_free, 1)

            def make_delta(q, b):
                v.wait_ge(soft_ready, q + 1)
                v.tensor_tensor(delta[b][:], delta[b][:], soft[:], ALU.add).then_inc(delta_ready, 1)

            def keep_x1(q, b):
                wait_past(v, out_ready, 2 * (q - 1))
                v.tensor_copy(x1[b][:], yg[:]).then_inc(x1_kept, 1)

            def slot(q, b, k, ahead, before):
                if ahead:
                    if k == 19:
                        keep_x1(q + 1, 1 - b)
                    if k == 2:
                        residual(q + 1, 1 - b)
                    if k == 4:
                        normed(q + 1)
                    if k in (12, 13):
                        conv(q + 1, 1 - b, k - 12)
                    if k == 15:
                        v.tensor_copy(halo[1 - b][:], xpad[:, :, CH:CH + KC - 1])
                    if k == 17:
                        low_part(q + 1, 1 - b)
                    if k == 24:
                        make_delta(q + 1, 1 - b)
                if before:
                    if k == 3:
                        add_skip(q - 1, 1 - b)

            def add_skip(q, b):
                v.wait_ge(y_added, DS * q + DS + STATE_BUFS)
                wait_past(v, m_free, group(q, G_OUT) + 2 if not isinstance(q, int) or q > 0 else 0)
                for d in range(DB):
                    v.scalar_tensor_tensor(y_fin[:, d, :], xc[b][:, d, :], cols1[:, d, KC + 2:KC + 3], bank[d][:],
                                           ALU.mult, ALU.add).then_inc(skip_added, 1)

            def gate_y(q):
                v.wait_ge(gates_ready, 2 * q + 2)
                for d in range(DB):
                    v.wait_ge(skip_added, DB * q + d + 1)
                    v.tensor_tensor(y_fin[:, d, :], y_fin[:, d, :], z_silu[:, d, :], ALU.mult).then_inc(y_ready, 1)

            def result(q, b):
                for h in range(2):
                    two = slice(2 * h, 2 * h + 2)
                    v.wait_ge(m_free, group(q + 1, G_OUT + h) + 1)
                    v.tensor_tensor(o_st[:, two, :], o_st[:, two, :], g_silu[:, two, :], ALU.mult).then_inc(out_mul, 1)
                    v.wait_ge(out_mul, 2 * q + h + 1)
                    v.tensor_tensor(o_st[:, two, :], o_st[:, two, :], x1[b][:, two, :],
                                    ALU.add).then_inc(out_ready, 1)

            def scan(q, b, ahead, before, fetch_j):
                def inputs(n):
                    v.wait_ge(b_spread, DS * q + n + 1)
                    v.tensor_tensor(dbu[n % 2][:], du[b][:],
                                    bank[4 + n % 2][:].unsqueeze(1).broadcast_to([P, DB, CH]), ALU.mult
                                    ).then_inc(dbu_ready, 1)

                v.wait_ge(du_ready, q + 1)
                inputs(0)
                for n in range(DS):
                    g = DS * q + n
                    if n + 1 < DS:
                        inputs(n + 1)
                    slot(q, b, 2 * n, ahead, before)
                    v.wait_ge(dbu_ready, g + 1)
                    h = hst[n % STATE_BUFS]
                    v.wait_ge(y_added, g + 1)
                    for d in range(DB):
                        u = DB * g + d
                        v.wait_ge(dA_ready, u + 1)
                        v.tensor_tensor_scan(h[:, d, :], dA[:, d, :], dbu[n % 2][:, d, :],
                                             carry1[b][:, n, d:d + 1], ALU.mult, ALU.add).then_inc(scan_done, 1)
                    v.wait_ge(scan_done, DA_BUFS + DB * g + DB)
                    v.tensor_copy(carry1[b][:, n, :], h[:, :, CH - 1]).then_inc(carry_done, 1)
                    slot(q, b, 2 * n + 1, ahead, before)
                    if n == 10 and fetch_j is not None:
                        places(q + 2, b, fetch_j)

            v.sem_inc(scan_done, DA_BUFS)
            places(0, 0, 0)
            for k in range(2 * DS):
                slot(-1, 1, k, True, False)
            places(1, 1, 0)
            v.wait_ge(delta_ready, 1)
            v.tensor_tensor(du[0][:], delta[0][:], xc[0][:], ALU.mult).then_inc(du_ready, 1)
            scan(0, 0, True, False, 1)
            scan(1, 1, True, True, 1)
            with v.Fori(1, CPB - 1) as j:
                for b in range(B):
                    scan(B * j + b, b, True, True, j + 1)
            scan(CHUNKS - 2, 0, True, True, None)
            scan(CHUNKS - 1, 1, False, True, None)
            add_skip(CHUNKS - 1, 1)
            gate_y(CHUNKS - 1)
            result(CHUNKS - 1, 1)

        @block.tensor
        def _(pe):
            pe.wait_ge(ld_small, 16 * 6)
            def turn_normed(c, u):
                pe.wait_ge(xn_ready, TPC * c + TPC)
                wait_past(pe, xnT_ready, KB * (c - 1))
                for k in range(KB):
                    for i in range(TPC):
                        ins = pe.transpose(bank[2 * u + k][:, i * P:(i + 1) * P],
                                           normed_st[u][:, i, k * P:(k + 1) * P], ident[:])
                    ins.then_inc(xn_turned, 1)

            def logits(c, u):
                pe.wait_ge(xnT_ready, KB * c + KB)
                for i in range(TPC):
                    for k in range(KB):
                        ins = pe.matmul(bank[7][:, bass.ds((c * TPC + i) * NE, NE)],
                                        normedT[u][:, k, i * P:(i + 1) * P],
                                        w_r[:, k, :], start=(k == 0), stop=(k == KB - 1))
                ins.then_inc(logits_ready, 1)

            turn_normed(0, 0)
            turn_normed(1, 1)
            logits(0, 0)
            with pe.Fori(1, CHUNKS // 2) as pair:
                turn_normed(2 * pair, 0)
                logits(2 * pair - 1, 1)
                turn_normed(2 * pair + 1, 1)
                logits(2 * pair, 0)
            logits(CHUNKS - 1, 1)
            pe.wait_ge(onehot_ready, 1)
            pe.wait_ge(set_done, 3)
            n = TILES * NE
            oh = rt[:, 4].rearrange("p t e -> p (t e)")
            pe.matmul(bank[7][:, n:2 * n], tri[:], oh, start=True, stop=True)
            pe.matmul(bank[7][:, 2 * n:3 * n], ones[:], oh, start=True, stop=True).then_inc(ranks_ready, 1)

            pe.wait_ge(ld_w0, 32)
            pe.wait_ge(split_ready, 2)

            def turn_inputs(c):
                pe.wait_ge(xr_ready, c + 1)
                for k in range(KB):
                    for i in range(TPC):
                        ins = pe.transpose(bank[k][:, i * P:(i + 1) * P], xr_st[:, i, k * P:(k + 1) * P], ident[:])
                    ins.then_inc(xr_turned, 1)

            def mixer(c, ahead):
                pe.wait_ge(xrT_ready, KB * c + KB)
                for s in range(SB):
                    if s == 0:
                        wait_past(pe, gated_ready, SB * c)
                    for w in range(5):
                        if s > 0 and w == PROJ_F:
                            pe.wait_ge(sig_ready, 6 * c + 1)
                        if s > 0 and w == PROJ_ZG:
                            pe.wait_ge(sig_ready, 6 * c + 2)
                        if s > 0 and w == PROJ_Z:
                            pe.wait_ge(v_l0, L0_STEPS * c + 5)
                        if s == 0 and w == PROJ_GB:
                            wait_past(pe, mix_added, 2 * c)
                        for k in range(KB):
                            ins = pe.matmul(bank[2 + w][:], w0[:, w, k, s * P:(s + 1) * P], xT[:, k, :],
                                            start=(k == 0), stop=(k == KB - 1))
                        ins.then_inc(proj_ready, 1)
                if ahead:
                    turn_inputs(c + 1)
                pe.wait_ge(gated_ready, SB * c + SB)
                for h in range(2):
                    if h == 0:
                        wait_past(pe, mix_added, 2 * c - 1)
                    for i in range(2):
                        o = bank[7 - h][:, i * D:(i + 1) * D]
                        pe.matmul(o, ones_b[:], bias_b[:, B_MIX, :], start=True, stop=False)
                        t = (2 * h + i) * P
                        for s in range(SB):
                            for part in range(3):
                                ins = pe.matmul(o, gated[:, s, t:t + P], wo_b[:, part, s, :], start=False,
                                                stop=(s == SB - 1 and part == 2))
                    ins.then_inc(mix_ready, 1)

            turn_inputs(0)
            mixer(0, True)
            with pe.Fori(1, CHUNKS - 1) as c:
                mixer(c, True)
            mixer(CHUNKS - 1, False)

            pe.wait_ge(ld_moe, 48)
            pe.wait_ge(eid_ready, 1)
            pe.wait_ge(mix_added, 2 * CHUNKS)

            def turn_in(j, u, loads):
                pe.wait_ge(xg_loaded[u], 16 * loads)
                for k in range(KB):
                    ins = pe.transpose(bank[0][:, k * P:(k + 1) * P], xg[:, u, k * P:(k + 1) * P], ident[:])
                ins.then_inc(xg_turned, 1)

            def up(j, e, half):
                if half == 0:
                    pe.wait_ge(xgT_ready, j + 1)
                for n, w in enumerate((w_g, w_u)):
                    for k in range(KB):
                        ins = pe.matmul(bank[1 + 2 * half + n][:], xgT[:, k, :],
                                        w[:, bass.ds(e * (KB * FF) + (k * FF + half * HALF), HALF)],
                                        start=(k == 0), stop=(k == KB - 1))
                ins.then_inc(up_ready, 1)

            def turn_hidden(j, half):
                pe.wait_ge(hid_ready, 2 * j + half + 1)
                for i in range(FB // 2):
                    ins = pe.transpose(bank[5 + half][:, i * P:(i + 1) * P], hid[:, half, i * P:(i + 1) * P],
                                       ident[:])
                ins.then_inc(hid_turned, 1)

            def down(j, e):
                pe.wait_ge(hidT_ready, 2 * j + 2)
                if isinstance(j, int) and j == 0:
                    pe.wait_ge(bwT_ready, 1)
                wait_past(pe, ye_ready, j)
                for i in range(FB):
                    ins = pe.matmul(bank[7][:, 0:D], hidT[:, i, :], w_d[:, bass.ds(e * (FB * D) + i * D, D)],
                                    start=(i == 0), stop=(i == FB - 1))
                ins.then_inc(down_ready, 1)

            def expert(j):
                return pe.value_load(eid[0:1, bass.ds(j, 1)], min_val=0, max_val=NE - 1)

            turn_in(0, 0, 1)
            e0 = expert(0)
            up(0, e0, 0)
            up(0, e0, 1)
            pe.wait_ge(bw_ready, 1)
            for k in range(KB):
                for o in range(KB):
                    ins = pe.transpose(bank[7][:, k * D + o * P:k * D + (o + 1) * P],
                                       bw_t[:, o, k * P:(k + 1) * P], ident[:])
            ins.then_inc(bw_turned, 1)
            turn_in(1, 1, 1)
            turn_hidden(0, 0)
            def pair(jj):
                for u in range(2):
                    j = 1 + 2 * jj + u
                    e = expert(j)
                    up(j, e, 0)
                    turn_hidden(j - 1, 1)
                    up(j, e, 1)
                    turn_in(j + 1, u, jj + 2)
                    down(j - 1, expert(j - 1))
                    turn_hidden(j, 0)

            pair(0)
            with pe.Fori(1, (SLOTS - 1) // 2) as jj:
                pair(jj)
            turn_hidden(SLOTS - 1, 1)
            down(SLOTS - 1, expert(SLOTS - 1))
            pe.sem_inc(layer0_done, 1)
            pe.wait_ge(layer0_done, 5)


            def claim(turn, g):
                wait_past(pe, m_free, group(turn, g) - 1)
                return shared(g)

            def skip(turn, g, n):
                wait_past(pe, m_free, group(turn, g))
                pe.sem_inc(m_full, n)
                pe.sem_inc(m_free, n)

            def turn_xn2(t, k):
                pe.wait_ge(xn2_ready, t + 2)
                M = claim(t, G_XNT + k)
                for i in range(TPC):
                    ins = pe.transpose(M[:, i * P:(i + 1) * P], x_ld[:, i, k * P:(k + 1) * P], ident[:])
                ins.then_inc(m_full, 1)

            def in_proj(t, b, e, g):
                M = claim(t, g)
                for k in range(KB):
                    ins = pe.matmul(M[:], w_in[:, k, e * P:(e + 1) * P], xn2T[b][:, k, :],
                                    start=(k == 0), stop=(k == KB - 1))
                ins.then_inc(m_full, 1)

            def x_half(t, b, d):
                if d == 0:
                    pe.wait_ge(m_free, group(t, G_XNT) + 2)
                in_proj(t, b, d, G_X + d)

            def z_half(t, b, d):
                in_proj(t, b, DB + d, G_Z + d)

            def gate_half(t, b, h):
                M = claim(t, G_GATE + h)
                for i in range(2):
                    o, r = M[:, i * D:(i + 1) * D], (2 * h + i) * P
                    pe.matmul(o, ones_b[:], bias_b[:, B_GATE, :], start=True, stop=False)
                    for k in range(KB):
                        ins = pe.matmul(o, xn2T[b][:, k, r:r + P], bwT[:, k, :], start=False, stop=(k == KB - 1))
                ins.then_inc(m_full, 1)

            def low_rank(t, b, g, lo, n):
                pe.wait_ge(xc_ready, DB * (t + 1) + DB)
                M = claim(t, g)
                for d in range(DB):
                    ins = pe.matmul(M[0:n, :], w_x[:, d, lo:lo + n], xc[b][:, d, :], start=(d == 0),
                                    stop=(d == DB - 1))
                ins.then_inc(m_full, 1)

            def dt(t, d):
                M = claim(t, G_DELTA + d)
                pe.matmul(M[:], w_dt[:, d * P:(d + 1) * P], dt_sb[:], start=True, stop=True).then_inc(m_full, 1)

            def out_proj(t, h):
                pe.wait_ge(y_ready, DB * t)
                M = claim(t, G_OUT + h)
                for i in range(2):
                    o, r = M[:, i * D:(i + 1) * D], (2 * h + i) * P
                    pe.matmul(o, ones_b[:], bias_b[:, B_OUT, :], start=True, stop=False)
                    for d in range(DB):
                        ins = pe.matmul(o, y_fin[:, d, r:r + P], w_out[:, d, :], start=False,
                                        stop=(d == DB - 1))
                ins.then_inc(m_full, 1)

            def slot(t, b, k, prepares, gates, before):
                if prepares:
                    if k in (5, 6):
                        turn_xn2(t, k - 5)
                    if 7 <= k < 7 + DB:
                        x_half(t, 1 - b, k - 7)
                    if k == 16:
                        low_rank(t, 1 - b, G_DT, 0, DR)
                        low_rank(t, 1 - b, G_BC, DR, SPLIT + DS)
                    if 18 <= k < 18 + DB:
                        dt(t, k - 18)
                elif k in (5, 15):
                    skip(t, *((G_XNT, G_OUT - G_XNT) if k == 5 else (G_DT, G_Z - G_DT)))
                if before and k in (11, 12):
                    out_proj(t, k - 11)
                if not before and k == 11:
                    skip(t, G_OUT, 2)
                if gates:
                    if 22 <= k < 22 + DB:
                        z_half(t, b, k - 22)
                    if k in (26, 27):
                        gate_half(t, b, k - 26)
                elif k == 22:
                    skip(t, G_Z, GROUPS - G_Z)

            def spread(q, b, n):
                g = DS * q + n
                if n == 0:
                    pe.wait_ge(m_free, group(q - 1, G_BC) + 1)
                wait_past(pe, dbu_ready, g - 1)
                pe.matmul(bank[4 + n % 2][:], pick[:, n:n + 1].broadcast_to([2 * SPLIT, P]), b_split[b][:],
                          start=True, stop=True).then_inc(b_spread, 1)

            def add_up(q, n, blocks):
                g = DS * q + n
                if blocks[0] == 0:
                    pe.wait_ge(hc_ready, g + 1)
                    if n == 0:
                        wait_past(pe, skip_added, DB * q)
                for d in blocks:
                    ins = pe.matmul(bank[d][:], ident[:], hst[n % STATE_BUFS][:, d, :], start=(n == 0),
                                    stop=(n == DS - 1))
                if blocks[-1] == DB - 1:
                    ins.then_inc(y_added, 1)

            def scan(q, b, ahead, before):
                for n in range(DS):
                    if n + 2 < DS:
                        spread(q, b, n + 2)
                    elif ahead:
                        spread(q + 1, 1 - b, n + 2 - DS)
                    for half in range(2):
                        slot(q, b, 2 * n + half, ahead, True, before)
                        blocks = range(half * DB // 2, (half + 1) * DB // 2)
                        if n >= LAG:
                            add_up(q, n - LAG, blocks)
                        elif before:
                            add_up(q - 1, DS + n - LAG, blocks)

            pe.sem_inc(y_added, STATE_BUFS)
            for k in range(2 * DS):
                slot(-1, 1, k, True, False, False)
            spread(0, 0, 0)
            spread(0, 0, 1)
            scan(0, 0, True, False)
            scan(1, 1, True, True)
            with pe.Fori(1, CPB - 1) as j:
                for b in range(B):
                    scan(B * j + b, b, True, True)
            scan(CHUNKS - 2, 0, True, True)
            scan(CHUNKS - 1, 1, False, True)
            for n in range(DS - LAG, DS):
                add_up(CHUNKS - 1, n, range(DB))
            skip(CHUNKS, G_XNT, G_OUT - G_XNT)
            for h in range(2):
                out_proj(CHUNKS, h)


L0_SB = 5
L0_STEPS = SB * L0_SB
PRE_HALO = 1
PRE_STEPS = 9 + DB * (KC - 2)


def kernel(L0_attn_x, L0_attn_rms_w, L0_attn_Wf_w, L0_attn_Wf_b, L0_attn_Wzg_w, L0_attn_Wz_w, L0_attn_Wga_w,
           L0_attn_Wgb_w, L0_attn_Wout_w, L0_attn_Wout_b, L0_ffn_Wr, L0_ffn_br, L0_ffn_Wg, L0_ffn_Wu, L0_ffn_Wd,
           L1_attn_W_in, L1_attn_conv_w, L1_attn_conv_b, L1_attn_W_x, L1_attn_W_dt, L1_attn_b_dt, L1_attn_A_log,
           L1_attn_D, L1_attn_W_out, L1_attn_b_out, L1_ffn_weight, L1_ffn_bias):
    import numpy as np
    import concourse.bacc as bacc
    from concourse.bass_utils import run_bass_kernel_spmd

    def rows(w):
        w = np.asarray(w)
        return np.swapaxes(w.reshape(w.shape[0] // P, P, *w.shape[1:]), 0, 1)

    def spread(r):
        r = np.asarray(r)
        return np.broadcast_to(r, (P, *r.shape))

    wt = [rows(np.asarray(w).T) for w in (L0_attn_Wf_w, L0_attn_Wzg_w, L0_attn_Wz_w, L0_attn_Wga_w, L0_attn_Wgb_w)]
    experts = [np.stack([rows(np.asarray(w)[e]) for e in range(NE)], 1).reshape(P, -1)
               for w in (L0_ffn_Wg, L0_ffn_Wu, L0_ffn_Wd)]
    consts = np.concatenate([np.arange(NE, 0, -1), P * np.arange(TILES), np.arange(SLOTS + 1)]).astype(np.float32)
    w_xT = np.asarray(L1_attn_W_x).T
    w_xT = np.concatenate([w_xT, w_xT[:, DR:DR + DS]], 1)
    arrays = {
        "x": rows(np.asarray(L0_attn_x).reshape(B * T, D)),
        "cols0": np.stack([rows(L0_attn_rms_w), rows(L0_attn_Wf_b)], 2),
        "w_r": rows(L0_ffn_Wr),
        "tri": np.triu(np.ones((P, P), np.float32), 1),
        "small": np.concatenate([spread(L0_ffn_br), spread(consts)], 1),
        "bias_f": np.concatenate([np.broadcast_to(np.concatenate([np.asarray(c) for c in (
            L0_attn_Wout_b, L1_ffn_bias, L1_attn_b_out)]), (PARTS, 3 * D)), np.eye(PARTS, dtype=np.float32)], 1),
        "ident": np.eye(P, dtype=np.float32),
        "w0": np.stack(wt, 1),
        "wo": rows(np.asarray(L0_attn_Wout_w).T),
        "w_g": experts[0], "w_u": experts[1], "w_d": experts[2],
        "w_in": rows(np.asarray(L1_attn_W_in).T),
        "w_x": rows(w_xT),
        "pick": np.kron(np.ones((2, 1)), np.eye(SPLIT, DS)).astype(np.float32),
        "w_dt": np.asarray(L1_attn_W_dt).T,
        "w_out": rows(np.asarray(L1_attn_W_out).T),
        "cols1": np.concatenate([rows(L1_attn_conv_w)] + [rows(c)[:, :, None] for c in
                                (L1_attn_conv_b, L1_attn_b_dt, L1_attn_D)], 2),
        "a_log": rows(L1_attn_A_log),
        "bw_w": rows(L1_ffn_weight),
    }
    nc = bacc.Bacc("TRN2", target_bir_lowering=False, num_devices=1)
    ins, aps = {}, {}
    for name, x in arrays.items():
        x = np.ascontiguousarray(x)
        ins[f"in_{name}"] = x
        aps[name] = nc.dram_tensor(f"in_{name}", x.shape, mybir.dt.from_np(x.dtype), kind="ExternalInput").ap()
    out = nc.dram_tensor("out_0", (P, TILES, D), F32, kind="ExternalOutput").ap()
    build(nc, aps, out)
    r = run_bass_kernel_spmd(nc, [ins], core_ids=[0])
    got = r.results[0]["out_0"]
    return np.ascontiguousarray(np.swapaxes(got, 0, 1)).reshape(B, T, D)
```
